# Optimizing a Trainium2 kernel written in Bass

```python
import numpy as np
import jax
import jax.numpy as jnp

def _softmax(x, axis=-1):
    return jax.nn.softmax(x, axis=axis)

def _gelu(x):
    return jax.nn.gelu(x, approximate=True)

def _silu(x):
    return jax.nn.silu(x)

def _sigmoid(x):
    return jax.nn.sigmoid(x)

def _layernorm(x, axis=-1, eps=1e-05):
    m = jnp.mean(x, axis=axis, keepdims=True)
    v = jnp.var(x, axis=axis, keepdims=True)
    return (x - m) / jnp.sqrt(v + eps)

def _scatter_add(tgt, idx, src, axis=0):
    return tgt.at[idx].add(src)

def _segment_sum(src, seg, n):
    return jax.ops.segment_sum(src, seg, n)
kernel_name = 'mk_gnn_resnorm_d4_gnn_r64_59b76c'

def setup_inputs(seed: int=0):
    np.random.seed(seed)
    _w = jnp.asarray

    def _rec_inputs():
        import jax
        import jax.numpy as jnp
        _gk = jax.random.key(seed)
        x = -8.776e-05 + 1 * jax.random.normal(jax.random.fold_in(_gk, 1), (10000, 512), jnp.float32)
        src = jax.random.randint(jax.random.fold_in(_gk, 2), (5000,), 0, 10000, jnp.int32)
        dst = jax.random.randint(jax.random.fold_in(_gk, 3), (5000,), 0, 10000, jnp.int32)
        _o = jnp.argsort(dst, stable=True)
        src = src[_o]
        dst = dst[_o]
        return (x, src, dst)
    x, src, dst = _rec_inputs()

    def _L0_gnn_setup():
        import jax, jax.numpy as jnp
        import numpy as np
        N_NODES = 10000
        N_EDGES = 2500
        D = 512
        key = jax.random.key(seed)
        k_h, k_e, k_w1, k_w2 = jax.random.split(key, 4)
        h = jax.random.normal(k_h, (N_NODES, D), dtype=jnp.float32)
        edge_index = jax.random.randint(k_e, (2, N_EDGES), 0, N_NODES, dtype=jnp.int64)
        scale = 1.0 / np.sqrt(D)
        W1 = jax.random.normal(k_w1, (D, D), dtype=jnp.float32) * scale
        b1 = jnp.zeros((D,), dtype=jnp.float32)
        W2 = jax.random.normal(k_w2, (D, D), dtype=jnp.float32) * scale
        b2 = jnp.zeros((D,), dtype=jnp.float32)
        return {'h': h, 'edge_index': edge_index, 'W1': W1, 'b1': b1, 'W2': W2, 'b2': b2}
    _L0_gnn_all = _L0_gnn_setup()
    _L0_gnn_in = {k: v for k, v in _L0_gnn_all.items() if k in ('W1', 'b1', 'W2', 'b2')}
    del _L0_gnn_all

    def _L1_gnn_setup():
        import jax, jax.numpy as jnp
        import numpy as np
        N, E, D = (50000, 6250, 512)
        EPS = 1e-05
        key = jax.random.key(seed)
        ks = jax.random.split(key, 5)
        scale = 1.0 / np.sqrt(D)
        x = jax.random.normal(ks[0], (N, D), dtype=jnp.float32)
        edge_index = jax.random.randint(ks[1], (2, E), 0, N, dtype=jnp.int32)
        W_l = jax.random.normal(ks[2], (D, D), dtype=jnp.float32) * scale
        b_l = jnp.zeros((D,), dtype=jnp.float32)
        W_r = jax.random.normal(ks[3], (D, D), dtype=jnp.float32) * scale
        gamma = jnp.ones((D,), dtype=jnp.float32)
        beta = jnp.zeros((D,), dtype=jnp.float32)
        return {'x': x, 'edge_index': edge_index, 'W_l': W_l, 'b_l': b_l, 'W_r': W_r, 'gamma': gamma, 'beta': beta}
    _L1_gnn_all = _L1_gnn_setup()
    _L1_gnn_in = {k: v for k, v in _L1_gnn_all.items() if k in ('W_l', 'b_l', 'W_r', 'gamma', 'beta')}
    del _L1_gnn_all

    def _L2_gnn_setup():
        import jax, jax.numpy as jnp
        import numpy as np
        N = 10000
        E = 2500
        H = 4
        C = 256
        D_IN = 512
        D_OUT = 512
        NEG_SLOPE = 0.2

        def gat_conv(x, src, dst, W, a_src, a_dst, bias):
            n = x.shape[0]
            h = (x @ W).reshape(n, H, C)
            al_s = jnp.einsum('nhc,hc->nh', h, a_src)
            al_d = jnp.einsum('nhc,hc->nh', h, a_dst)
            e = jax.nn.leaky_relu(al_s[src] + al_d[dst], NEG_SLOPE)
            emax = jax.ops.segment_max(e, dst, num_segments=n)
            w = jnp.exp(e - emax[dst])
            denom = jax.ops.segment_sum(w, dst, num_segments=n)
            alpha = w / denom[dst]
            out = jax.ops.segment_sum(h[src] * alpha[:, :, None], dst, num_segments=n)
            return out.reshape(n, H * C) + bias
        key = jax.random.key(seed)
        ks = jax.random.split(key, 13)
        s = 0.05
        return {'x': jax.random.normal(ks[0], (N, D_IN), jnp.float32), 'edge_index': jax.random.randint(ks[1], (2, E), 0, N, dtype=jnp.int32), 'W1': jax.random.normal(ks[2], (D_IN, H * C), jnp.float32) * s, 'a_src1': jax.random.normal(ks[3], (H, C), jnp.float32) * s, 'a_dst1': jax.random.normal(ks[4], (H, C), jnp.float32) * s, 'b1': jnp.zeros((H * C,), jnp.float32), 'W2': jax.random.normal(ks[5], (H * C, H * C), jnp.float32) * s, 'a_src2': jax.random.normal(ks[6], (H, C), jnp.float32) * s, 'a_dst2': jax.random.normal(ks[7], (H, C), jnp.float32) * s, 'b2': jnp.zeros((H * C,), jnp.float32), 'Wfc': jax.random.normal(ks[8], (H * C, D_OUT), jnp.float32) * s, 'bfc': jnp.zeros((D_OUT,), jnp.float32)}
    _L2_gnn_all = _L2_gnn_setup()
    _L2_gnn_in = {k: v for k, v in _L2_gnn_all.items() if k in ('W1', 'a_src1', 'a_dst1', 'b1', 'W2', 'a_src2', 'a_dst2', 'b2', 'Wfc', 'bfc')}
    del _L2_gnn_all

    def _L3_gnn_setup():
        import jax, jax.numpy as jnp
        import numpy as np
        N = 50000
        E = 12500
        D = 512

        def _gcn_conv(x, edge_index, W, b):
            n = x.shape[0]
            xw = x @ W.T
            loop = jnp.arange(n, dtype=edge_index.dtype)
            row = jnp.concatenate([edge_index[0], loop])
            col = jnp.concatenate([edge_index[1], loop])
            deg = jax.ops.segment_sum(jnp.ones_like(row, dtype=xw.dtype), col, num_segments=n)
            dinv = jnp.where(deg > 0, jax.lax.rsqrt(deg), 0.0)
            norm = dinv[row] * dinv[col]
            msgs = norm[:, None] * xw[row]
            out = jax.ops.segment_sum(msgs, col, num_segments=n)
            return out + b

        def _batch_norm(h, gamma, beta, eps=1e-05):
            mean = jnp.mean(h, axis=0)
            var = jnp.var(h, axis=0)
            return (h - mean) * jax.lax.rsqrt(var + eps) * gamma + beta
        key = jax.random.key(seed)
        k1, k2, k3, k4, k5, k6 = jax.random.split(key, 6)
        x = jax.random.normal(k1, (N, D), dtype=jnp.float32)
        edge_index = jax.random.randint(k2, (2, E), 0, N, dtype=jnp.int64)
        W = jax.random.normal(k3, (D, D), dtype=jnp.float32) * (1.0 / np.sqrt(D))
        b = jnp.zeros((D,), dtype=jnp.float32)
        gamma = jnp.ones((D,), dtype=jnp.float32)
        beta = jnp.zeros((D,), dtype=jnp.float32)
        return {'x': x, 'edge_index': edge_index, 'W': W, 'b': b, 'gamma': gamma, 'beta': beta}
    _L3_gnn_all = _L3_gnn_setup()
    _L3_gnn_in = {k: v for k, v in _L3_gnn_all.items() if k in ('W', 'b', 'gamma', 'beta')}
    del _L3_gnn_all
    return {'x': x, 'src': src, 'dst': dst, 'L0_gnn_W1': _L0_gnn_in['W1'], 'L0_gnn_b1': _L0_gnn_in['b1'], 'L0_gnn_W2': _L0_gnn_in['W2'], 'L0_gnn_b2': _L0_gnn_in['b2'], 'L1_gnn_W_l': _L1_gnn_in['W_l'], 'L1_gnn_b_l': _L1_gnn_in['b_l'], 'L1_gnn_W_r': _L1_gnn_in['W_r'], 'L1_gnn_gamma': _L1_gnn_in['gamma'], 'L1_gnn_beta': _L1_gnn_in['beta'], 'L2_gnn_W1': _L2_gnn_in['W1'], 'L2_gnn_a_src1': _L2_gnn_in['a_src1'], 'L2_gnn_a_dst1': _L2_gnn_in['a_dst1'], 'L2_gnn_b1': _L2_gnn_in['b1'], 'L2_gnn_W2': _L2_gnn_in['W2'], 'L2_gnn_a_src2': _L2_gnn_in['a_src2'], 'L2_gnn_a_dst2': _L2_gnn_in['a_dst2'], 'L2_gnn_b2': _L2_gnn_in['b2'], 'L2_gnn_Wfc': _L2_gnn_in['Wfc'], 'L2_gnn_bfc': _L2_gnn_in['bfc'], 'L3_gnn_W': _L3_gnn_in['W'], 'L3_gnn_b': _L3_gnn_in['b'], 'L3_gnn_gamma': _L3_gnn_in['gamma'], 'L3_gnn_beta': _L3_gnn_in['beta']}

def reference(x, src, dst, L0_gnn_W1, L0_gnn_b1, L0_gnn_W2, L0_gnn_b2, L1_gnn_W_l, L1_gnn_b_l, L1_gnn_W_r, L1_gnn_gamma, L1_gnn_beta, L2_gnn_W1, L2_gnn_a_src1, L2_gnn_a_dst1, L2_gnn_b1, L2_gnn_W2, L2_gnn_a_src2, L2_gnn_a_dst2, L2_gnn_b2, L2_gnn_Wfc, L2_gnn_bfc, L3_gnn_W, L3_gnn_b, L3_gnn_gamma, L3_gnn_beta):
    import jax
    import jax.numpy as jnp

    def _L0_gnn_ref(h, edge_index, W1, b1, W2, b2):
        import jax, jax.numpy as jnp
        import numpy as np
        N_NODES = 10000
        N_EDGES = 2500
        D = 512
        send, rec = (edge_index[0], edge_index[1])
        agg = jax.ops.segment_sum(h[send], rec, num_segments=h.shape[0])
        x = h + agg
        x = jax.nn.relu(x @ W1 + b1)
        x = x @ W2 + b2
        return x

    def _L1_gnn_ref(x, edge_index, W_l, b_l, W_r, gamma, beta):
        import jax, jax.numpy as jnp
        import numpy as np
        N, E, D = (50000, 6250, 512)
        EPS = 1e-05
        n = x.shape[0]
        src, dst = (edge_index[0], edge_index[1])
        agg = jax.ops.segment_sum(x[src], dst, num_segments=n)
        cnt = jax.ops.segment_sum(jnp.ones((src.shape[0],), x.dtype), dst, num_segments=n)
        mean_agg = agg / jnp.maximum(cnt, 1.0)[:, None]
        h = mean_agg @ W_l.T + b_l + x @ W_r.T
        mu = jnp.mean(h, axis=0)
        var = jnp.var(h, axis=0)
        h = (h - mu) * jax.lax.rsqrt(var + EPS) * gamma + beta
        return jax.nn.relu(h) + x

    def _L2_gnn_ref(x, edge_index, W1, a_src1, a_dst1, b1, W2, a_src2, a_dst2, b2, Wfc, bfc):
        import jax, jax.numpy as jnp
        import numpy as np
        N = 10000
        E = 2500
        H = 4
        C = 256
        D_IN = 512
        D_OUT = 512
        NEG_SLOPE = 0.2

        def gat_conv(x, src, dst, W, a_src, a_dst, bias):
            n = x.shape[0]
            h = (x @ W).reshape(n, H, C)
            al_s = jnp.einsum('nhc,hc->nh', h, a_src)
            al_d = jnp.einsum('nhc,hc->nh', h, a_dst)
            e = jax.nn.leaky_relu(al_s[src] + al_d[dst], NEG_SLOPE)
            emax = jax.ops.segment_max(e, dst, num_segments=n)
            w = jnp.exp(e - emax[dst])
            denom = jax.ops.segment_sum(w, dst, num_segments=n)
            alpha = w / denom[dst]
            out = jax.ops.segment_sum(h[src] * alpha[:, :, None], dst, num_segments=n)
            return out.reshape(n, H * C) + bias
        loop = jnp.arange(N, dtype=edge_index.dtype)
        src = jnp.concatenate([edge_index[0], loop])
        dst = jnp.concatenate([edge_index[1], loop])
        h = jax.nn.relu(gat_conv(x, src, dst, W1, a_src1, a_dst1, b1))
        h = jax.nn.relu(gat_conv(h, src, dst, W2, a_src2, a_dst2, b2))
        return h @ Wfc + bfc

    def _L3_gnn_ref(x, edge_index, W, b, gamma, beta):
        import jax, jax.numpy as jnp
        import numpy as np
        N = 50000
        E = 12500
        D = 512

        def _gcn_conv(x, edge_index, W, b):
            n = x.shape[0]
            xw = x @ W.T
            loop = jnp.arange(n, dtype=edge_index.dtype)
            row = jnp.concatenate([edge_index[0], loop])
            col = jnp.concatenate([edge_index[1], loop])
            deg = jax.ops.segment_sum(jnp.ones_like(row, dtype=xw.dtype), col, num_segments=n)
            dinv = jnp.where(deg > 0, jax.lax.rsqrt(deg), 0.0)
            norm = dinv[row] * dinv[col]
            msgs = norm[:, None] * xw[row]
            out = jax.ops.segment_sum(msgs, col, num_segments=n)
            return out + b

        def _batch_norm(h, gamma, beta, eps=1e-05):
            mean = jnp.mean(h, axis=0)
            var = jnp.var(h, axis=0)
            return (h - mean) * jax.lax.rsqrt(var + eps) * gamma + beta
        identity = x
        h = _gcn_conv(x, edge_index, W, b)
        h = _batch_norm(h, gamma, beta)
        h = jax.nn.gelu(h, approximate=False)
        return h + identity
    edge_index = jnp.stack([src, dst])
    x = _layernorm(x + _L0_gnn_ref(x, edge_index, L0_gnn_W1, L0_gnn_b1, L0_gnn_W2, L0_gnn_b2), axis=-1)
    x = _layernorm(x + _L1_gnn_ref(x, edge_index, L1_gnn_W_l, L1_gnn_b_l, L1_gnn_W_r, L1_gnn_gamma, L1_gnn_beta), axis=-1)
    x = _layernorm(x + _L2_gnn_ref(x, edge_index, L2_gnn_W1, L2_gnn_a_src1, L2_gnn_a_dst1, L2_gnn_b1, L2_gnn_W2, L2_gnn_a_src2, L2_gnn_a_dst2, L2_gnn_b2, L2_gnn_Wfc, L2_gnn_bfc), axis=-1)
    x = _layernorm(x + _L3_gnn_ref(x, edge_index, L3_gnn_W, L3_gnn_b, L3_gnn_gamma, L3_gnn_beta), axis=-1)
    return x

_drawn_inputs = setup_inputs


def setup_inputs(seed=0):
    import zlib

    import numpy as np

    out = dict(_drawn_inputs(seed))
    spreads = {'L0_gnn_b1': (0.0, 0.1),
     'L0_gnn_b2': (0.0, 0.1),
     'L1_gnn_b_l': (0.0, 2.0),
     'L1_gnn_gamma': (1.0, 0.2),
     'L1_gnn_beta': (0.0, 0.1),
     'L2_gnn_b1': (0.0, 0.1),
     'L2_gnn_b2': (0.0, 0.1),
     'L2_gnn_bfc': (0.0, 0.1),
     'L3_gnn_b': (0.0, 2.0),
     'L3_gnn_gamma': (1.0, 0.2),
     'L3_gnn_beta': (0.0, 0.1)}
    factors = {'L2_gnn_a_dst2': 11.871}
    for name, (base, spread) in spreads.items():
        noise = np.random.default_rng([zlib.crc32(name.encode()), seed]).standard_normal(out[name].shape)
        drawn = base * np.exp(spread * noise) if base else spread * noise
        out[name] = jnp.asarray(drawn.astype(out[name].dtype))
    for name, factor in factors.items():
        out[name] = (out[name] * factor).astype(out[name].dtype)
    return out
```

```python
from contextlib import ExitStack

import concourse.bass as bass
from concourse import mybir

F32 = mybir.dt.float32
F16 = mybir.dt.float16
I32 = mybir.dt.int32
ALU = mybir.AluOpType
ACT = mybir.ActivationFunctionType
AX = mybir.AxisListType
ds = bass.ds

P = 128
D = 512
HC = 1024
HEADS = 4
C = HC // HEADS
S = 4
GROUP = S * P
EDGES = P - 1
EPS = 1e-5
SLOPE = 0.2
A_SCALE = 16.0
GIN_SCALE = 2.0
W_SCALE = 256.0
UNSCALE = 1.0 / (A_SCALE * W_SCALE)
GIN_UNSCALE = 1.0 / (GIN_SCALE * W_SCALE)
FAR = 20000
BIG = 1e30
CARRY_IN = (0, 96)
CARRY_OUT = (96, 0)

W_GIN1, W_GIN2, W_SAGE_L, W_SAGE_R, W_GAT1, W_GAT2, W_FC, W_GCN = 0, 1, 2, 3, 4, 6, 10, 12
UNITS = 13
V_GIN_B1, V_SAGE_B, V_SAGE_G, V_SAGE_BETA, V_GAT1_B, V_GAT2_B, V_GCN_B, V_GCN_G, V_GCN_BETA = (
    0, 4, 8, 12, 16, 24, 32, 36, 40)
VECTORS = 44


class Dims:
    def __init__(self, nodes, edges):
        self.nodes = nodes
        self.edges = edges
        self.groups = -(-nodes // (2 * GROUP)) * 2
        self.padded = self.groups * GROUP
        self.sent = self.padded - 1
        self.edge_cols = -(-(edges + 1) // P)
        self.edge_rows = self.edge_cols * P
        self.tiles = -(-edges // (2 * EDGES)) * 2
        self.last_real = nodes - (self.groups - 1) * GROUP
        assert self.sent >= nodes and 0 < self.last_real <= GROUP
        assert self.tiles * EDGES + 2 <= self.edge_rows + 1
        assert self.padded * self.edge_cols < 1 << 24


class Signal:

    def __init__(self, sem, base):
        self.sem, self.base = sem, base

    def at(self, n):
        return self.base + n


class Signals:

    def __init__(self, nc, ctx):
        self.nc, self.ctx, self.sems, self.total, self.raised = nc, ctx, {}, {}, []

    def take(self, name, total, software=False):
        if name not in self.sems:
            self.sems[name] = self.ctx.enter_context(self.nc.semaphore(name))
            self.total[name] = 0 if software else 1
            if not software:
                self.raised.append(self.sems[name])
        s = Signal(self.sems[name], self.total[name])
        self.total[name] += total
        return s

    def raise_all(self, eng, which):
        for sem in self.raised[which::5]:
            eng.sem_inc(sem, 1)

    def pair(self, name, total, software=False):
        return [self.take(f"{name}{u}", total, software) for u in range(2)]


class Steps:

    def __init__(self, sig):
        self.sig, self.first, self.n = sig, 0, 0

    def begin(self, first):
        self.first, self.n = first, 0

    def mark(self, ins):
        ins.then_inc(self.sig.sem, 1)
        self.n += 1
        return self.sig.at(self.first + self.n)


def settle(eng, kn):
    eng.sem_inc(kn.passed, 1)


def in_pairs(eng, n, body):
    if n > 2:
        with eng.Fori(0, n // 2 - 1) as i:
            for u in range(2):
                body(i, u, False)
    body(n // 2 - 1, 0, False)
    body(n // 2 - 1, 1, True)


def following(i, u):
    return i + u, 1 - u


class Kernel:
    def __init__(self, nc, ctx, dims, dram):
        self.nc, self.ctx, self.d, self.dram = nc, ctx, dims, dram
        self.sig = Signals(nc, ctx)
        self.stages = []
        self.meet = ctx.enter_context(nc.semaphore("meet"))
        self.passed = ctx.enter_context(nc.semaphore("passed"))
        self.buffers = 0
        d = dims

        def sb(name, shape, dt):
            return ctx.enter_context(nc.sbuf_tensor(name, shape, dt))

        self.ident = sb("ident", [P, P], F32)
        self.ones = sb("ones", [P, P], F32)
        self.w_hi = sb("w_hi", [P, UNITS, 4 * D], F16)
        self.w_lo = sb("w_lo", [P, UNITS, 4 * D], F16)
        self.wa_hi = sb("wa_hi", [P, 12, 2 * HEADS], F16)
        self.wa_lo = sb("wa_lo", [P, 12, 2 * HEADS], F16)
        self.vec = sb("vec", [P, VECTORS], F32)
        self.vec_scaled = sb("vec_scaled", [P, VECTORS], F32)
        self.gin_b2 = sb("gin_b2", [P, D], F32)
        self.fc_b = sb("fc_b", [P, D], F32)
        self.same = sb("same", [P, d.tiles * P], F16)
        self.dst_f = sb("dst_f", [P, d.tiles], F32)
        self.src_i = sb("src_i", [P, d.tiles], I32)
        self.dst_i = sb("dst_i", [P, d.tiles], I32)
        self.final_i = sb("final_i", [P, d.tiles], I32)
        self.count = sb("count", [P, d.tiles], F32)
        self.mean_scale = sb("mean_scale", [P, d.tiles], F32)
        self.dinv = sb("dinv_sb", [P, d.tiles], F32)
        self.src_dinv = sb("src_dinv", [P, d.tiles], F32)
        self.bn_scale = sb("bn_scale", [P, 4], F32)
        self.bn_shift = sb("bn_shift", [P, 4], F32)
        self.bn_stats = sb("bn_stats", [P, 4, 2 * 6 * (d.groups // 2)], F32)
        self.minus_half = sb("minus_half", [P, d.tiles], F32)
        self.eps = sb("eps", [P, S], F32)
        self.bank = [ctx.enter_context(nc.psum_tensor(f"bank{n}", [P, D], F32)) for n in range(8)]

    def weights(self, lo, unit, k, n, width):
        w = self.w_lo if lo else self.w_hi
        per = 4 * D // width
        at = (k % per) * width + n * D
        return w[:, unit + k // per, at:at + D]

    def buffer(self, mem, name, shape, dt):
        self.buffers += 1
        return mem.enter_context(self.nc.sbuf_tensor(f"{name}_{self.buffers}", shape, dt))

    def add(self, stage):
        self.stages.append(stage)

    def run(self):
        nc = self.nc
        meet = self.meet
        block = self.ctx.enter_context(nc.Block())
        stages = self.stages

        def program(eng, which):
            names = ("sync", "gpsimd", "scalar", "vector", "tensor")
            self.sig.raise_all(eng, names.index(which))
            eng.drain().then_inc(meet, 1)
            eng.wait_ge(meet, 5)
            for n, stage in enumerate(stages):
                if which in stage:
                    stage[which](eng)
                eng.drain().then_inc(meet, 1)
                eng.wait_ge(meet, 5 * (n + 2))

        @block.sync
        def _(sp):
            program(sp, "sync")

        @block.gpsimd
        def _(pool):
            program(pool, "gpsimd")

        @block.scalar
        def _(act):
            program(act, "scalar")

        @block.vector
        def _(dve):
            program(dve, "vector")

        @block.tensor
        def _(pe):
            program(pe, "tensor")


def split_product(pe, out, stationary, moving, chunks):
    for k in range(chunks):
        s_hi, s_lo = stationary(k)
        m_hi, m_lo = moving(k)
        last = k == chunks - 1
        pe.matmul(out, s_lo, m_hi, start=(k == 0), stop=False)
        pe.matmul(out, s_hi, m_lo, start=False, stop=False)
        mm = pe.matmul(out, s_hi, m_hi, start=False, stop=last)
    return mm


def setup_stage(kn):
    nc, d, dram, take = kn.nc, kn.d, kn.dram, kn.sig.take
    J = d.edge_cols
    mem = ExitStack()

    def sb(name, shape, dt):
        return kn.buffer(mem, name, shape, dt)

    blank = sb("blank", [P, HC + HEADS], F32)
    dst_row = sb("dst_row", [P, J * P], I32)
    key_row = sb("key_row", [P, J * P], F32)
    junk = dst_row[:, 0:J * P // 2].bitcast(F16)
    pairs = sb("pairs", [P, J, 2], I32)
    key_col = sb("key_col", [P, J], F32)
    j_col = sb("j_col", [P, J], F32)
    before = sb("before", [P, P], F32)
    junk2 = sb("junk2", [P, P], F16)
    less = sb("less", [P, J], F32)
    tied = sb("tied", [P, J], F32)
    place = sb("place", [P, J], I32)
    stage_w = [sb(f"stage_w{u}", [P, 4 * D], F32) for u in range(2)]
    a_rows = sb("a_rows", [P, 2, HC], F32)
    prod = sb("prod", [P, HC], F32)
    wa = sb("wa", [P, 12, 2 * HEADS], F32)
    sentinel = sb("sentinel", [1, 2], I32)

    small_in = take("small_in", 16 * 3)
    dst_in = take("dst_in", 16)
    pairs_in = take("pairs_in", 16)
    a_in = [take(f"a_in{n}", 16) for n in range(2)]
    zeroed = take("zeroed", 16 * (2 * d.groups + 1))
    blank_ready = take("blank_ready", 1)
    pool_steps = Steps(take("pool_steps", 10))
    w_in = [take("w_in0", 16 * 7), take("w_in1", 16 * 6)]
    w_hi_done = take("w_hi_done", UNITS)
    w_done = take("w_done", UNITS)
    wa_read = take("wa_read", 6 * 2 * 2 + 1)
    wa_steps = take("wa_steps", 12 * 4 + 2)
    order = take("order", 2 * J + 6)
    vec_done = take("vec_done", 2)
    sorted_out = take("sorted_out", 16 * (J - 1), software=True)
    sorted_first = kn.sig.pair("scattered", 16, software=True)

    gat_units = list(range(W_GAT1, W_FC))

    def sync(sp):
        sp.dma_start(dst_row[:], dram["dst"].partition_broadcast(P)).then_inc(dst_in.sem, 16)
        sp.dma_start(pairs[:], dram["edges"]).then_inc(pairs_in.sem, 16)
        sp.dma_start(kn.vec[:], dram["vectors"]).then_inc(small_in.sem, 16)
        sp.dma_start(kn.gin_b2[:], dram["gin_b2"].partition_broadcast(P)).then_inc(small_in.sem, 16)
        sp.dma_start(kn.fc_b[:], dram["fc_b"].partition_broadcast(P)).then_inc(small_in.sem, 16)
        for n in range(2):
            if n == 1:
                sp.wait_ge(wa_read.sem, wa_read.at(4 * 2))
            sp.dma_start(a_rows[:], dram["attention"][n].partition_broadcast(P)).then_inc(a_in[n].sem, 16)
            for unit in (range(0, 6) if n == 0 else range(6, UNITS)):
                if unit >= 2:
                    sp.wait_ge(w_done.sem, w_done.at(unit - 1))
                    done = sum(2 * 2 for g in gat_units if g <= unit - 2)
                    if done:
                        sp.wait_ge(wa_read.sem, wa_read.at(done))
                sp.dma_start(stage_w[unit % 2][:], dram["weights"][unit]).then_inc(w_in[unit % 2].sem, 16)
        sp.wait_ge(blank_ready.sem, blank_ready.at(1))
        rows = d.padded // P
        per = rows // d.groups
        wide = dram["sum_gat"].rearrange("(p r) c -> p r c", r=rows)
        thin = dram["sum"].rearrange("(p r) c -> p r c", r=rows)
        for g in range(d.groups):
            sp.dma_start(wide[:, g * per:(g + 1) * per, :],
                         blank[:].unsqueeze(1).broadcast_to([P, per, HC + HEADS])).then_inc(zeroed.sem, 16)
            sp.dma_start(thin[:, g * per:(g + 1) * per, :],
                         blank[:, 0:D].unsqueeze(1).broadcast_to([P, per, D])).then_inc(zeroed.sem, 16)
        sp.dma_start(dram["dinv"].rearrange("(p r) c -> p (r c)", p=P), kn.ones[:, 0:rows]).then_inc(zeroed.sem, 16)
        sp.wait_ge(zeroed.sem, zeroed.at(16 * (2 * d.groups + 1)))

    def gpsimd(pool):
        st = pool_steps
        st.begin(0)
        g = nc.gpsimd
        g.memset(blank[:, 0:HC], 0.0)
        a = st.mark(g.memset(kn.ones[:], 1.0))
        st.mark(g.memset(kn.ident[:], 0.0))
        g.memset(kn.eps[:], EPS)
        b = st.mark(g.memset(kn.minus_half[:], -0.5))
        pool.wait_ge(st.sig.sem, a)
        g.memset(blank[:, HC:], 1.0).then_inc(blank_ready.sem, 1)
        pool.wait_ge(st.sig.sem, b)
        st.mark(g.affine_select(out=kn.ident[:], in_=kn.ident[:], compare_op=ALU.not_equal, fill=1.0,
                                base=0, pattern=[[-1, P]], channel_multiplier=1))
        st.mark(g.affine_select(out=before[:], in_=kn.ones[:], compare_op=ALU.is_gt, fill=0.0,
                                base=0, pattern=[[-1, P]], channel_multiplier=1))
        st.mark(g.iota(key_row[:].rearrange("p (j q) -> p j q", q=P), [[1, J], [0, P]], base=0,
                       channel_multiplier=0, allow_small_or_imprecise_dtypes=True))
        st.mark(g.iota(j_col[:], [[1, J]], base=0, channel_multiplier=0,
                       allow_small_or_imprecise_dtypes=True))
        st.mark(g.memset(sentinel[:, 0:1], 0))
        st.mark(g.memset(sentinel[:, 1:2], d.sent))
        n = st.mark(g.memset(kn.src_dinv[:], 1.0))
        pool.wait_ge(st.sig.sem, n)
        pool.dma_start(dram["sorted"][0:1, :], sentinel[:]).then_inc(sorted_out.sem, 16)
        pool.wait_ge(order.sem, order.at(2 * J + 6))
        pool.wait_ge(small_in.sem, small_in.at(48))
        pool.wait_ge(pairs_in.sem, pairs_in.at(16))
        for j in range(J):
            pool.indirect_dma_start(dram["sorted"], bass.IndirectOffsetOnAxis(ap=place[:, j:j + 1], axis=0),
                                    pairs[:, j, :], None)\
                .then_inc((sorted_first[j] if j < 2 else sorted_out).sem, 16)
        pool.wait_ge(sorted_out.sem, sorted_out.at(16 * (J - 1)))
        for first in sorted_first:
            pool.wait_ge(first.sem, first.at(16))

    def scalar(act):
        for unit in range(UNITS):
            act.wait_ge(w_in[unit % 2].sem, w_in[unit % 2].at(16 * (unit // 2 + 1)))
            act.activation(kn.w_hi[:, unit, :], stage_w[unit % 2][:], ACT.Copy, scale=W_SCALE)\
               .then_inc(w_hi_done.sem, 1)
        act.wait_ge(small_in.sem, small_in.at(48))
        act.mul(kn.vec_scaled[:, 0:V_GIN_B1 + 4], kn.vec[:, 0:V_GIN_B1 + 4], GIN_SCALE).then_inc(vec_done.sem, 1)
        act.mul(kn.vec_scaled[:, V_GIN_B1 + 4:], kn.vec[:, V_GIN_B1 + 4:], A_SCALE).then_inc(vec_done.sem, 1)

    def vector(dve):
        v = nc.vector
        dve.wait_ge(pool_steps.sig.sem, pool_steps.sig.at(10))
        dve.wait_ge(dst_in.sem, dst_in.at(16))
        dve.wait_ge(pairs_in.sem, pairs_in.at(16))
        dve.wait_ge(small_in.sem, small_in.at(48))
        v.scalar_tensor_tensor(out=key_row[:], in0=dst_row[:], scalar=float(J), in1=key_row[:],
                               op0=ALU.mult, op1=ALU.add).then_inc(order.sem, 1)
        v.scalar_tensor_tensor(out=key_col[:], in0=pairs[:, :, 1], scalar=float(J), in1=j_col[:],
                               op0=ALU.mult, op1=ALU.add).then_inc(order.sem, 1)
        with dve.Fori(0, J) as j:
            dve.wait_ge(order.sem, order.at(j * 2 + 2))
            v.tensor_scalar(junk, key_row[:], key_col[:, ds(j, 1)], None, ALU.is_lt, ALU.add,
                            accum_out=less[:, ds(j, 1)]).then_inc(order.sem, 1)
            v.scalar_tensor_tensor(out=junk2[:], in0=key_row[:, ds(j * P, P)], scalar=key_col[:, ds(j, 1)],
                                   in1=before[:], op0=ALU.is_equal, op1=ALU.mult,
                                   accum_out=tied[:, ds(j, 1)]).then_inc(order.sem, 1)
        dve.wait_ge(order.sem, order.at(2 * J + 2))
        v.tensor_tensor(less[:], less[:], tied[:], ALU.add).then_inc(order.sem, 1)
        dve.wait_ge(order.sem, order.at(2 * J + 3))
        v.tensor_scalar(less[:], less[:], 1.0, None, ALU.add).then_inc(order.sem, 1)
        dve.wait_ge(order.sem, order.at(2 * J + 4))
        v.tensor_copy(place[:], less[:]).then_inc(order.sem, 2)
        n = 0
        for unit in range(UNITS):
            dve.wait_ge(w_in[unit % 2].sem, w_in[unit % 2].at(16 * (unit // 2 + 1)))
            dve.wait_ge(w_hi_done.sem, w_hi_done.at(unit + 1))
            v.scalar_tensor_tensor(out=kn.w_lo[:, unit, :], in0=stage_w[unit % 2][:], scalar=W_SCALE,
                                   in1=kn.w_hi[:, unit, :], op0=ALU.mult, op1=ALU.subtract)\
                .then_inc(w_done.sem, 1)
            if unit not in gat_units:
                continue
            layer = 0 if unit < W_GAT2 else 1
            dve.wait_ge(a_in[layer].sem, a_in[layer].at(16))
            for half in range(2):
                k = 2 * (unit - W_GAT1) + half
                w = stage_w[unit % 2][:, half * HC:(half + 1) * HC]
                for side in range(2):
                    if n:
                        dve.wait_ge(wa_steps.sem, wa_steps.at(n))
                    v.tensor_tensor(prod[:], w, a_rows[:, side, :], ALU.mult).then_inc(wa_read.sem, 1)
                    n_read = 4 * (unit - W_GAT1) + 2 * half + side + 1
                    dve.wait_ge(wa_read.sem, wa_read.at(n_read))
                    v.tensor_reduce(wa[:, k, side * HEADS:(side + 1) * HEADS],
                                    prod[:].rearrange("p (h c) -> p h c", h=HEADS), AX.X, ALU.add)\
                        .then_inc(wa_steps.sem, 2)
                    n += 2
        dve.wait_ge(wa_steps.sem, wa_steps.at(n))
        v.tensor_scalar(kn.wa_hi[:], wa[:], W_SCALE, None, ALU.mult).then_inc(wa_steps.sem, 1)
        dve.wait_ge(wa_steps.sem, wa_steps.at(n + 1))
        v.scalar_tensor_tensor(out=kn.wa_lo[:], in0=wa[:], scalar=W_SCALE, in1=kn.wa_hi[:],
                               op0=ALU.mult, op1=ALU.subtract).then_inc(wa_steps.sem, 1)
        v.memset(kn.bn_stats[:], 0.0).then_inc(wa_read.sem, 1)

    mem.close()
    return {"sync": sync, "gpsimd": gpsimd, "scalar": scalar, "vector": vector}


def tiles_stage(kn):
    nc, d, dram, take = kn.nc, kn.d, kn.dram, kn.sig.take
    T = d.tiles
    mem = ExitStack()

    def sb(name, shape, dt):
        return kn.buffer(mem, name, shape, dt)

    rec = sb("rec", [P, T, 4], I32)
    equal_next = sb("equal_next", [P, T], F32)
    next_f = sb("next_f", [P, T], F32)
    spread = [sb(f"spread{u}", [P, P], F32) for u in range(2)]
    same_f = [sb(f"same_f{u}", [P, P], F32) for u in range(2)]
    one = [sb(f"one{u}", [P, 1], F32) for u in range(2)]
    tmp = sb("tmp", [P, T], F32)
    row_ps = [kn.bank[u][:, 0:P] for u in range(2)]
    count_ps = [kn.bank[2 + u][:, 0:1] for u in range(2)]

    rec_in = take("rec_in", 16 * 6)
    cols = take("cols", 9)
    spread_done = kn.sig.pair("spread_done", T // 2)
    row_done = kn.sig.pair("row_done", T // 2)
    same_done = kn.sig.pair("same_done", T // 2)
    same_f_done = kn.sig.pair("same_f_done", T // 2)
    count_done = kn.sig.pair("count_done", T // 2)
    carried = kn.sig.pair("carried", T // 2)
    counts = take("counts", T)
    ends = take("ends", 6)

    def rows(first, partitions, step, n):
        base = dram["sorted"]
        return bass.AP(base.tensor, base.offset + 2 * first, [[2, partitions], [2 * step, n], [1, 4]])

    def sync(sp):
        sp.dma_start(rec[1:96], rows(1, 95, EDGES, T)).then_inc(rec_in.sem, 16)
        sp.dma_start(rec[97:128], rows(96, 31, EDGES, T)).then_inc(rec_in.sem, 16)
        for u in range(2):
            for p, first in ((CARRY_IN[u], u * EDGES), (CARRY_OUT[u], (u + 1) * EDGES)):
                sp.dma_start(rec[p:p + 1, u:T:2, :], rows(first, 1, 2 * EDGES, T // 2)).then_inc(rec_in.sem, 16)

    def vector(dve):
        v = nc.vector
        dve.wait_ge(rec_in.sem, rec_in.at(16 * 6))
        v.tensor_copy(kn.dst_f[:], rec[:, :, 1]).then_inc(cols.sem, 1)
        v.tensor_copy(next_f[:], rec[:, :, 3]).then_inc(cols.sem, 1)
        v.tensor_copy(kn.src_i[:], rec[:, :, 0]).then_inc(cols.sem, 1)
        v.tensor_copy(kn.dst_i[:], rec[:, :, 1]).then_inc(cols.sem, 1)
        dve.wait_ge(cols.sem, cols.at(2))
        v.tensor_tensor(equal_next[:], kn.dst_f[:], next_f[:], ALU.is_equal).then_inc(cols.sem, 1)
        dve.wait_ge(cols.sem, cols.at(5))
        v.scalar_tensor_tensor(out=kn.final_i[:], in0=equal_next[:], scalar=float(FAR), in1=kn.dst_f[:],
                               op0=ALU.mult, op1=ALU.add).then_inc(cols.sem, 1)
        dve.wait_ge(cols.sem, cols.at(6))
        for u in range(2):
            v.memset(kn.final_i[CARRY_IN[u]:CARRY_IN[u] + 1, u:T:2], FAR).then_inc(cols.sem, 1)
        for u in range(2):
            ins = v.memset(one[u][:], 1.0)
        ins.then_inc(cols.sem, 1)
        dve.wait_ge(cols.sem, cols.at(9))

        def tile(i, u, last):
            t = i * 2 + u
            c = CARRY_OUT[u]
            v.tensor_scalar(spread[u][:], kn.ones[:], kn.dst_f[:, ds(t, 1)], None, ALU.mult)\
                .then_inc(spread_done[u].sem, 1)
            dve.wait_ge(row_done[u].sem, row_done[u].at(i + 1))
            v.tensor_scalar(same_f[u][:], row_ps[u], kn.dst_f[:, ds(t, 1)], None, ALU.is_equal)\
                .then_inc(same_f_done[u].sem, 1)
            v.tensor_scalar(kn.same[:, ds(t * P, P)], row_ps[u], kn.dst_f[:, ds(t, 1)], None, ALU.is_equal)\
                .then_inc(same_done[u].sem, 1)
            dve.wait_ge(count_done[u].sem, count_done[u].at(i + 1))
            v.tensor_copy(kn.count[:, ds(t, 1)], count_ps[u]).then_inc(counts.sem, 1)
            v.tensor_copy(one[1 - u][c:c + 1, :], count_ps[u][c:c + 1, :]).then_inc(carried[u].sem, 1)

        in_pairs(dve, T, tile)
        dve.wait_ge(counts.sem, counts.at(T))
        v.tensor_scalar(tmp[:], kn.count[:], 1.0, None, ALU.max).then_inc(ends.sem, 1)
        v.tensor_scalar(kn.dinv[:], kn.count[:], 1.0, None, ALU.add).then_inc(ends.sem, 1)
        dve.wait_ge(ends.sem, ends.at(1))
        v.reciprocal(kn.mean_scale[:], tmp[:]).then_inc(ends.sem, 1)

    def gpsimd(pool):
        pool.wait_ge(ends.sem, ends.at(3))
        nc.gpsimd.tensor_tensor(kn.dinv[:], kn.dinv[:], kn.minus_half[:], ALU.pow).then_inc(ends.sem, 3)

    def tensor(pe):
        def tile(i, u, last):
            pe.wait_ge(spread_done[u].sem, spread_done[u].at(i + 1))
            pe.matmul(row_ps[u], spread[u][:], kn.ident[:], start=True, stop=True).then_inc(row_done[u].sem, 1)
            pe.wait_ge(same_f_done[u].sem, same_f_done[u].at(i + 1))
            pe.wait_ge(carried[1 - u].sem, carried[1 - u].at(i + u))
            pe.matmul(count_ps[u], same_f[u][:], one[u][:], start=True, stop=True).then_inc(count_done[u].sem, 1)

        in_pairs(pe, T, tile)

    mem.close()
    return {"sync": sync, "vector": vector, "tensor": tensor, "gpsimd": gpsimd}


def edge_sum_stage(kn, rows_dram, in_scale, out_scale):
    nc, d, dram, take, pair = kn.nc, kn.d, kn.dram, kn.sig.take, kn.sig.pair
    T, H = d.tiles, d.tiles // 2
    mem = ExitStack()

    def two(name, shape, dt):
        return [kn.buffer(mem, f"{name}{u}", shape, dt) for u in range(2)]

    rows = two("e_rows", [P, D], F32)
    lhs = two("e_lhs", [P, P], F32)
    out = two("e_out", [P, D], F32)
    gather_at = two("e_gather_at", [P, 1], I32)
    final_at = two("e_final_at", [P, 1], I32)
    total = [kn.bank[u] for u in range(2)]

    indexed = take("indexed", 2 * T)
    gathered = pair("gathered", 16 * H, software=True)
    scattered = pair("scattered", 16 * H, software=True)
    lhs_ready = pair("lhs_ready", H)
    carried = pair("carried", H)
    summed = pair("summed", H)
    evacuated = pair("evacuated", H)
    start = take("start", 1)

    def gpsimd(pool):
        g = nc.gpsimd

        def gather(i, u, n):
            pool.wait_ge(gathered[u].sem, gathered[u].at(i * 16))
            g.tensor_copy(gather_at[u][:], kn.src_i[:, ds(i * 2 + u, 1)]).then_inc(indexed.sem, 1)
            pool.wait_ge(indexed.sem, indexed.at(n))
            pool.wait_ge(summed[u].sem, summed[u].at(i))
            settle(pool, kn)
            pool.indirect_dma_start(rows[u][:], None, rows_dram,
                                    bass.IndirectOffsetOnAxis(ap=gather_at[u][:], axis=0),
                                    bounds_check=d.padded - 1, oob_is_err=False)\
                .then_inc(gathered[u].sem, 16)

        def tile(i, u, last):
            prefetch = not (isinstance(i, int) and i == H - 1)
            pool.wait_ge(scattered[u].sem, scattered[u].at(i * 16))
            n = 2 + (i * 2 + u) * 2 + 1 if prefetch else 2 + 2 * (T - 2) + u + 1
            g.tensor_copy(final_at[u][:], kn.final_i[:, ds(i * 2 + u, 1)]).then_inc(indexed.sem, 1)
            pool.wait_ge(indexed.sem, indexed.at(n))
            pool.wait_ge(evacuated[u].sem, evacuated[u].at(i + 1))
            settle(pool, kn)
            pool.indirect_dma_start(dram["sum"], bass.IndirectOffsetOnAxis(ap=final_at[u][:], axis=0),
                                    out[u][:], None, bounds_check=d.nodes - 1, oob_is_err=False)\
                .then_inc(scattered[u].sem, 16)
            if prefetch:
                gather(i + 1, u, n + 1)

        for u in range(2):
            gather(0, u, u + 1)
        in_pairs(pool, T, tile)
        for u in range(2):
            pool.wait_ge(scattered[u].sem, scattered[u].at(16 * H))

    def vector(dve):
        v = nc.vector
        v.memset(total[1][0:1, :], 0.0).then_inc(start.sem, 1)

        def tile(i, u, last):
            t = i * 2 + u
            dve.wait_ge(summed[u].sem, summed[u].at(i))
            v.tensor_scalar(lhs[u][:], kn.same[:, ds(t * P, P)], in_scale[:, ds(t, 1)], None, ALU.mult)\
                .then_inc(lhs_ready[u].sem, 1)

        in_pairs(dve, T, tile)

    def scalar(act):
        act.wait_ge(start.sem, start.at(1))

        def carry(i, u):
            c = CARRY_IN[u]
            act.wait_ge(gathered[u].sem, gathered[u].at(i * 16 + 16))
            act.wait_ge(summed[1 - u].sem, summed[1 - u].at(i + u))
            act.copy(rows[u][c:c + 1, :], total[1 - u][c:c + 1, :]).then_inc(carried[u].sem, 1)

        def tile(i, u, last):
            if not last:
                carry(*following(i, u))
            act.wait_ge(summed[u].sem, summed[u].at(i + 1))
            act.wait_ge(scattered[u].sem, scattered[u].at(i * 16))
            act.activation(out[u][:], total[u][:], ACT.Copy, scale=out_scale[:, ds(i * 2 + u, 1)])\
               .then_inc(evacuated[u].sem, 1)

        carry(0, 0)
        in_pairs(act, T, tile)

    def tensor(pe):
        def tile(i, u, last):
            pe.wait_ge(lhs_ready[u].sem, lhs_ready[u].at(i + 1))
            pe.wait_ge(carried[u].sem, carried[u].at(i + 1))
            pe.wait_ge(evacuated[u].sem, evacuated[u].at(i))
            pe.matmul(total[u][:], lhs[u][:], rows[u][:], start=True, stop=True).then_inc(summed[u].sem, 1)

        in_pairs(pe, T, tile)

    mem.close()
    return {"gpsimd": gpsimd, "vector": vector, "scalar": scalar, "tensor": tensor}


def degree_stage(kn):
    nc, d, dram, take = kn.nc, kn.d, kn.dram, kn.sig.take
    T = d.tiles
    dinv_out = take("dinv_out", 16 * T, software=True)
    dinv_in = take("dinv_in", 16 * T, software=True)
    fixed = take("fixed", 2)

    def gpsimd(pool):
        for t in range(T):
            pool.indirect_dma_start(dram["dinv"], bass.IndirectOffsetOnAxis(ap=kn.final_i[:, t:t + 1], axis=0),
                                    kn.dinv[:, t:t + 1], None, bounds_check=d.nodes - 1, oob_is_err=False)\
                .then_inc(dinv_out.sem, 16)
        pool.wait_ge(dinv_out.sem, dinv_out.at(16 * T))
        for t in range(T):
            pool.indirect_dma_start(kn.src_dinv[:, t:t + 1], None, dram["dinv"],
                                    bass.IndirectOffsetOnAxis(ap=kn.src_i[:, t:t + 1], axis=0),
                                    bounds_check=d.padded - 1, oob_is_err=False).then_inc(dinv_in.sem, 16)
        pool.wait_ge(dinv_in.sem, dinv_in.at(16 * T))
        for u in range(2):
            nc.gpsimd.memset(kn.src_dinv[CARRY_IN[u]:CARRY_IN[u] + 1, u:T:2], 1.0).then_inc(fixed.sem, 1)
        pool.wait_ge(fixed.sem, fixed.at(2))

    return {"gpsimd": gpsimd}


def edge_attention_stage(kn, rows_dram, logits_dram):
    nc, d, dram, take, pair = kn.nc, kn.d, kn.dram, kn.sig.take, kn.sig.pair
    T, H = d.tiles, d.tiles // 2
    mem = ExitStack()

    def two(name, shape, dt):
        return [kn.buffer(mem, f"{name}{u}", shape, dt) for u in range(2)]

    K = HEADS
    rows = two("a_rows_", [P, HC], F32)
    src_al = two("a_src", [P, 2 * K], F32)
    dst_al = two("a_dst", [P, 2 * K], F32)
    tmp = two("a_tmp", [P, K], F32)
    score = two("a_score", [P, 2 * K], F32)
    spread = two("a_spread", [P, K, P], F32)
    pen = two("a_pen", [P, P], F32)
    masked = two("a_masked", [P, K, P], F32)
    top = two("a_top", [P, K], F32)
    shifted = two("a_shifted", [P, 2 * K], F32)
    weight = two("a_weight", [P, 2 * K], F32)
    lhs = two("a_lhs", [P, K, P], F32)
    dval = two("a_dval", [P, K], F32)
    den = two("a_den", [P, K], F32)
    rden = two("a_rden", [P, K], F32)
    out = two("a_out", [P, HC + K], F32)
    gather_at = two("a_gather_at", [P, 1], I32)
    dst_at = two("a_dst_at", [P, 1], I32)
    final_at = two("a_final_at", [P, 1], I32)
    total = [[kn.bank[2 * u], kn.bank[2 * u + 1]] for u in range(2)]
    row_ps = [kn.bank[4 + u][:].rearrange("p (h q) -> p h q", h=K) for u in range(2)]
    den_ps = [kn.bank[6 + u][:, 0:K] for u in range(2)]

    indexed = take("indexed", 3 * T)
    gathered = pair("gathered", 16 * H, software=True)
    src_in = pair("src_in", 16 * H, software=True)
    dst_in = pair("dst_in_", 16 * H, software=True)
    scattered = pair("scattered", 16 * H, software=True)
    FRONT, BACK = 8, 3
    front = Steps(take("front_steps", FRONT * T))
    back = Steps(take("back_steps", BACK * T))
    spread_ready = pair("spread_ready", H)
    row_done = pair("row_done", H)
    shift_ready = pair("shift_ready", H)
    weighed = pair("weighed", H)
    lhs_ready = pair("lhs_ready", H)
    den_done = pair("den_done", H)
    summed = pair("summed", H)
    carried = pair("carried", H)
    rden_ready = pair("rden_ready", H)
    evacuated = pair("evacuated", H)
    start = take("start", 4)

    def gpsimd(pool):
        g = nc.gpsimd

        def gather(i, u, n):
            t = i * 2 + u
            pool.wait_ge(gathered[u].sem, gathered[u].at(i * 16))
            pool.wait_ge(src_in[u].sem, src_in[u].at(i * 16))
            pool.wait_ge(dst_in[u].sem, dst_in[u].at(i * 16))
            g.tensor_copy(gather_at[u][:], kn.src_i[:, ds(t, 1)]).then_inc(indexed.sem, 1)
            g.tensor_copy(dst_at[u][:], kn.dst_i[:, ds(t, 1)]).then_inc(indexed.sem, 1)
            pool.wait_ge(indexed.sem, indexed.at(n))
            pool.wait_ge(shift_ready[u].sem, shift_ready[u].at(i))
            settle(pool, kn)
            for to, sem, at in ((src_al[u], src_in[u], gather_at[u]), (dst_al[u], dst_in[u], dst_at[u])):
                pool.indirect_dma_start(to[:], None, logits_dram, bass.IndirectOffsetOnAxis(ap=at[:], axis=0),
                                        bounds_check=d.padded - 1, oob_is_err=False).then_inc(sem.sem, 16)
            pool.wait_ge(summed[u].sem, summed[u].at(i))
            settle(pool, kn)
            pool.indirect_dma_start(rows[u][:], None, rows_dram,
                                    bass.IndirectOffsetOnAxis(ap=gather_at[u][:], axis=0),
                                    bounds_check=d.padded - 1, oob_is_err=False)\
                .then_inc(gathered[u].sem, 16)

        def tile(i, u, last):
            prefetch = not (isinstance(i, int) and i == H - 1)
            n = 4 + (i * 2 + u) * 3 + 1 if prefetch else 4 + 3 * (T - 2) + u + 1
            pool.wait_ge(scattered[u].sem, scattered[u].at(i * 16))
            g.tensor_copy(final_at[u][:], kn.final_i[:, ds(i * 2 + u, 1)]).then_inc(indexed.sem, 1)
            pool.wait_ge(indexed.sem, indexed.at(n))
            pool.wait_ge(evacuated[u].sem, evacuated[u].at(i + 1))
            settle(pool, kn)
            pool.indirect_dma_start(dram["sum_gat"], bass.IndirectOffsetOnAxis(ap=final_at[u][:], axis=0),
                                    out[u][:], None, bounds_check=d.nodes - 1, oob_is_err=False)\
                .then_inc(scattered[u].sem, 16)
            if prefetch:
                gather(i + 1, u, n + 2)

        for u in range(2):
            gather(0, u, 2 * u + 2)
        in_pairs(pool, T, tile)
        for u in range(2):
            pool.wait_ge(scattered[u].sem, scattered[u].at(16 * H))

    def vector(dve):
        v = nc.vector
        v.memset(total[1][0][0:1, :], 0.0).then_inc(start.sem, 1)
        v.memset(total[1][1][0:1, :], 0.0).then_inc(start.sem, 1)
        v.memset(den_ps[1][0:1, :], 1.0).then_inc(start.sem, 1)
        v.memset(top[1][0:1, :], 0.0)
        for u in range(2):
            ins = v.memset(dval[u][:], 1.0)
        ins.then_inc(start.sem, 1)
        dve.wait_ge(start.sem, start.at(4))

        def scores(i, u):
            t = i * 2 + u
            c = CARRY_IN[u]
            front.begin(t * FRONT)
            own = front.sig.sem
            dve.wait_ge(src_in[u].sem, src_in[u].at(i * 16 + 16))
            dve.wait_ge(dst_in[u].sem, dst_in[u].at(i * 16 + 16))
            dve.wait_ge(weighed[u].sem, weighed[u].at(i))
            front.mark(v.tensor_tensor(score[u][:, 0:K], src_al[u][:, 0:K], dst_al[u][:, K:2 * K], ALU.add))
            n = front.mark(v.tensor_tensor(score[u][:, K:2 * K], dst_al[u][:, 0:K], dst_al[u][:, K:2 * K], ALU.add))
            dve.wait_ge(own, n)
            n = front.mark(v.scalar_tensor_tensor(out=score[u][:], in0=score[u][:], scalar=SLOPE, in1=score[u][:],
                                                  op0=ALU.mult, op1=ALU.max))
            front.mark(v.tensor_scalar(pen[u][:], kn.same[:, ds(t * P, P)], BIG, -BIG, ALU.mult, ALU.add))
            dve.wait_ge(own, n)
            n = front.mark(v.tensor_copy(score[u][c:c + 1, 0:K], top[1 - u][c:c + 1, :]))
            dve.wait_ge(own, n)
            v.tensor_copy(spread[u][:], score[u][:, 0:K].unsqueeze(2).broadcast_to([P, K, P]))\
                .then_inc(spread_ready[u].sem, 1)
            dve.wait_ge(row_done[u].sem, row_done[u].at(i + 1))
            n = front.mark(v.tensor_tensor(masked[u][:], row_ps[u], pen[u][:].unsqueeze(1).broadcast_to([P, K, P]),
                                           ALU.add))
            dve.wait_ge(own, n)
            n = front.mark(v.tensor_reduce(top[u][:], masked[u][:], AX.X, ALU.max))
            dve.wait_ge(own, n)
            n = front.mark(v.tensor_tensor(top[u][:], top[u][:], score[u][:, K:2 * K], ALU.max))
            dve.wait_ge(own, n)
            v.tensor_tensor(shifted[u][:, 0:K], score[u][:, 0:K], top[u][:], ALU.subtract)
            v.tensor_tensor(shifted[u][:, K:2 * K], score[u][:, K:2 * K], top[u][:], ALU.subtract)\
                .then_inc(shift_ready[u].sem, 1)
            assert front.n == FRONT

        def sums(i, u, last):
            c = CARRY_IN[u]
            t = i * 2 + u
            back.begin(t * BACK)
            own = back.sig.sem
            if not last:
                scores(*following(i, u))
            dve.wait_ge(weighed[u].sem, weighed[u].at(i + 1))
            dve.wait_ge(summed[u].sem, summed[u].at(i))
            dve.wait_ge(den_done[1 - u].sem, den_done[1 - u].at(i + u))
            back.mark(v.tensor_copy(dval[u][c:c + 1, :], den_ps[1 - u][c:c + 1, :]))
            v.tensor_tensor(lhs[u][:], kn.same[:, ds(t * P, P)].unsqueeze(1).broadcast_to([P, K, P]),
                            weight[u][:, 0:K].unsqueeze(2).broadcast_to([P, K, P]), ALU.mult)\
                .then_inc(lhs_ready[u].sem, 1)
            dve.wait_ge(den_done[u].sem, den_done[u].at(i + 1))
            n = back.mark(v.tensor_tensor(den[u][:], den_ps[u], weight[u][:, K:2 * K], ALU.add))
            dve.wait_ge(own, n)
            dve.wait_ge(evacuated[u].sem, evacuated[u].at(i))
            dve.wait_ge(scattered[u].sem, scattered[u].at(i * 16))
            n = back.mark(v.reciprocal(rden[u][:], den[u][:]))
            dve.wait_ge(own, n)
            v.tensor_tensor(out[u][:, HC:HC + K], weight[u][:, K:2 * K], rden[u][:], ALU.mult)\
                .then_inc(rden_ready[u].sem, 1)
            assert back.n == BACK

        scores(0, 0)
        in_pairs(dve, T, sums)

    def scalar(act):
        act.wait_ge(start.sem, start.at(4))

        def weigh(i, u):
            act.wait_ge(shift_ready[u].sem, shift_ready[u].at(i + 1))
            act.wait_ge(rden_ready[u].sem, rden_ready[u].at(i))
            act.activation(weight[u][:], shifted[u][:], ACT.Exp).then_inc(weighed[u].sem, 1)

        def tile(i, u, last):
            c = CARRY_IN[u]
            act.wait_ge(gathered[u].sem, gathered[u].at(i * 16 + 16))
            act.wait_ge(summed[1 - u].sem, summed[1 - u].at(i + u))
            act.copy(rows[u][c:c + 1, 0:D], total[1 - u][0][c:c + 1, :])
            act.copy(rows[u][c:c + 1, D:HC], total[1 - u][1][c:c + 1, :]).then_inc(carried[u].sem, 1)
            if not last:
                weigh(*following(i, u))
            act.wait_ge(rden_ready[u].sem, rden_ready[u].at(i + 1))
            act.wait_ge(summed[u].sem, summed[u].at(i + 1))
            act.wait_ge(scattered[u].sem, scattered[u].at(i * 16))
            for h in range(K):
                ins = act.activation(out[u][:, h * C:(h + 1) * C],
                                     total[u][h // 2][:, (h % 2) * C:(h % 2 + 1) * C], ACT.Copy,
                                     scale=rden[u][:, h:h + 1])
            ins.then_inc(evacuated[u].sem, 1)

        weigh(0, 0)
        in_pairs(act, T, tile)

    def tensor(pe):
        def score_rows(i, u):
            pe.wait_ge(spread_ready[u].sem, spread_ready[u].at(i + 1))
            for h in range(K):
                mm = pe.matmul(row_ps[u][:, h, :], spread[u][:, h, :], kn.ident[:], start=True, stop=True)
            mm.then_inc(row_done[u].sem, 1)

        def tile(i, u, last):
            if not last:
                score_rows(*following(i, u))
            pe.wait_ge(lhs_ready[u].sem, lhs_ready[u].at(i + 1))
            pe.wait_ge(rden_ready[u].sem, rden_ready[u].at(i))
            for h in range(K):
                mm = pe.matmul(den_ps[u][:, h:h + 1], lhs[u][:, h, :], dval[u][:, h:h + 1], start=True, stop=True)
            mm.then_inc(den_done[u].sem, 1)
            pe.wait_ge(carried[u].sem, carried[u].at(i + 1))
            pe.wait_ge(evacuated[u].sem, evacuated[u].at(i))
            for h in range(K):
                mm = pe.matmul(total[u][h // 2][:, (h % 2) * C:(h % 2 + 1) * C], lhs[u][:, h, :],
                               rows[u][:, h * C:(h + 1) * C], start=True, stop=True)
            mm.then_inc(summed[u].sem, 1)

        score_rows(0, 0)
        in_pairs(pe, T, tile)

    mem.close()
    return {"gpsimd": gpsimd, "vector": vector, "scalar": scalar, "tensor": tensor}


class Norm:

    def __init__(self, kn, mem):
        self.kn, self.nc, n = kn, kn.nc, kn.d.groups
        self.stats = kn.buffer(mem, "n_stats", [P, S, 6], F32)
        self.moments = kn.buffer(mem, "n_moments", [P, S, 2], F32)
        self.power = kn.buffer(mem, "n_power", [P, S], F32)
        self.seen = kn.sig.take("n_seen", 2 * S * n)
        self.rstd = kn.sig.take("n_rstd", 2 * n)

    def moments_of(self, dve, row, s, g):
        self.nc.vector.bn_stats(self.stats[:, s, :], row).then_inc(self.seen.sem, 1)
        dve.wait_ge(self.seen.sem, self.seen.at(g * (2 * S) + 2 * s + 1))
        settle(dve, self.kn)
        self.nc.vector.bn_aggr(self.moments[:, s, :], self.stats[:, s, :]).then_inc(self.seen.sem, 1)

    def pool(self, pool, g):
        pool.wait_ge(self.seen.sem, self.seen.at(g * (2 * S) + 2 * S))
        self.nc.gpsimd.tensor_tensor(self.power[:], self.moments[:, :, 1], self.kn.eps[:], ALU.add)\
            .then_inc(self.rstd.sem, 1)
        pool.wait_ge(self.rstd.sem, self.rstd.at(g * 2 + 1))
        self.nc.gpsimd.tensor_tensor(self.power[:], self.power[:], self.kn.minus_half[:, 0:1].broadcast_to([P, S]),
                                     ALU.pow).then_inc(self.rstd.sem, 1)

    def apply(self, dve, out, rows, g, signal):
        dve.wait_ge(self.rstd.sem, self.rstd.at(g * 2 + 2))
        for s in range(S):
            self.nc.vector.tensor_scalar(out[:, s, :], rows[:, s, :], self.moments[:, s, 0:1],
                                         self.power[:, s:s + 1], ALU.subtract, ALU.mult).then_inc(signal.sem, 1)


def node_rows(ap, i, u):
    return ap[ds(i * (2 * GROUP) + u * GROUP, GROUP), :].rearrange("(s p) c -> p s c", p=P)


def gin_stage(kn):
    nc, d, dram, take, pair = kn.nc, kn.d, kn.dram, kn.sig.take, kn.sig.pair
    G, H = d.groups, d.groups // 2
    mem = ExitStack()

    def two(name, shape, dt):
        return [kn.buffer(mem, f"{name}{u}", shape, dt) for u in range(2)]

    x = two("g_x", [P, S, D], F32)
    z = two("g_z", [P, S, D], F32)
    z_hi = kn.buffer(mem, "g_z_hi", [P, 4, D], F16)
    z_lo = kn.buffer(mem, "g_z_lo", [P, 4, D], F16)
    r_f = two("g_r", [P, D], F32)
    r_hi = kn.buffer(mem, "g_r_hi", [P, 4, D], F16)
    r_lo = kn.buffer(mem, "g_r_lo", [P, 4, D], F16)
    y = kn.buffer(mem, "g_y", [P, S, D], F32)
    norm = Norm(kn, mem)
    tp = [kn.bank[0], kn.bank[1]]
    mm = [kn.bank[2 + n] for n in range(4)]

    x_in = pair("x_in", 16 * H)
    sum_in = pair("sum_in", 16 * H)
    z_ready = pair("z_ready", H * S)
    x_ready = pair("x_ready", H)
    turned = take("turned", 4 * G)
    hi_done = take("hi_done", 4 * G)
    lo_done = take("lo_done", 4 * G)
    mid = take("mid", 4 * G)
    r_done = take("r_done", 4 * G)
    r_hi_done = take("r_hi_done", 4 * G)
    r_lo_done = take("r_lo_done", 4 * G)
    prod = take("prod", S * G)
    y_done = take("y_done", S * G)
    rows_out = pair("rows_out", S * H)
    stored = pair("stored", 16 * H)

    def sync(sp):
        def load(i, u):
            sp.wait_ge(rows_out[u].sem, rows_out[u].at(i * S))
            sp.dma_start(x[u][:], node_rows(dram["x"], i, u)).then_inc(x_in[u].sem, 16)
            sp.wait_ge(stored[u].sem, stored[u].at(i * 16))
            sp.dma_start(z[u][:], node_rows(dram["sum"], i, u)).then_inc(sum_in[u].sem, 16)

        def group(i, u, last):
            if not last:
                load(*following(i, u))
            sp.wait_ge(rows_out[u].sem, rows_out[u].at(i * S + S))
            sp.dma_start(node_rows(dram["x1"], i, u), z[u][:]).then_inc(stored[u].sem, 16)

        load(0, 0)
        in_pairs(sp, G, group)
        for u in range(2):
            sp.wait_ge(stored[u].sem, stored[u].at(16 * H))

    def gpsimd(pool):
        def group(i, u, last):
            pool.wait_ge(z_ready[u].sem, z_ready[u].at(i * S + S))
            nc.gpsimd.tensor_tensor(x[u][:], x[u][:], kn.gin_b2[:].unsqueeze(1).broadcast_to([P, S, D]), ALU.add)\
                .then_inc(x_ready[u].sem, 1)
            norm.pool(pool, i * 2 + u)

        in_pairs(pool, G, group)

    def vector(dve):
        v = nc.vector

        def add_sums(i, u):
            dve.wait_ge(x_in[u].sem, x_in[u].at(i * 16 + 16))
            dve.wait_ge(sum_in[u].sem, sum_in[u].at(i * 16 + 16))
            for s in range(S):
                v.tensor_tensor(z[u][:, s, :], z[u][:, s, :], x[u][:, s, :], ALU.add).then_inc(z_ready[u].sem, 1)

        def low_parts(i, u):
            g = i * 2 + u
            for k in range(4):
                dve.wait_ge(hi_done.sem, hi_done.at(g * 4 + k + 1))
                v.scalar_tensor_tensor(out=z_lo[:, k, :], in0=tp[k % 2][:], scalar=GIN_SCALE, in1=z_hi[:, k, :],
                                       op0=ALU.mult, op1=ALU.subtract).then_inc(lo_done.sem, 1)

        def group(i, u, last):
            g = i * 2 + u
            if not last:
                add_sums(*following(i, u))
            for m in range(4):
                dve.wait_ge(r_hi_done.sem, r_hi_done.at(g * 4 + m + 1))
                v.tensor_tensor(r_lo[:, m, :], r_f[m % 2][:], r_hi[:, m, :], ALU.subtract).then_inc(r_lo_done.sem, 1)
            if not last:
                low_parts(*following(i, u))
            dve.wait_ge(x_ready[u].sem, x_ready[u].at(i + 1))
            for s in range(S):
                dve.wait_ge(prod.sem, prod.at(g * S + s + 1))
                v.scalar_tensor_tensor(out=y[:, s, :], in0=mm[s][:], scalar=GIN_UNSCALE, in1=x[u][:, s, :],
                                       op0=ALU.mult, op1=ALU.add).then_inc(y_done.sem, 1)
                dve.wait_ge(y_done.sem, y_done.at(g * S + s + 1))
                norm.moments_of(dve, y[:, s, :], s, g)
            norm.apply(dve, z[u], y, g, rows_out[u])

        add_sums(0, 0)
        low_parts(0, 0)
        in_pairs(dve, G, group)

    def scalar(act):
        def high_parts(i, u):
            g = i * 2 + u
            for k in range(4):
                act.wait_ge(turned.sem, turned.at(g * 4 + k + 1))
                act.activation(z_hi[:, k, :], tp[k % 2][:], ACT.Copy, scale=GIN_SCALE).then_inc(hi_done.sem, 1)

        def group(i, u, last):
            g = i * 2 + u
            for m in range(4):
                act.wait_ge(mid.sem, mid.at(g * 4 + m + 1))
                if m >= 2:
                    act.wait_ge(r_lo_done.sem, r_lo_done.at(g * 4 + m - 1))
                act.wait_ge(prod.sem, prod.at(g * S))
                act.activation(r_f[m % 2][:], mm[m][:], ACT.Relu, scale=GIN_UNSCALE * GIN_SCALE,
                               bias=kn.vec_scaled[:, V_GIN_B1 + m:V_GIN_B1 + m + 1]).then_inc(r_done.sem, 1)
                act.wait_ge(r_done.sem, r_done.at(g * 4 + m + 1))
                act.copy(r_hi[:, m, :], r_f[m % 2][:]).then_inc(r_hi_done.sem, 1)
            if not last:
                high_parts(*following(i, u))

        high_parts(0, 0)
        in_pairs(act, G, group)

    def tensor(pe):
        def turn(i, u):
            g = i * 2 + u
            pe.wait_ge(z_ready[u].sem, z_ready[u].at(i * S + S))
            for k in range(4):
                if k >= 2:
                    pe.wait_ge(lo_done.sem, lo_done.at(g * 4 + k - 1))
                else:
                    pe.wait_ge(lo_done.sem, lo_done.at(g * 4))
                for s in range(S):
                    ins = pe.transpose(tp[k % 2][:, s * P:(s + 1) * P], z[u][:, s, k * P:(k + 1) * P], kn.ident[:])
                ins.then_inc(turned.sem, 1)

        def group(i, u, last):
            g = i * 2 + u
            pe.wait_ge(lo_done.sem, lo_done.at(g * 4 + 4))
            pe.wait_ge(y_done.sem, y_done.at(g * S))
            for m in range(4):
                split_product(pe, mm[m][:],
                              lambda k: (kn.weights(False, W_GIN1, k, 0, D)[:, m * P:(m + 1) * P],
                                         kn.weights(True, W_GIN1, k, 0, D)[:, m * P:(m + 1) * P]),
                              lambda k: (z_hi[:, k, :], z_lo[:, k, :]), 4).then_inc(mid.sem, 1)
            if not last:
                turn(*following(i, u))
            pe.wait_ge(r_lo_done.sem, r_lo_done.at(g * 4 + 4))
            for s in range(S):
                split_product(pe, mm[s][:],
                              lambda k: (r_hi[:, k, s * P:(s + 1) * P], r_lo[:, k, s * P:(s + 1) * P]),
                              lambda k: (kn.weights(False, W_GIN2, k, 0, D), kn.weights(True, W_GIN2, k, 0, D)),
                              4).then_inc(prod.sem, 1)

        turn(0, 0)
        in_pairs(pe, G, group)

    mem.close()
    return {"sync": sync, "gpsimd": gpsimd, "vector": vector, "scalar": scalar, "tensor": tensor}


def linear_stage(kn, layer):
    nc, d, dram, take, pair = kn.nc, kn.d, kn.dram, kn.sig.take, kn.sig.pair
    G, H = d.groups, d.groups // 2
    sage = layer == "sage"
    chunks = 8 if sage else 4
    unit = W_SAGE_L if sage else W_GCN
    bias = V_SAGE_B if sage else V_GCN_B
    x_dram = dram["x1"] if sage else dram["x3"]
    mem = ExitStack()

    def two(name, shape, dt):
        return [kn.buffer(mem, f"{name}{u}", shape, dt) for u in range(2)]

    x = two("l_x", [P, S, D], F32)
    z = two("l_z", [P, S, D], F32)
    node_dinv = two("l_dinv", [P, S, 1], F32)
    z_hi = kn.buffer(mem, "l_z_hi", [P, 2, chunks, D], F16)
    z_lo = kn.buffer(mem, "l_z_lo", [P, 2, chunks, D], F16)
    h = kn.buffer(mem, "l_h", [P, 4, D], F32)
    tp = [kn.bank[0], kn.bank[1]]
    mm = [kn.bank[2 + n] for n in range(4)]

    x_in = pair("x_in", 16 * H)
    sum_in = pair("sum_in", 16 * H)
    dinv_in = pair("dinv_in_", 0 if sage else 16 * H)
    z_ready = pair("z_ready", 0 if sage else H * 2 * S)
    turned = pair("turned", chunks * H)
    hi_done = take("hi_done", chunks * G)
    lo_done = take("lo_done", chunks * G)
    mid = take("mid", 4 * G)
    h_done = take("h_done", 4 * G)
    seen = take("h_seen", 4 * G)
    stored = take("h_stored", 16 * G)

    def sync(sp):
        def load(i, u):
            sp.wait_ge(turned[u].sem, turned[u].at(i * chunks))
            sp.dma_start(x[u][:], node_rows(x_dram, i, u)).then_inc(x_in[u].sem, 16)
            sp.dma_start(z[u][:], node_rows(dram["sum"], i, u)).then_inc(sum_in[u].sem, 16)
            if not sage:
                sp.dma_start(node_dinv[u][:], node_rows(dram["dinv"], i, u),
                             allow_slow_non_contiguous=True).then_inc(dinv_in[u].sem, 16)

        def group(i, u, last):
            g = i * 2 + u
            if not last:
                load(*following(i, u))
            sp.wait_ge(h_done.sem, h_done.at(g * 4 + 4))
            settle(sp, kn)
            sp.dma_start(dram["h"][:, :, ds(i * (2 * GROUP) + u * GROUP, GROUP)].rearrange("m p n -> p m n"), h[:])\
                .then_inc(stored.sem, 16)

        load(0, 0)
        in_pairs(sp, G, group)
        sp.wait_ge(stored.sem, stored.at(16 * G))

    def vector(dve):
        v = nc.vector

        def scale(i, u):
            if sage:
                return
            dve.wait_ge(x_in[u].sem, x_in[u].at(i * 16 + 16))
            dve.wait_ge(sum_in[u].sem, sum_in[u].at(i * 16 + 16))
            dve.wait_ge(dinv_in[u].sem, dinv_in[u].at(i * 16 + 16))
            for s in range(S):
                v.scalar_tensor_tensor(out=z[u][:, s, :], in0=x[u][:, s, :], scalar=node_dinv[u][:, s, :],
                                       in1=z[u][:, s, :], op0=ALU.mult, op1=ALU.add).then_inc(z_ready[u].sem, 1)
            dve.wait_ge(z_ready[u].sem, z_ready[u].at(i * (2 * S) + S))
            for s in range(S):
                v.tensor_scalar(z[u][:, s, :], z[u][:, s, :], node_dinv[u][:, s, :], None, ALU.mult)\
                    .then_inc(z_ready[u].sem, 1)

        def low_parts(i, u):
            g = i * 2 + u
            for k in range(chunks):
                dve.wait_ge(hi_done.sem, hi_done.at(g * chunks + k + 1))
                v.scalar_tensor_tensor(out=z_lo[:, u, k, :], in0=tp[k % 2][:], scalar=A_SCALE, in1=z_hi[:, u, k, :],
                                       op0=ALU.mult, op1=ALU.subtract).then_inc(lo_done.sem, 1)

        def group(i, u, last):
            g = i * 2 + u

            def statistics(ms):
                real = d.last_real if last else GROUP
                for m in ms:
                    dve.wait_ge(h_done.sem, h_done.at(g * 4 + m + 1))
                    v.bn_stats(kn.bn_stats[:, m, ds(g * 6, 6)], h[:, m, 0:real]).then_inc(seen.sem, 1)

            if not last:
                scale(*following(i, u))
            statistics(range(2))
            if not last:
                low_parts(*following(i, u))
            statistics(range(2, 4))

        scale(0, 0)
        low_parts(0, 0)
        in_pairs(dve, G, group)

    def scalar(act):
        def high_parts(i, u):
            g = i * 2 + u
            for k in range(chunks):
                act.wait_ge(turned[u].sem, turned[u].at(i * chunks + k + 1))
                act.activation(z_hi[:, u, k, :], tp[k % 2][:], ACT.Copy, scale=A_SCALE).then_inc(hi_done.sem, 1)

        def group(i, u, last):
            g = i * 2 + u

            def out(ms):
                for m in ms:
                    act.wait_ge(mid.sem, mid.at(g * 4 + m + 1))
                    act.activation(h[:, m, :], mm[m][:], ACT.Identity, scale=UNSCALE,
                                   bias=kn.vec[:, bias + m:bias + m + 1]).then_inc(h_done.sem, 1)

            act.wait_ge(stored.sem, stored.at(g * 16))
            act.wait_ge(seen.sem, seen.at(g * 4))
            out(range(2))
            if not last:
                high_parts(*following(i, u))
            out(range(2, 4))

        high_parts(0, 0)
        in_pairs(act, G, group)

    def tensor(pe):
        def turn(i, u):
            g = i * 2 + u
            if sage:
                pe.wait_ge(x_in[u].sem, x_in[u].at(i * 16 + 16))
                pe.wait_ge(sum_in[u].sem, sum_in[u].at(i * 16 + 16))
            else:
                pe.wait_ge(z_ready[u].sem, z_ready[u].at(i * (2 * S) + 2 * S))
            for k in range(chunks):
                pe.wait_ge(lo_done.sem, lo_done.at(g * chunks + (k - 1 if k >= 2 else 0)))
                rows = z[u] if k < 4 else x[u]
                for s in range(S):
                    ins = pe.transpose(tp[k % 2][:, s * P:(s + 1) * P], rows[:, s, (k % 4) * P:(k % 4 + 1) * P],
                                       kn.ident[:])
                ins.then_inc(turned[u].sem, 1)

        def group(i, u, last):
            g = i * 2 + u
            pe.wait_ge(lo_done.sem, lo_done.at(g * chunks + chunks))
            pe.wait_ge(h_done.sem, h_done.at(g * 4))
            for m in range(4):
                if m == 2 and not last:
                    turn(*following(i, u))
                split_product(pe, mm[m][:],
                              lambda k: (kn.weights(False, unit, k, 0, D)[:, m * P:(m + 1) * P],
                                         kn.weights(True, unit, k, 0, D)[:, m * P:(m + 1) * P]),
                              lambda k: (z_hi[:, u, k, :], z_lo[:, u, k, :]), chunks).then_inc(mid.sem, 1)

        turn(0, 0)
        in_pairs(pe, G, group)

    mem.close()
    return {"sync": sync, "vector": vector, "scalar": scalar, "tensor": tensor}


def norm_coefficients_stage(kn, gamma, beta):
    nc, take = kn.nc, kn.sig.take
    mem = ExitStack()
    mv = kn.buffer(mem, "c_mv", [P, 4, 2], F32)
    rstd = kn.buffer(mem, "c_rstd", [P, 4], F32)
    neg = kn.buffer(mem, "c_neg", [P, 4], F32)
    steps = take("coef_steps", 9)

    def vector(dve):
        v = nc.vector
        for m in range(4):
            v.bn_aggr(mv[:, m, :], kn.bn_stats[:, m, :]).then_inc(steps.sem, 1)
        dve.wait_ge(steps.sem, steps.at(6))
        v.tensor_tensor(kn.bn_scale[:], rstd[:], kn.vec[:, gamma:gamma + 4], ALU.mult).then_inc(steps.sem, 1)
        dve.wait_ge(steps.sem, steps.at(7))
        v.tensor_tensor(neg[:], mv[:, :, 0], kn.bn_scale[:], ALU.mult).then_inc(steps.sem, 1)
        dve.wait_ge(steps.sem, steps.at(8))
        v.tensor_tensor(kn.bn_shift[:], kn.vec[:, beta:beta + 4], neg[:], ALU.subtract).then_inc(steps.sem, 1)

    def gpsimd(pool):
        g = nc.gpsimd
        pool.wait_ge(steps.sem, steps.at(4))
        g.tensor_scalar(rstd[:], mv[:, :, 1], EPS, None, ALU.add).then_inc(steps.sem, 1)
        pool.wait_ge(steps.sem, steps.at(5))
        g.tensor_tensor(rstd[:], rstd[:], kn.minus_half[:, 0:1].broadcast_to([P, 4]), ALU.pow).then_inc(steps.sem, 1)

    mem.close()
    return {"vector": vector, "gpsimd": gpsimd}


def batch_norm_stage(kn, layer):
    nc, d, dram, take, pair = kn.nc, kn.d, kn.dram, kn.sig.take, kn.sig.pair
    G, H = d.groups, d.groups // 2
    sage = layer == "sage"
    func = ACT.Relu if sage else ACT.Gelu
    x_dram, out_dram = (dram["x1"], dram["x2"]) if sage else (dram["x3"], dram["out"])
    K = HEADS
    mem = ExitStack()

    def two(name, shape, dt):
        return [kn.buffer(mem, f"{name}{u}", shape, dt) for u in range(2)]

    h = two("b_h", [P, 4, D], F32)
    x = two("b_x", [P, S, D], F32)
    y = kn.buffer(mem, "b_y", [P, S, D], F32)
    o = two("b_o", [P, S, D], F32)
    if sage:
        z_hi = kn.buffer(mem, "b_z_hi", [P, 2, 4, D], F16)
        z_lo = kn.buffer(mem, "b_z_lo", [P, 2, 4, D], F16)
        wide = two("b_wide", [P, HC], F32)
        al = two("b_al", [P, S, 2 * K], F32)
    norm = Norm(kn, mem)
    tp = [kn.bank[n] for n in ((0, 1, 0, 1) if sage else (0, 1, 2, 3))]
    tq = [kn.bank[2], kn.bank[3]]
    mm = [kn.bank[4], kn.bank[5]]
    al_ps = kn.bank[7][:, 0:2 * K]

    h_in = pair("h_in", 16 * H)
    x_in = pair("x_in", 16 * H)
    f_done = pair("f_done", 4 * H)
    rows_turned = pair("rows_turned", S * H)
    y_done = pair("y_done_", S * H)
    rows_out = pair("rows_out", S * H)
    stored = pair("stored", 16 * H)
    turned = take("turned_", 4 * G if sage else 0)
    hi_done = take("hi_done", 4 * G if sage else 0)
    lo_done = take("lo_done", 4 * G if sage else 0)
    prod = take("prod", 2 * S * G if sage else 0)
    wide_done = take("wide_done", 2 * S * G if sage else 0)
    wide_stored = pair("wide_stored", 16 * 2 * G if sage else 0)
    al_prod = take("al_prod", S * G if sage else 0)
    al_done = take("al_done", S * G if sage else 0)
    al_stored = pair("al_stored", 16 * H if sage else 0)

    def sync(sp):
        def load(i, u):
            sp.wait_ge(rows_turned[u].sem, rows_turned[u].at(i * S))
            settle(sp, kn)
            sp.dma_start(h[u][:], dram["h"][:, :, ds(i * (2 * GROUP) + u * GROUP, GROUP)]
                         .rearrange("m p n -> p m n")).then_inc(h_in[u].sem, 16)
            sp.wait_ge(y_done[u].sem, y_done[u].at(i * S))
            sp.dma_start(x[u][:], node_rows(x_dram, i, u)).then_inc(x_in[u].sem, 16)

        def store(i, u):
            sp.wait_ge(rows_out[u].sem, rows_out[u].at(i * S + S))
            sp.dma_start(node_rows(out_dram, i, u), o[u][:]).then_inc(stored[u].sem, 16)

        def group(i, u, last):
            g = i * 2 + u
            if not last:
                load(*following(i, u))
            store(i, u)
            if sage:
                for s in range(S):
                    sp.wait_ge(wide_done.sem, wide_done.at(g * (2 * S) + 2 * s + 2))
                    sp.dma_start(dram["h1"][ds(i * (2 * GROUP) + u * GROUP + s * P, P), :], wide[s % 2][:])\
                        .then_inc(wide_stored[s % 2].sem, 16)
                sp.wait_ge(al_done.sem, al_done.at(g * S + S))
                sp.dma_start(node_rows(dram["al1"], i, u), al[u][:]).then_inc(al_stored[u].sem, 16)

        load(0, 0)
        in_pairs(sp, G, group)
        for u in range(2):
            sp.wait_ge(stored[u].sem, stored[u].at(16 * H))
            if sage:
                sp.wait_ge(wide_stored[u].sem, wide_stored[u].at(16 * 2 * G))
                sp.wait_ge(al_stored[u].sem, al_stored[u].at(16 * H))

    def gpsimd(pool):
        in_pairs(pool, G, lambda i, u, last: norm.pool(pool, i * 2 + u))

    def vector(dve):
        v = nc.vector

        def residual(i, u, subtiles):
            g = i * 2 + u
            dve.wait_ge(x_in[u].sem, x_in[u].at(i * 16 + 16))
            for s in subtiles:
                dve.wait_ge(rows_turned[u].sem, rows_turned[u].at(i * S + s + 1))
                v.scalar_tensor_tensor(out=y[:, s, :], in0=x[u][:, s, :], scalar=2.0, in1=tp[s][:],
                                       op0=ALU.mult, op1=ALU.add).then_inc(y_done[u].sem, 1)
                dve.wait_ge(y_done[u].sem, y_done[u].at(i * S + s + 1))
                norm.moments_of(dve, y[:, s, :], s, g)

        def finish(i, u):
            dve.wait_ge(stored[u].sem, stored[u].at(i * 16))
            norm.apply(dve, o[u], y, i * 2 + u, rows_out[u])

        def low_parts(i, u):
            g = i * 2 + u
            for k in range(4):
                dve.wait_ge(hi_done.sem, hi_done.at(g * 4 + k + 1))
                v.scalar_tensor_tensor(out=z_lo[:, u, k, :], in0=tq[k % 2][:], scalar=A_SCALE, in1=z_hi[:, u, k, :],
                                       op0=ALU.mult, op1=ALU.subtract).then_inc(lo_done.sem, 1)

        def logits(i, u, s):
            g = i * 2 + u
            dve.wait_ge(al_prod.sem, al_prod.at(g * S + s + 1))
            v.tensor_scalar(al[u][:, s, :], al_ps, UNSCALE, None, ALU.mult).then_inc(al_done.sem, 1)

        def group(i, u, last):
            dve.wait_ge(al_stored[u].sem, al_stored[u].at(i * 16))
            logits(i, u, 0)
            if not last:
                residual(*following(i, u), (0, 1))
            logits(i, u, 1)
            if not last:
                residual(*following(i, u), (2, 3))
                finish(*following(i, u))
            logits(i, u, 2)
            logits(i, u, 3)
            if not last:
                low_parts(*following(i, u))

        def group_alone(i, u, last):
            dve.wait_ge(rows_out[1 - u].sem, rows_out[1 - u].at((i + u) * S))
            residual(i, u, range(S))
            finish(i, u)

        if sage:
            residual(0, 0, range(S))
            finish(0, 0)
            low_parts(0, 0)
        in_pairs(dve, G, group if sage else group_alone)

    def scalar(act):
        def apply(i, u):
            act.wait_ge(h_in[u].sem, h_in[u].at(i * 16 + 16))
            for m in range(4):
                act.activation(h[u][:, m, :], h[u][:, m, :], func, scale=kn.bn_scale[:, m:m + 1],
                               bias=kn.bn_shift[:, m:m + 1]).then_inc(f_done[u].sem, 1)

        def high_parts(i, u):
            g = i * 2 + u
            for k in range(4):
                act.wait_ge(turned.sem, turned.at(g * 4 + k + 1))
                act.activation(z_hi[:, u, k, :], tq[k % 2][:], ACT.Copy, scale=A_SCALE).then_inc(hi_done.sem, 1)

        def group(i, u, last):
            g = i * 2 + u
            if not last:
                apply(*following(i, u))
            for s in range(S):
                w = wide_stored[s % 2]
                act.wait_ge(w.sem, w.at(g * 32 + (s // 2) * 16))
                for n in range(2):
                    act.wait_ge(prod.sem, prod.at(g * (2 * S) + 2 * s + n + 1))
                    act.activation(wide[s % 2][:, n * D:(n + 1) * D], mm[n][:], ACT.Copy, scale=UNSCALE)\
                       .then_inc(wide_done.sem, 1)
            if not last:
                high_parts(*following(i, u))

        if sage:
            apply(0, 0)
            high_parts(0, 0)
            in_pairs(act, G, group)
        else:
            in_pairs(act, G, lambda i, u, last: apply(i, u))

    def tensor(pe):
        def turn_rows(i, u, subtiles):
            pe.wait_ge(f_done[u].sem, f_done[u].at(i * 4 + 4))
            for s in subtiles:
                if sage and s >= 2:
                    pe.wait_ge(y_done[u].sem, y_done[u].at(i * S + s - 1))
                else:
                    pe.wait_ge(y_done[1 - u].sem, y_done[1 - u].at((i + u) * S))
                for m in range(4):
                    ins = pe.transpose(tp[s][:, m * P:(m + 1) * P], h[u][:, m, s * P:(s + 1) * P], kn.ident[:])
                ins.then_inc(rows_turned[u].sem, 1)

        def turn_back(i, u):
            g = i * 2 + u
            pe.wait_ge(rows_out[u].sem, rows_out[u].at(i * S + S))
            for k in range(4):
                pe.wait_ge(lo_done.sem, lo_done.at(g * 4 + (k - 1 if k >= 2 else 0)))
                for s in range(S):
                    ins = pe.transpose(tq[k % 2][:, s * P:(s + 1) * P], o[u][:, s, k * P:(k + 1) * P], kn.ident[:])
                ins.then_inc(turned.sem, 1)

        def products(i, u, s):
            g = i * 2 + u
            parts = lambda k: (z_hi[:, u, k, s * P:(s + 1) * P], z_lo[:, u, k, s * P:(s + 1) * P])
            for n in range(2):
                if s:
                    pe.wait_ge(wide_done.sem, wide_done.at(g * (2 * S) + 2 * s + n - 1))
                else:
                    pe.wait_ge(wide_done.sem, wide_done.at(g * (2 * S)))
                split_product(pe, mm[n][:], parts,
                              lambda k: (kn.weights(False, W_GAT1, k, n, HC), kn.weights(True, W_GAT1, k, n, HC)),
                              4).then_inc(prod.sem, 1)
            pe.wait_ge(al_done.sem, al_done.at(g * S + s))
            split_product(pe, al_ps, parts, lambda k: (kn.wa_hi[:, k, :], kn.wa_lo[:, k, :]), 4)\
                .then_inc(al_prod.sem, 1)

        def group(i, u, last):
            pe.wait_ge(lo_done.sem, lo_done.at((i * 2 + u) * 4 + 4))
            products(i, u, 0)
            if not last:
                turn_rows(*following(i, u), (0, 1))
            products(i, u, 1)
            if not last:
                turn_rows(*following(i, u), (2, 3))
            products(i, u, 2)
            products(i, u, 3)
            if not last:
                turn_back(*following(i, u))

        if sage:
            turn_rows(0, 0, range(S))
            turn_back(0, 0)
            in_pairs(pe, G, group)
        else:
            in_pairs(pe, G, lambda i, u, last: turn_rows(i, u, range(S)))

    mem.close()
    return {"sync": sync, "gpsimd": gpsimd, "vector": vector, "scalar": scalar, "tensor": tensor}


def gat_stage(kn, layer):
    nc, d, dram, take, pair = kn.nc, kn.d, kn.dram, kn.sig.take, kn.sig.pair
    G, H = d.groups, d.groups // 2
    first = layer == 1
    K = HEADS
    CH = HC // P
    bias = V_GAT1_B if first else V_GAT2_B
    h_dram = dram["h1"] if first else dram["h2"]
    products = 2 * S if first else S
    turns = CH // products
    mem = ExitStack()

    def two(name, shape, dt):
        return [kn.buffer(mem, f"{name}{u}", shape, dt) for u in range(2)]

    z = two("t_z", [P, S, HC + K], F32)
    hrow = two("t_h", [P, HC], F32)
    r_f = two("t_r", [P, D], F32)
    r_hi = kn.buffer(mem, "t_r_hi", [P, 2, CH, D], F16)
    r_lo = kn.buffer(mem, "t_r_lo", [P, 2, CH, D], F16)
    if first:
        wide = two("t_wide", [P, HC], F32)
        al = two("t_al", [P, S, 2 * K], F32)
    else:
        x = kn.buffer(mem, "t_x", [P, S, D], F32)
        norm = Norm(kn, mem)
    tp = [kn.bank[0], kn.bank[1]]
    mm = [kn.bank[2], kn.bank[3]] if first else [kn.bank[2 + s] for s in range(S)]
    al_ps = kn.bank[7][:, 0:2 * K]

    sum_in = pair("sum_in", 16 * H)
    h_in = pair("h_in", 16 * 2 * G)
    z_ready = pair("z_ready", S * H)
    turned = pair("turned", CH * H)
    r_done = take("r_done", CH * G)
    r_hi_done = take("r_hi_done", CH * G)
    r_lo_done = take("r_lo_done", CH * G)
    prod = take("prod", products * G)
    if first:
        wide_done = take("wide_done", 2 * S * G)
        wide_stored = pair("wide_stored", 16 * 2 * G)
        al_prod = take("al_prod", S * G)
        al_done = take("al_done", S * G)
        al_stored = pair("al_stored", 16 * H)
    else:
        x_in = take("x2_in", 16 * G)
        x_ready = take("x2_ready", G)
        y_done = take("y_done", S * G)
        rows_out = take("x3_out", S * G)
        stored = take("x3_stored", 16 * G)

    def ahead(i):
        return not (isinstance(i, int) and i == H - 1)

    def sync(sp):
        def load(i, u):
            sp.wait_ge(turned[u].sem, turned[u].at(i * CH))
            sp.dma_start(z[u][:], node_rows(dram["sum_gat"], i, u)).then_inc(sum_in[u].sem, 16)
            for s in range(S):
                if s >= 2:
                    sp.wait_ge(z_ready[u].sem, z_ready[u].at(i * S + s - 1))
                else:
                    sp.wait_ge(z_ready[1 - u].sem, z_ready[1 - u].at((i + u) * S))
                sp.dma_start(hrow[s % 2][:], h_dram[ds(i * (2 * GROUP) + u * GROUP + s * P, P), :])\
                    .then_inc(h_in[s % 2].sem, 16)

        def load_x(i, u):
            g = i * 2 + u
            sp.wait_ge(stored.sem, stored.at(g * 16))
            sp.dma_start(x[:], node_rows(dram["x2"], i, u)).then_inc(x_in.sem, 16)

        def group(i, u, last):
            g = i * 2 + u
            if not first:
                load_x(i, u)
            if ahead(i):
                load(i + 1, u)
            if first:
                for s in range(S):
                    sp.wait_ge(wide_done.sem, wide_done.at(g * (2 * S) + 2 * s + 2))
                    sp.dma_start(dram["h2"][ds(i * (2 * GROUP) + u * GROUP + s * P, P), :], wide[s % 2][:])\
                        .then_inc(wide_stored[s % 2].sem, 16)
                sp.wait_ge(al_done.sem, al_done.at(g * S + S))
                sp.dma_start(node_rows(dram["al2"], i, u), al[u][:]).then_inc(al_stored[u].sem, 16)
            else:
                sp.wait_ge(rows_out.sem, rows_out.at(g * S + S))
                sp.dma_start(node_rows(dram["x3"], i, u), x[:]).then_inc(stored.sem, 16)

        load(0, 0)
        load(0, 1)
        in_pairs(sp, G, group)
        if first:
            for u in range(2):
                sp.wait_ge(wide_stored[u].sem, wide_stored[u].at(16 * 2 * G))
                sp.wait_ge(al_stored[u].sem, al_stored[u].at(16 * H))
        else:
            sp.wait_ge(stored.sem, stored.at(16 * G))

    def gpsimd(pool):
        g_ = nc.gpsimd

        def low_parts(i, u, chunks):
            g = i * 2 + u
            for k in chunks:
                pool.wait_ge(r_hi_done.sem, r_hi_done.at(g * CH + k + 1))
                g_.tensor_tensor(r_lo[:, u, k, :], r_f[k % 2][:], r_hi[:, u, k, :], ALU.subtract)\
                  .then_inc(r_lo_done.sem, 1)

        def group(i, u, last):
            g = i * 2 + u
            if not first:
                pool.wait_ge(x_in.sem, x_in.at(g * 16 + 16))
                g_.tensor_tensor(x[:], x[:], kn.fc_b[:].unsqueeze(1).broadcast_to([P, S, D]), ALU.add)\
                  .then_inc(x_ready.sem, 1)
            if not last:
                low_parts(*following(i, u), range(CH))
            if not first:
                norm.pool(pool, g)

        low_parts(0, 0, range(CH))
        in_pairs(pool, G, group)

    def vector(dve):
        v = nc.vector

        def combine(i, u):
            dve.wait_ge(sum_in[u].sem, sum_in[u].at(i * 16 + 16))
            for s in range(S):
                w = h_in[s % 2]
                dve.wait_ge(w.sem, w.at(i * 64 + u * 32 + (s // 2) * 16 + 16))
                for h in range(K):
                    cols = slice(h * C, (h + 1) * C)
                    ins = v.scalar_tensor_tensor(out=z[u][:, s, cols], in0=hrow[s % 2][:, cols],
                                                 scalar=z[u][:, s, HC + h:HC + h + 1], in1=z[u][:, s, cols],
                                                 op0=ALU.mult, op1=ALU.add)
                ins.then_inc(z_ready[u].sem, 1)

        def group(i, u, last):
            g = i * 2 + u
            if ahead(i):
                combine(i + 1, u)
            if first:
                dve.wait_ge(al_stored[u].sem, al_stored[u].at(i * 16))
                for s in range(S):
                    dve.wait_ge(al_prod.sem, al_prod.at(g * S + s + 1))
                    v.tensor_scalar(al[u][:, s, :], al_ps, UNSCALE, None, ALU.mult).then_inc(al_done.sem, 1)
                return
            dve.wait_ge(x_ready.sem, x_ready.at(g + 1))
            for s in range(S):
                dve.wait_ge(prod.sem, prod.at(g * S + s + 1))
                v.scalar_tensor_tensor(out=x[:, s, :], in0=mm[s][:], scalar=UNSCALE, in1=x[:, s, :],
                                       op0=ALU.mult, op1=ALU.add).then_inc(y_done.sem, 1)
                dve.wait_ge(y_done.sem, y_done.at(g * S + s + 1))
                norm.moments_of(dve, x[:, s, :], s, g)
            norm.apply(dve, x, x, g, rows_out)

        combine(0, 0)
        combine(0, 1)
        in_pairs(dve, G, group)

    def scalar(act):
        def parts(i, u, chunks):
            g = i * 2 + u
            for k in chunks:
                act.wait_ge(turned[u].sem, turned[u].at(i * CH + k + 1))
                act.wait_ge(r_lo_done.sem, r_lo_done.at(g * CH + (k - 1 if k >= 2 else 0)))
                act.activation(r_f[k % 2][:], tp[k % 2][:], ACT.Relu, scale=A_SCALE,
                               bias=kn.vec_scaled[:, bias + k:bias + k + 1]).then_inc(r_done.sem, 1)
                act.wait_ge(r_done.sem, r_done.at(g * CH + k + 1))
                act.copy(r_hi[:, u, k, :], r_f[k % 2][:]).then_inc(r_hi_done.sem, 1)

        def group(i, u, last):
            g = i * 2 + u
            for n in range(products):
                if first:
                    s, half = divmod(n, 2)
                    w = wide_stored[s % 2]
                    act.wait_ge(w.sem, w.at(g * 32 + (s // 2) * 16))
                    act.wait_ge(prod.sem, prod.at(g * products + n + 1))
                    act.activation(wide[s % 2][:, half * D:(half + 1) * D], mm[half][:], ACT.Copy, scale=UNSCALE)\
                       .then_inc(wide_done.sem, 1)
                if not last:
                    parts(*following(i, u), range(n * turns, (n + 1) * turns))

        parts(0, 0, range(CH))
        in_pairs(act, G, group)

    def tensor(pe):
        def turn(i, u, chunks):
            g = i * 2 + u
            pe.wait_ge(z_ready[u].sem, z_ready[u].at(i * S + S))
            for k in chunks:
                pe.wait_ge(r_done.sem, r_done.at(g * CH + (k - 1 if k >= 2 else 0)))
                for s in range(S):
                    ins = pe.transpose(tp[k % 2][:, s * P:(s + 1) * P], z[u][:, s, k * P:(k + 1) * P], kn.ident[:])
                ins.then_inc(turned[u].sem, 1)

        def group(i, u, last):
            g = i * 2 + u
            pe.wait_ge(r_lo_done.sem, r_lo_done.at(g * CH + CH))
            for n in range(products):
                s, half = divmod(n, 2) if first else (n, 0)
                split = lambda k: (r_hi[:, u, k, s * P:(s + 1) * P], r_lo[:, u, k, s * P:(s + 1) * P])
                unit, width = (W_GAT2, HC) if first else (W_FC, D)
                if first:
                    pe.wait_ge(wide_done.sem, wide_done.at(g * (2 * S) + (n - 1 if s else 0)))
                else:
                    pe.wait_ge(y_done.sem, y_done.at(g * S))
                split_product(pe, mm[half if first else s][:], split,
                              lambda k: (kn.weights(False, unit, k, half, width),
                                         kn.weights(True, unit, k, half, width)), CH).then_inc(prod.sem, 1)
                if first and half:
                    pe.wait_ge(al_done.sem, al_done.at(g * S + s))
                    split_product(pe, al_ps, split,
                                  lambda k: (kn.wa_hi[:, 4 + k, :], kn.wa_lo[:, 4 + k, :]), CH)\
                        .then_inc(al_prod.sem, 1)
                if not last:
                    turn(*following(i, u), range(n * turns, (n + 1) * turns))

        turn(0, 0, range(CH))
        in_pairs(pe, G, group)

    mem.close()
    return {"sync": sync, "gpsimd": gpsimd, "vector": vector, "scalar": scalar, "tensor": tensor}


def graph_layers_kernel(nc, nodes, edges, io):
    d = Dims(nodes, edges)
    dram = dict(io)

    def scratch(name, shape, dt=F32):
        dram[name] = nc.dram_tensor(name, shape, dt, kind="Internal").ap()

    scratch("sorted", (d.edge_rows + 1, 2), I32)
    scratch("sum", (d.padded, D))
    scratch("sum_gat", (d.padded, HC + HEADS))
    scratch("dinv", (d.padded, 1))
    for name in ("x1", "x2", "x3"):
        scratch(name, (d.padded, D))
    for name in ("h1", "h2"):
        scratch(name, (d.padded, HC))
    for name in ("al1", "al2"):
        scratch(name, (d.padded, 2 * HEADS))
    scratch("h", (4, P, d.padded))

    with ExitStack() as ctx:
        kn = Kernel(nc, ctx, d, dram)
        ones = kn.ones
        kn.add(setup_stage(kn))
        kn.add(tiles_stage(kn))
        kn.add(edge_sum_stage(kn, dram["x"], ones, ones))
        kn.add(degree_stage(kn))
        kn.add(gin_stage(kn))
        kn.add(edge_sum_stage(kn, dram["x1"], ones, kn.mean_scale))
        kn.add(linear_stage(kn, "sage"))
        kn.add(norm_coefficients_stage(kn, V_SAGE_G, V_SAGE_BETA))
        kn.add(batch_norm_stage(kn, "sage"))
        kn.add(edge_attention_stage(kn, dram["h1"], dram["al1"]))
        kn.add(gat_stage(kn, 1))
        kn.add(edge_attention_stage(kn, dram["h2"], dram["al2"]))
        kn.add(gat_stage(kn, 2))
        kn.add(edge_sum_stage(kn, dram["x3"], kn.src_dinv, ones))
        kn.add(linear_stage(kn, "gcn"))
        kn.add(norm_coefficients_stage(kn, V_GCN_G, V_GCN_BETA))
        kn.add(batch_norm_stage(kn, "gcn"))
        kn.run()


def lay_out(inputs, d):
    import numpy as np

    x = np.asarray(inputs["x"])
    pad = np.zeros((d.padded - d.nodes, D), x.dtype)
    src, dst = np.asarray(inputs["src"]), np.asarray(inputs["dst"])
    more = d.edge_rows - d.edges
    src = np.concatenate([src, np.zeros(more, src.dtype)])
    dst = np.concatenate([dst, np.full(more, d.sent, dst.dtype)])

    def unit(w):
        k, n = w.shape
        per = 4 * D // n
        return w.reshape(k // P // per, per, P, n).transpose(0, 2, 1, 3).reshape(-1, P, 4 * D)

    weights = [np.asarray(inputs["L0_gnn_W1"]), np.asarray(inputs["L0_gnn_W2"]),
               np.asarray(inputs["L1_gnn_W_l"]).T, np.asarray(inputs["L1_gnn_W_r"]).T,
               np.asarray(inputs["L2_gnn_W1"]), np.asarray(inputs["L2_gnn_W2"]), np.asarray(inputs["L2_gnn_Wfc"]),
               np.asarray(inputs["L3_gnn_W"]).T]
    vectors = [np.asarray(inputs[n]).reshape(-1, P).T for n in (
        "L0_gnn_b1", "L1_gnn_b_l", "L1_gnn_gamma", "L1_gnn_beta", "L2_gnn_b1", "L2_gnn_b2",
        "L3_gnn_b", "L3_gnn_gamma", "L3_gnn_beta")]
    attention = np.stack([np.stack([np.asarray(inputs[f"L2_gnn_a_src{n}"]).reshape(-1),
                                    np.asarray(inputs[f"L2_gnn_a_dst{n}"]).reshape(-1)]) for n in (1, 2)])
    return {
        "x": np.concatenate([x, pad]),
        "dst": dst,
        "edges": np.stack([src, dst], axis=-1).reshape(d.edge_cols, P, 2).transpose(1, 0, 2),
        "weights": np.concatenate([unit(w) for w in weights]),
        "vectors": np.ascontiguousarray(np.concatenate(vectors, axis=1)),
        "attention": attention,
        "gin_b2": np.asarray(inputs["L0_gnn_b2"]),
        "fc_b": np.asarray(inputs["L2_gnn_bfc"]),
    }


def program(nc, inputs):
    import numpy as np

    nodes, edges = inputs["x"].shape[0], inputs["src"].shape[0]
    d = Dims(nodes, edges)
    arrays = {f"in_{n}": np.ascontiguousarray(a) for n, a in lay_out(inputs, d).items()}
    io = {n[3:]: nc.dram_tensor(n, a.shape, mybir.dt.from_np(a.dtype), kind="ExternalInput").ap()
          for n, a in arrays.items()}
    io["out"] = nc.dram_tensor("out", (d.padded, D), F32, kind="ExternalOutput").ap()
    graph_layers_kernel(nc, nodes, edges, io)
    return arrays


def kernel(**inputs):
    import concourse.bacc as bacc
    from concourse.bass_utils import run_bass_kernel_spmd

    nc = bacc.Bacc("TRN2", target_bir_lowering=False, num_devices=1)
    arrays = program(nc, inputs)
    return run_bass_kernel_spmd(nc, [arrays], core_ids=[0]).results[0]["out"][:inputs["x"].shape[0]]
```

```python
from contextlib import ExitStack

import concourse.bass as bass
from concourse import mybir

F32 = mybir.dt.float32
F16 = mybir.dt.float16
I32 = mybir.dt.int32
ALU = mybir.AluOpType
ACT = mybir.ActivationFunctionType
AX = mybir.AxisListType
ds = bass.ds

P = 128
D = 512
HC = 1024
HEADS = 4
C = HC // HEADS
S = 4
GROUP = S * P
EDGES = P - 1
EPS = 1e-5
SLOPE = 0.2
A_SCALE = 16.0
GIN_SCALE = 2.0
W_SCALE = 256.0
UNSCALE = 1.0 / (A_SCALE * W_SCALE)
GIN_UNSCALE = 1.0 / (GIN_SCALE * W_SCALE)
FAR = 20000
BIG = 1e30
START = 8
CARRY_IN = (0, 96)
CARRY_OUT = (96, 0)

W_GIN1, W_GIN2, W_SAGE_L, W_SAGE_R, W_GAT1, W_GAT2, W_FC, W_GCN = 0, 1, 2, 3, 4, 6, 10, 12
UNITS = 13
V_GIN_B1, V_SAGE_B, V_SAGE_G, V_SAGE_BETA, V_GAT1_B, V_GAT2_B, V_GCN_B, V_GCN_G, V_GCN_BETA = (
    0, 4, 8, 12, 16, 24, 32, 36, 40)
VECTORS = 44


ENGINES = ("sync", "gpsimd", "scalar", "vector", "tensor")


class Dims:
    def __init__(self, nodes, edges):
        self.nodes = nodes
        self.edges = edges
        self.groups = -(-nodes // (2 * GROUP)) * 2
        self.padded = self.groups * GROUP
        self.sent = self.padded - 1
        self.edge_cols = -(-(edges + 1) // P)
        self.edge_rows = self.edge_cols * P
        self.tiles = -(-edges // (4 * EDGES)) * 4
        self.last_real = nodes - (self.groups - 1) * GROUP
        assert self.sent >= nodes and 0 < self.last_real <= GROUP
        assert self.tiles * EDGES + 2 <= self.edge_rows + 1
        assert self.padded * self.edge_cols < 1 << 24


class Signal:

    def __init__(self, sem, base):
        self.sem, self.base = sem, base

    def at(self, n):
        return self.base + n


class Signals:

    def __init__(self, nc, ctx):
        self.nc, self.ctx, self.sems, self.total, self.raised = nc, ctx, {}, {}, []

    def take(self, name, total, software=False):
        if name not in self.sems:
            self.sems[name] = self.ctx.enter_context(self.nc.semaphore(name))
            self.total[name] = 0 if software else START
            if not software:
                self.raised.append(self.sems[name])
        s = Signal(self.sems[name], self.total[name])
        self.total[name] += total
        return s

    def raise_all(self, eng, which):
        for sem in self.raised[which::5]:
            eng.sem_inc(sem, START)

    def pair(self, name, total, software=False):
        return [self.take(f"{name}{u}", total, software) for u in range(2)]

    def four(self, name, total, software=False):
        return [self.take(f"{name}{v}", total, software) for v in range(4)]


class Steps:

    def __init__(self, sig):
        self.sig, self.first, self.n = sig, 0, 0

    def begin(self, first):
        self.first, self.n = first, 0

    def mark(self, ins):
        ins.then_inc(self.sig.sem, 1)
        self.n += 1
        return self.sig.at(self.first + self.n)


def settle(eng, kn):
    eng.sem_inc(kn.passed, 1)


def in_pairs(eng, n, body):
    if n > 2:
        with eng.Fori(0, n // 2 - 1) as i:
            for u in range(2):
                body(i, u, False)
    body(n // 2 - 1, 0, False)
    body(n // 2 - 1, 1, True)


def ahead(i, n):
    return not (isinstance(i, int) and i == n // 2 - 1)


def following(i, u):
    return i + u, 1 - u


def in_quads(eng, n, body):
    if n > 4:
        with eng.Fori(0, n // 4 - 1) as i:
            for v in range(4):
                body(i, v, 4)
    for v in range(4):
        body(n // 4 - 1, v, 3 - v)


def after(i, v, by):
    return i + (v + by) // 4, (v + by) % 4


def in_two(i, v):
    return i * 2 + v // 2, v % 2


class Kernel:
    def __init__(self, nc, ctx, dims, dram):
        self.nc, self.ctx, self.d, self.dram = nc, ctx, dims, dram
        self.sig = Signals(nc, ctx)
        self.stages = []
        self.meet = ctx.enter_context(nc.semaphore("meet"))
        self.passed = ctx.enter_context(nc.semaphore("passed"))
        self.buffers = 0
        d = dims

        def sb(name, shape, dt):
            return ctx.enter_context(nc.sbuf_tensor(name, shape, dt))

        self.ident = sb("ident", [P, P], F32)
        self.ones = sb("ones", [P, P], F32)
        self.w_hi = sb("w_hi", [P, UNITS, 4 * D], F16)
        self.w_lo = sb("w_lo", [P, UNITS, 4 * D], F16)
        self.wa_hi = sb("wa_hi", [P, 12, 2 * HEADS], F16)
        self.wa_lo = sb("wa_lo", [P, 12, 2 * HEADS], F16)
        self.vec = sb("vec", [P, VECTORS], F32)
        self.vec_scaled = sb("vec_scaled", [P, VECTORS], F32)
        self.gin_b2 = sb("gin_b2", [P, D], F32)
        self.fc_b = sb("fc_b", [P, D], F32)
        self.same = sb("same", [P, d.tiles * P], F16)
        self.dst_f = sb("dst_f", [P, d.tiles], F32)
        self.src_i = sb("src_i", [P, d.tiles], I32)
        self.dst_i = sb("dst_i", [P, d.tiles], I32)
        self.final_i = sb("final_i", [P, d.tiles], I32)
        self.count = sb("count", [P, d.tiles], F32)
        self.mean_scale = sb("mean_scale", [P, d.tiles], F32)
        self.degree = sb("degree", [P, d.tiles], F32)
        self.dinv = sb("dinv_sb", [P, d.tiles], F32)
        self.src_dinv = sb("src_dinv", [P, d.tiles], F32)
        self.bn_scale = sb("bn_scale", [P, 4], F32)
        self.bn_shift = sb("bn_shift", [P, 4], F32)
        self.bn_stats = sb("bn_stats", [P, 4, 2 * 6 * (d.groups // 2)], F32)
        self.minus_half = sb("minus_half", [P, d.tiles], F32)
        self.eps = sb("eps", [P, S], F32)
        self.bank = [ctx.enter_context(nc.psum_tensor(f"bank{n}", [P, D], F32)) for n in range(8)]

    def weights(self, lo, unit, k, n, width):
        w = self.w_lo if lo else self.w_hi
        per = 4 * D // width
        at = (k % per) * width + n * D
        return w[:, unit + k // per, at:at + D]

    def buffer(self, mem, name, shape, dt):
        self.buffers += 1
        return mem.enter_context(self.nc.sbuf_tensor(f"{name}_{self.buffers}", shape, dt))

    def add(self, stage):
        self.stages.append(stage)

    def run(self):
        nc = self.nc
        meet = self.meet
        block = self.ctx.enter_context(nc.Block())
        stages = self.stages

        def program(eng, which):
            self.sig.raise_all(eng, ENGINES.index(which))
            eng.drain().then_inc(meet, 1)
            eng.wait_ge(meet, 5)
            for n, stage in enumerate(stages):
                if which in stage:
                    stage[which](eng)
                eng.drain().then_inc(meet, 1)
                eng.wait_ge(meet, 5 * (n + 2))

        @block.sync
        def _(sp):
            program(sp, "sync")

        @block.gpsimd
        def _(pool):
            program(pool, "gpsimd")

        @block.scalar
        def _(act):
            program(act, "scalar")

        @block.vector
        def _(dve):
            program(dve, "vector")

        @block.tensor
        def _(pe):
            program(pe, "tensor")


def split_product(pe, out, stationary, moving, chunks, before=None):
    for k in range(chunks):
        if before:
            before(k)
        s_hi, s_lo = stationary(k)
        m_hi, m_lo = moving(k)
        last = k == chunks - 1
        pe.matmul(out, s_lo, m_hi, start=(k == 0), stop=False)
        pe.matmul(out, s_hi, m_lo, start=False, stop=False)
        mm = pe.matmul(out, s_hi, m_hi, start=False, stop=last)
    return mm


def together(*stages):
    def programs(which):
        def run(eng):
            for stage in stages:
                if which in stage:
                    stage[which](eng)
        return run

    return {which: programs(which) for which in ENGINES}


def setup_stage(kn):
    nc, d, dram, take = kn.nc, kn.d, kn.dram, kn.sig.take
    J = d.edge_cols
    JV = -(-J * 3 // 7)
    mem = ExitStack()

    def sb(name, shape, dt):
        return kn.buffer(mem, name, shape, dt)

    blank = sb("blank", [P, HC + HEADS], F32)
    dst_row = sb("dst_row", [P, J * P], I32)
    key_row = sb("key_row", [P, J * P], F32)
    junk = [dst_row[:, u * (J * P // 2):(u + 1) * (J * P // 2)].bitcast(F16) for u in range(2)]
    pairs = sb("pairs", [P, J, 2], I32)
    key_col = sb("key_col", [P, J], F32)
    key_half = sb("key_half", [P, J], F32)
    j_col = sb("j_col", [P, J], F32)
    before = sb("before", [P, P], F32)
    junk2 = sb("junk2", [P, P], F16)
    less = sb("less", [P, J], F32)
    tied = sb("tied", [P, J], F32)
    signs = sb("signs", [P, J], F32)
    place = sb("place", [P, J], I32)
    sentinel = sb("sentinel", [1, 2], I32)

    small_in = take("small_in", 16 * 3)
    dst_in = take("dst_in", 16)
    pairs_in = take("pairs_in", 16)
    blank_ready = take("blank_ready", 1)
    zeroed = take("zeroed", 16 * (d.groups + 1))
    kn.wide_zeroed = take("wide_zeroed", 16 * d.groups)
    pool_steps = Steps(take("pool_steps", 10))
    order = take("order", JV + J + 7)
    sign_steps = take("sign_steps", J - JV)
    vec_done = take("vec_done", 2)
    sorted_out = take("sorted_out", 16 * (J - 1), software=True)
    sorted_first = kn.sig.pair("scattered", 16, software=True)

    def sync(sp):
        sp.dma_start(dst_row[:], dram["dst"].partition_broadcast(P)).then_inc(dst_in.sem, 16)
        sp.dma_start(pairs[:], dram["edges"]).then_inc(pairs_in.sem, 16)
        sp.dma_start(kn.vec[:], dram["vectors"]).then_inc(small_in.sem, 16)
        sp.dma_start(kn.gin_b2[:], dram["gin_b2"].partition_broadcast(P)).then_inc(small_in.sem, 16)
        sp.dma_start(kn.fc_b[:], dram["fc_b"].partition_broadcast(P)).then_inc(small_in.sem, 16)
        sp.wait_ge(blank_ready.sem, blank_ready.at(1))
        rows = d.padded // P
        per = rows // d.groups
        wide = dram["sum_gat"].rearrange("(p r) c -> p r c", r=rows)
        thin = dram["sum"].rearrange("(p r) c -> p r c", r=rows)
        for g in range(d.groups):
            sp.dma_start(thin[:, g * per:(g + 1) * per, :],
                         blank[:, 0:D].unsqueeze(1).broadcast_to([P, per, D])).then_inc(zeroed.sem, 16)
        sp.dma_start(dram["dinv"].rearrange("(p r) c -> p (r c)", p=P), kn.ones[:, 0:rows]).then_inc(zeroed.sem, 16)
        for g in range(d.groups):
            sp.dma_start(wide[:, g * per:(g + 1) * per, :],
                         blank[:].unsqueeze(1).broadcast_to([P, per, HC + HEADS])).then_inc(kn.wide_zeroed.sem, 16)
        sp.wait_ge(zeroed.sem, zeroed.at(16 * (d.groups + 1)))
        sp.wait_ge(kn.wide_zeroed.sem, kn.wide_zeroed.at(16 * d.groups))

    def gpsimd(pool):
        st = pool_steps
        st.begin(0)
        g = nc.gpsimd
        g.memset(blank[:, 0:HC], 0.0)
        a = st.mark(g.memset(kn.ones[:], 1.0))
        st.mark(g.memset(kn.ident[:], 0.0))
        g.memset(kn.eps[:], EPS)
        b = st.mark(g.memset(kn.minus_half[:], -0.5))
        pool.wait_ge(st.sig.sem, a)
        g.memset(blank[:, HC:], 1.0).then_inc(blank_ready.sem, 1)
        st.mark(g.iota(key_row[:].rearrange("p (j q) -> p j q", q=P), [[1, J], [0, P]], base=0,
                       channel_multiplier=0, allow_small_or_imprecise_dtypes=True))
        st.mark(g.iota(j_col[:], [[1, J]], base=0, channel_multiplier=0,
                       allow_small_or_imprecise_dtypes=True))
        st.mark(g.affine_select(out=before[:], in_=kn.ones[:], compare_op=ALU.is_gt, fill=0.0,
                                base=0, pattern=[[-1, P]], channel_multiplier=1))
        pool.wait_ge(st.sig.sem, b)
        st.mark(g.affine_select(out=kn.ident[:], in_=kn.ident[:], compare_op=ALU.not_equal, fill=1.0,
                                base=0, pattern=[[-1, P]], channel_multiplier=1))
        st.mark(g.memset(sentinel[:, 0:1], 0))
        st.mark(g.memset(sentinel[:, 1:2], d.sent))
        n = st.mark(g.memset(kn.src_dinv[:], 1.0))
        pool.wait_ge(st.sig.sem, n)
        pool.dma_start(dram["sorted"][0:1, :], sentinel[:]).then_inc(sorted_out.sem, 16)
        pool.wait_ge(order.sem, order.at(JV + J + 7))
        pool.wait_ge(small_in.sem, small_in.at(48))
        pool.wait_ge(pairs_in.sem, pairs_in.at(16))
        for j in range(J):
            pool.indirect_dma_start(dram["sorted"], bass.IndirectOffsetOnAxis(ap=place[:, j:j + 1], axis=0),
                                    pairs[:, j, :], None)\
                .then_inc((sorted_first[j] if j < 2 else sorted_out).sem, 16)
        pool.wait_ge(sorted_out.sem, sorted_out.at(16 * (J - 1)))
        for first in sorted_first:
            pool.wait_ge(first.sem, first.at(16))

    def scalar(act):
        act.wait_ge(order.sem, order.at(3))
        with act.Fori(0, J - JV) as j:
            act.wait_ge(sign_steps.sem, sign_steps.at(j))
            settle(act, kn)
            act.activation(junk[1], key_row[:], ACT.Sign, scale=-1.0, bias=key_half[:, ds(j + JV, 1)],
                           accum_out=signs[:, ds(j + JV, 1)]).then_inc(sign_steps.sem, 1)
        act.wait_ge(small_in.sem, small_in.at(48))
        act.mul(kn.vec_scaled[:, 0:V_GIN_B1 + 4], kn.vec[:, 0:V_GIN_B1 + 4], GIN_SCALE).then_inc(vec_done.sem, 1)
        act.mul(kn.vec_scaled[:, V_GIN_B1 + 4:], kn.vec[:, V_GIN_B1 + 4:], A_SCALE).then_inc(vec_done.sem, 1)

    def vector(dve):
        v = nc.vector
        dve.wait_ge(pool_steps.sig.sem, pool_steps.sig.at(6))
        dve.wait_ge(dst_in.sem, dst_in.at(16))
        dve.wait_ge(pairs_in.sem, pairs_in.at(16))
        v.scalar_tensor_tensor(out=key_row[:], in0=dst_row[:], scalar=float(J), in1=key_row[:],
                               op0=ALU.mult, op1=ALU.add).then_inc(order.sem, 1)
        v.scalar_tensor_tensor(out=key_col[:], in0=pairs[:, :, 1], scalar=float(J), in1=j_col[:],
                               op0=ALU.mult, op1=ALU.add).then_inc(order.sem, 1)
        dve.wait_ge(order.sem, order.at(2))
        v.tensor_scalar(key_half[:], key_col[:], -0.5, None, ALU.add).then_inc(order.sem, 1)

        def ties(j):
            v.scalar_tensor_tensor(out=junk2[:], in0=key_row[:, ds(j * P, P)], scalar=key_col[:, ds(j, 1)],
                                   in1=before[:], op0=ALU.is_equal, op1=ALU.mult,
                                   accum_out=tied[:, ds(j, 1)]).then_inc(order.sem, 1)

        with dve.Fori(0, JV) as j:
            dve.wait_ge(order.sem, order.at(j * 2 + 3))
            v.tensor_scalar(junk[0], key_row[:], key_col[:, ds(j, 1)], None, ALU.is_lt, ALU.add,
                            accum_out=less[:, ds(j, 1)]).then_inc(order.sem, 1)
            ties(j)
        with dve.Fori(0, J - JV) as j:
            dve.wait_ge(order.sem, order.at(j + 2 * JV + 3))
            ties(j + JV)
        dve.wait_ge(sign_steps.sem, sign_steps.at(J - JV))
        dve.wait_ge(order.sem, order.at(JV + J + 3))
        v.tensor_scalar(less[:, JV:], signs[:, JV:], float(J * P), 0.5, ALU.add, ALU.mult).then_inc(order.sem, 1)
        dve.wait_ge(order.sem, order.at(JV + J + 4))
        v.tensor_tensor(less[:], less[:], tied[:], ALU.add).then_inc(order.sem, 1)
        dve.wait_ge(order.sem, order.at(JV + J + 5))
        v.tensor_scalar(place[:], less[:], 1.0, None, ALU.add).then_inc(order.sem, 2)
        v.memset(kn.bn_stats[:], 0.0)

    mem.close()
    return {"sync": sync, "gpsimd": gpsimd, "scalar": scalar, "vector": vector}


def plain_weights(kn, mem):
    nc, dram, take = kn.nc, kn.dram, kn.sig.take
    units = [n for n in range(UNITS) if not W_GAT1 <= n < W_FC]
    stage_w = [kn.buffer(mem, f"p_stage{u}", [P, 4 * D], F32) for u in range(2)]
    w_in = [take("w_in0", 16 * 4), take("w_in1", 16 * 3)]
    scaled = take("w_scaled", len(units))
    hi_done = take("w_hi_done", len(units))
    lo_done = take("w_lo_done", len(units))

    def sync(sp):
        for n, unit in enumerate(units):
            if n >= 2:
                sp.wait_ge(lo_done.sem, lo_done.at(n - 1))
            sp.dma_start(stage_w[n % 2][:], dram["weights"][unit]).then_inc(w_in[n % 2].sem, 16)

    def scalar(act):
        for n, unit in enumerate(units):
            w = stage_w[n % 2]
            act.wait_ge(w_in[n % 2].sem, w_in[n % 2].at(16 * (n // 2 + 1)))
            act.mul(w[:], w[:], W_SCALE).then_inc(scaled.sem, 1)
            act.wait_ge(scaled.sem, scaled.at(n + 1))
            act.copy(kn.w_hi[:, unit, :], w[:]).then_inc(hi_done.sem, 1)

    def gpsimd(pool):
        for n, unit in enumerate(units):
            pool.wait_ge(hi_done.sem, hi_done.at(n + 1))
            nc.gpsimd.tensor_tensor(kn.w_lo[:, unit, :], stage_w[n % 2][:], kn.w_hi[:, unit, :], ALU.subtract)\
                .then_inc(lo_done.sem, 1)

    return {"sync": sync, "scalar": scalar, "gpsimd": gpsimd}


def attention_weights(kn, mem):
    nc, dram, take = kn.nc, kn.dram, kn.sig.take
    units = list(range(W_GAT1, W_FC))
    stage_w = [kn.buffer(mem, f"f_stage{u}", [P, 4 * D], F32) for u in range(2)]
    a_rows = kn.buffer(mem, "a_rows", [P, 2, HC], F32)
    prod = kn.buffer(mem, "f_prod", [P, HC], F32)
    wa = kn.buffer(mem, "f_wa", [P, 12, 2 * HEADS], F32)
    a_in = [take(f"a_in{n}", 16) for n in range(2)]
    w_in = [take(f"w_in{n}", 16 * 3) for n in range(2)]
    w_hi_done = take("w_hi_done", len(units))
    w_done = take("w_lo_done", len(units))
    wa_read = take("wa_read", 4 * len(units))
    wa_done = take("wa_done", 4 * len(units) + 2)

    def sync(sp):
        sp.dma_start(a_rows[:], dram["attention"][0].partition_broadcast(P)).then_inc(a_in[0].sem, 16)
        for n, unit in enumerate(units):
            if n >= 2:
                sp.wait_ge(w_done.sem, w_done.at(n - 1))
                sp.wait_ge(wa_read.sem, wa_read.at(4 * (n - 1)))
            if unit == W_GAT2:
                sp.wait_ge(wa_read.sem, wa_read.at(4 * n))
                sp.dma_start(a_rows[:], dram["attention"][1].partition_broadcast(P)).then_inc(a_in[1].sem, 16)
            sp.dma_start(stage_w[n % 2][:], dram["weights"][unit]).then_inc(w_in[n % 2].sem, 16)

    def vector(dve):
        v = nc.vector
        done = 0
        for n, unit in enumerate(units):
            layer = 0 if unit < W_GAT2 else 1
            dve.wait_ge(w_in[n % 2].sem, w_in[n % 2].at(16 * (n // 2 + 1)))
            v.tensor_scalar(kn.w_hi[:, unit, :], stage_w[n % 2][:], W_SCALE, None, ALU.mult)\
                .then_inc(w_hi_done.sem, 1)
            dve.wait_ge(w_hi_done.sem, w_hi_done.at(n + 1))
            v.scalar_tensor_tensor(out=kn.w_lo[:, unit, :], in0=stage_w[n % 2][:], scalar=W_SCALE,
                                   in1=kn.w_hi[:, unit, :], op0=ALU.mult, op1=ALU.subtract)\
                .then_inc(w_done.sem, 1)
            dve.wait_ge(a_in[layer].sem, a_in[layer].at(16))
            for half in range(2):
                w = stage_w[n % 2][:, half * HC:(half + 1) * HC]
                for side in range(2):
                    dve.wait_ge(wa_done.sem, wa_done.at(done))
                    v.tensor_tensor(prod[:], w, a_rows[:, side, :], ALU.mult).then_inc(wa_read.sem, 1)
                    done += 1
                    dve.wait_ge(wa_read.sem, wa_read.at(done))
                    v.tensor_reduce(wa[:, 2 * n + half, side * HEADS:(side + 1) * HEADS],
                                    prod[:].rearrange("p (h c) -> p h c", h=HEADS), AX.X, ALU.add)\
                        .then_inc(wa_done.sem, 1)
        dve.wait_ge(wa_done.sem, wa_done.at(done))
        v.tensor_scalar(kn.wa_hi[:], wa[:], W_SCALE, None, ALU.mult).then_inc(wa_done.sem, 1)
        dve.wait_ge(wa_done.sem, wa_done.at(done + 1))
        v.scalar_tensor_tensor(out=kn.wa_lo[:], in0=wa[:], scalar=W_SCALE, in1=kn.wa_hi[:],
                               op0=ALU.mult, op1=ALU.subtract).then_inc(wa_done.sem, 1)

    return {"sync": sync, "vector": vector}


def tiles_stage(kn):
    nc, d, dram, take = kn.nc, kn.d, kn.dram, kn.sig.take
    T = d.tiles
    mem = ExitStack()

    def sb(name, shape, dt):
        return kn.buffer(mem, name, shape, dt)

    rec = sb("rec", [P, T, 4], I32)
    equal_next = sb("equal_next", [P, T], F32)
    next_f = sb("next_f", [P, T], F32)
    spread = [sb(f"spread{u}", [P, P], F32) for u in range(2)]
    same_f = [sb(f"same_f{u}", [P, P], F32) for u in range(2)]
    one = [sb(f"one{u}", [P, 1], F32) for u in range(2)]
    tmp = sb("tmp", [P, T], F32)
    row_ps = [kn.bank[u][:, 0:P] for u in range(2)]
    count_ps = [kn.bank[2 + u][:, 0:1] for u in range(2)]

    rec_in = take("rec_in", 16 * 6)
    cols = take("cols", 9)
    spread_done = kn.sig.pair("spread_done", T // 2)
    row_done = kn.sig.pair("row_done", T // 2)
    same_done = kn.sig.pair("same_done", T // 2)
    same_f_done = kn.sig.pair("same_f_done", T // 2)
    count_done = kn.sig.pair("count_done", T // 2)
    carried = kn.sig.pair("carried", T // 2)
    counts = take("counts", T)
    ends = take("ends", 3)

    def rows(first, partitions, step, n):
        base = dram["sorted"]
        return bass.AP(base.tensor, base.offset + 2 * first, [[2, partitions], [2 * step, n], [1, 4]])

    def sync(sp):
        sp.dma_start(rec[1:96], rows(1, 95, EDGES, T)).then_inc(rec_in.sem, 16)
        sp.dma_start(rec[97:128], rows(96, 31, EDGES, T)).then_inc(rec_in.sem, 16)
        for u in range(2):
            for p, first in ((CARRY_IN[u], u * EDGES), (CARRY_OUT[u], (u + 1) * EDGES)):
                sp.dma_start(rec[p:p + 1, u:T:2, :], rows(first, 1, 2 * EDGES, T // 2)).then_inc(rec_in.sem, 16)

    def vector(dve):
        v = nc.vector
        dve.wait_ge(rec_in.sem, rec_in.at(16 * 6))
        v.tensor_copy(kn.dst_f[:], rec[:, :, 1]).then_inc(cols.sem, 1)
        v.tensor_copy(next_f[:], rec[:, :, 3]).then_inc(cols.sem, 1)
        v.tensor_copy(kn.src_i[:], rec[:, :, 0]).then_inc(cols.sem, 1)
        v.tensor_copy(kn.dst_i[:], rec[:, :, 1]).then_inc(cols.sem, 1)
        dve.wait_ge(cols.sem, cols.at(2))
        v.tensor_tensor(equal_next[:], kn.dst_f[:], next_f[:], ALU.is_equal).then_inc(cols.sem, 1)
        dve.wait_ge(cols.sem, cols.at(5))
        v.scalar_tensor_tensor(out=kn.final_i[:], in0=equal_next[:], scalar=float(FAR), in1=kn.dst_f[:],
                               op0=ALU.mult, op1=ALU.add).then_inc(cols.sem, 1)
        dve.wait_ge(cols.sem, cols.at(6))
        for u in range(2):
            v.memset(kn.final_i[CARRY_IN[u]:CARRY_IN[u] + 1, u:T:2], FAR).then_inc(cols.sem, 1)
        for u in range(2):
            ins = v.memset(one[u][:], 1.0)
        ins.then_inc(cols.sem, 1)
        dve.wait_ge(cols.sem, cols.at(9))

        def spread_out(i, u):
            v.tensor_scalar(spread[u][:], kn.ones[:], kn.dst_f[:, ds(i * 2 + u, 1)], None, ALU.mult)\
                .then_inc(spread_done[u].sem, 1)

        def compare(i, u):
            t = i * 2 + u
            dve.wait_ge(row_done[u].sem, row_done[u].at(i + 1))
            v.tensor_scalar(same_f[u][:], row_ps[u], kn.dst_f[:, ds(t, 1)], None, ALU.is_equal)\
                .then_inc(same_f_done[u].sem, 1)
            v.tensor_scalar(kn.same[:, ds(t * P, P)], row_ps[u], kn.dst_f[:, ds(t, 1)], None, ALU.is_equal)\
                .then_inc(same_done[u].sem, 1)

        def tile(i, u, last):
            c = CARRY_OUT[u]
            if not last:
                compare(*following(i, u))
            if ahead(i, T):
                spread_out(i + 1, u)
            dve.wait_ge(count_done[u].sem, count_done[u].at(i + 1))
            v.tensor_copy(one[1 - u][c:c + 1, :], count_ps[u][c:c + 1, :]).then_inc(carried[u].sem, 1)
            v.tensor_copy(kn.count[:, ds(i * 2 + u, 1)], count_ps[u]).then_inc(counts.sem, 1)

        spread_out(0, 0)
        spread_out(0, 1)
        compare(0, 0)
        in_pairs(dve, T, tile)
        dve.wait_ge(counts.sem, counts.at(T))
        v.tensor_scalar(tmp[:], kn.count[:], 1.0, None, ALU.max).then_inc(ends.sem, 1)
        v.tensor_scalar(kn.degree[:], kn.count[:], 1.0, None, ALU.add).then_inc(ends.sem, 1)
        dve.wait_ge(ends.sem, ends.at(1))
        v.reciprocal(kn.mean_scale[:], tmp[:]).then_inc(ends.sem, 1)

    def tensor(pe):
        def row(i, u):
            pe.wait_ge(spread_done[u].sem, spread_done[u].at(i + 1))
            pe.wait_ge(same_done[u].sem, same_done[u].at(i))
            pe.matmul(row_ps[u], spread[u][:], kn.ident[:], start=True, stop=True).then_inc(row_done[u].sem, 1)

        def tile(i, u, last):
            pe.wait_ge(same_f_done[u].sem, same_f_done[u].at(i + 1))
            pe.wait_ge(carried[1 - u].sem, carried[1 - u].at(i + u))
            pe.wait_ge(counts.sem, counts.at(i * 2))
            pe.matmul(count_ps[u], same_f[u][:], one[u][:], start=True, stop=True).then_inc(count_done[u].sem, 1)
            if ahead(i, T):
                row(i + 1, u)

        row(0, 0)
        row(0, 1)
        in_pairs(pe, T, tile)

    mem.close()
    return {"sync": sync, "vector": vector, "tensor": tensor}


def edge_sum_stage(kn, rows_dram, in_scale, out_scale):
    nc, d, dram, take, pair, four = kn.nc, kn.d, kn.dram, kn.sig.take, kn.sig.pair, kn.sig.four
    T, H, Q = d.tiles, d.tiles // 2, d.tiles // 4
    AHEAD = 3
    mem = ExitStack()

    def several(n, name, shape, dt):
        return [kn.buffer(mem, f"{name}{u}", shape, dt) for u in range(n)]

    rows = several(4, "e_rows", [P, D], F32)
    gather_at = several(4, "e_gather_at", [P, 1], I32)
    lhs = several(2, "e_lhs", [P, P], F32)
    out = several(2, "e_out", [P, D], F32)
    final_at = several(2, "e_final_at", [P, 1], I32)
    total = [kn.bank[u] for u in range(2)]

    indexed = take("indexed", 2 * T)
    gathered = four("gathered", 16 * Q, software=True)
    scattered = pair("scattered", 16 * H, software=True)
    lhs_ready = pair("lhs_ready", H)
    carried = pair("carried", H)
    summed = pair("summed", H)
    evacuated = pair("evacuated", H)
    start = take("start", 1)

    def gpsimd(pool):
        g = nc.gpsimd

        def gather(i, v, n):
            j, u = in_two(i, v)
            if not (isinstance(i, int) and i == 0):
                pool.wait_ge(summed[u].sem, summed[u].at(j - 1))
            g.tensor_copy(gather_at[v][:], kn.src_i[:, ds(i * 4 + v, 1)]).then_inc(indexed.sem, 1)
            pool.wait_ge(indexed.sem, indexed.at(n))
            settle(pool, kn)
            pool.indirect_dma_start(rows[v][:], None, rows_dram,
                                    bass.IndirectOffsetOnAxis(ap=gather_at[v][:], axis=0),
                                    bounds_check=d.padded - 1, oob_is_err=False)\
                .then_inc(gathered[v].sem, 16)

        def tile(i, v, left):
            t = i * 4 + v
            j, u = in_two(i, v)
            n = t + 1 + AHEAD + t if left >= AHEAD else T + t
            if left >= AHEAD:
                gather(*after(i, v, AHEAD), n)
            pool.wait_ge(scattered[u].sem, scattered[u].at(j * 16))
            g.tensor_copy(final_at[u][:], kn.final_i[:, ds(t, 1)]).then_inc(indexed.sem, 1)
            pool.wait_ge(indexed.sem, indexed.at(n + 1))
            pool.wait_ge(evacuated[u].sem, evacuated[u].at(j + 1))
            settle(pool, kn)
            pool.indirect_dma_start(dram["sum"], bass.IndirectOffsetOnAxis(ap=final_at[u][:], axis=0),
                                    out[u][:], None, bounds_check=d.nodes - 1, oob_is_err=False)\
                .then_inc(scattered[u].sem, 16)

        for v in range(AHEAD):
            gather(0, v, v + 1)
        in_quads(pool, T, tile)
        for u in range(2):
            pool.wait_ge(scattered[u].sem, scattered[u].at(16 * H))

    def vector(dve):
        nc.vector.memset(total[1][0:1, :], 0.0).then_inc(start.sem, 1)

    def scalar(act):
        act.wait_ge(start.sem, start.at(1))

        def matrix_and_carry(i, v):
            t = i * 4 + v
            j, u = in_two(i, v)
            c = CARRY_IN[u]
            act.wait_ge(summed[u].sem, summed[u].at(j))
            settle(act, kn)
            act.activation(lhs[u][:], kn.same[:, ds(t * P, P)], ACT.Copy, scale=in_scale[:, ds(t, 1)])\
               .then_inc(lhs_ready[u].sem, 1)
            act.wait_ge(gathered[v].sem, gathered[v].at(i * 16 + 16))
            act.wait_ge(summed[1 - u].sem, summed[1 - u].at(j + u))
            act.copy(rows[v][c:c + 1, :], total[1 - u][c:c + 1, :]).then_inc(carried[u].sem, 1)

        def tile(i, v, left):
            j, u = in_two(i, v)
            if left:
                matrix_and_carry(*after(i, v, 1))
            act.wait_ge(summed[u].sem, summed[u].at(j + 1))
            act.wait_ge(scattered[u].sem, scattered[u].at(j * 16))
            settle(act, kn)
            act.activation(out[u][:], total[u][:], ACT.Copy, scale=out_scale[:, ds(i * 4 + v, 1)])\
               .then_inc(evacuated[u].sem, 1)

        matrix_and_carry(0, 0)
        in_quads(act, T, tile)

    def tensor(pe):
        def tile(i, v, left):
            j, u = in_two(i, v)
            pe.wait_ge(lhs_ready[u].sem, lhs_ready[u].at(j + 1))
            pe.wait_ge(carried[u].sem, carried[u].at(j + 1))
            pe.wait_ge(evacuated[u].sem, evacuated[u].at(j))
            pe.matmul(total[u][:], lhs[u][:], rows[v][:], start=True, stop=True).then_inc(summed[u].sem, 1)

        in_quads(pe, T, tile)

    mem.close()
    return {"gpsimd": gpsimd, "vector": vector, "scalar": scalar, "tensor": tensor}


def degree_stage(kn):
    nc, d, dram, take = kn.nc, kn.d, kn.dram, kn.sig.take
    T = d.tiles
    dinv_out = take("dinv_out", 16 * T, software=True)
    dinv_in = take("dinv_in", 16 * T, software=True)
    fixed = take("fixed", 2)
    dinv_done = take("dinv_done", 1)

    def gpsimd(pool):
        nc.gpsimd.tensor_tensor(kn.dinv[:], kn.degree[:], kn.minus_half[:], ALU.pow).then_inc(dinv_done.sem, 1)
        pool.wait_ge(dinv_done.sem, dinv_done.at(1))
        for t in range(T):
            pool.indirect_dma_start(dram["dinv"], bass.IndirectOffsetOnAxis(ap=kn.final_i[:, t:t + 1], axis=0),
                                    kn.dinv[:, t:t + 1], None, bounds_check=d.nodes - 1, oob_is_err=False)\
                .then_inc(dinv_out.sem, 16)
        pool.wait_ge(dinv_out.sem, dinv_out.at(16 * T))
        for t in range(T):
            pool.indirect_dma_start(kn.src_dinv[:, t:t + 1], None, dram["dinv"],
                                    bass.IndirectOffsetOnAxis(ap=kn.src_i[:, t:t + 1], axis=0),
                                    bounds_check=d.padded - 1, oob_is_err=False).then_inc(dinv_in.sem, 16)
        pool.wait_ge(dinv_in.sem, dinv_in.at(16 * T))
        for u in range(2):
            nc.gpsimd.memset(kn.src_dinv[CARRY_IN[u]:CARRY_IN[u] + 1, u:T:2], 1.0).then_inc(fixed.sem, 1)
        pool.wait_ge(fixed.sem, fixed.at(2))

    return {"gpsimd": gpsimd}


def edge_attention_stage(kn, rows_dram, logits_dram):
    nc, d, dram, take, pair, four = kn.nc, kn.d, kn.dram, kn.sig.take, kn.sig.pair, kn.sig.four
    T, H, Q = d.tiles, d.tiles // 2, d.tiles // 4
    AHEAD = 3
    mem = ExitStack()

    def two(name, shape, dt):
        return [kn.buffer(mem, f"{name}{u}", shape, dt) for u in range(2)]

    def fourfold(name, shape, dt):
        return [kn.buffer(mem, f"{name}{v}", shape, dt) for v in range(4)]

    K = HEADS
    rows = fourfold("a_rows_", [P, HC], F32)
    src_al = fourfold("a_src", [P, 2 * K], F32)
    dst_al = fourfold("a_dst", [P, 2 * K], F32)
    gather_at = fourfold("a_gather_at", [P, 1], I32)
    dst_at = fourfold("a_dst_at", [P, 1], I32)
    score = two("a_score", [P, 2 * K], F32)
    spread = two("a_spread", [P, K, P], F32)
    pen = two("a_pen", [P, P], F32)
    masked = two("a_masked", [P, K, P], F32)
    top = two("a_top", [P, K], F32)
    shifted = two("a_shifted", [P, 2 * K], F32)
    weight = two("a_weight", [P, 2 * K], F32)
    lhs = two("a_lhs", [P, K, P], F32)
    dval = two("a_dval", [P, K], F32)
    den = two("a_den", [P, K], F32)
    rden = two("a_rden", [P, K], F32)
    out = two("a_out", [P, HC + K], F32)
    final_at = two("a_final_at", [P, 1], I32)
    total = [[kn.bank[2 * u], kn.bank[2 * u + 1]] for u in range(2)]
    row_ps = [kn.bank[4 + u][:].rearrange("p (h q) -> p h q", h=K) for u in range(2)]
    den_ps = [kn.bank[6 + u][:, 0:K] for u in range(2)]

    indexed = take("indexed", 3 * T)
    gathered = four("gathered", 16 * Q, software=True)
    src_in = four("src_in", 16 * Q, software=True)
    dst_in = four("dst_in_", 16 * Q, software=True)
    scattered = pair("scattered", 16 * H, software=True)
    FRONT, BACK = 8, 3
    front = Steps(take("front_steps", FRONT * T))
    back = Steps(take("back_steps", BACK * T))
    spread_ready = pair("spread_ready", H)
    row_done = pair("row_done", H)
    shift_ready = pair("shift_ready", H)
    weighed = pair("weighed", H)
    lhs_ready = pair("lhs_ready", H)
    den_done = pair("den_done", H)
    summed = pair("summed", H)
    carried = pair("carried", H)
    rden_ready = pair("rden_ready", H)
    evacuated = pair("evacuated", H)
    start = take("start", 4)

    def gpsimd(pool):
        g = nc.gpsimd

        def gather(i, v, n):
            t = i * 4 + v
            j, u = in_two(i, v)
            if not (isinstance(i, int) and i == 0):
                pool.wait_ge(summed[u].sem, summed[u].at(j - 1))
            g.tensor_copy(gather_at[v][:], kn.src_i[:, ds(t, 1)]).then_inc(indexed.sem, 1)
            g.tensor_copy(dst_at[v][:], kn.dst_i[:, ds(t, 1)]).then_inc(indexed.sem, 1)
            pool.wait_ge(indexed.sem, indexed.at(n))
            settle(pool, kn)
            for to, sem, at in ((src_al[v], src_in[v], gather_at[v]), (dst_al[v], dst_in[v], dst_at[v])):
                pool.indirect_dma_start(to[:], None, logits_dram, bass.IndirectOffsetOnAxis(ap=at[:], axis=0),
                                        bounds_check=d.padded - 1, oob_is_err=False).then_inc(sem.sem, 16)
            pool.indirect_dma_start(rows[v][:], None, rows_dram,
                                    bass.IndirectOffsetOnAxis(ap=gather_at[v][:], axis=0),
                                    bounds_check=d.padded - 1, oob_is_err=False)\
                .then_inc(gathered[v].sem, 16)

        def tile(i, v, left):
            t = i * 4 + v
            j, u = in_two(i, v)
            n = (t + 1 + AHEAD) * 2 + t if left >= AHEAD else 2 * T + t
            if left >= AHEAD:
                gather(*after(i, v, AHEAD), n)
            pool.wait_ge(scattered[u].sem, scattered[u].at(j * 16))
            g.tensor_copy(final_at[u][:], kn.final_i[:, ds(t, 1)]).then_inc(indexed.sem, 1)
            pool.wait_ge(indexed.sem, indexed.at(n + 1))
            pool.wait_ge(evacuated[u].sem, evacuated[u].at(j + 1))
            settle(pool, kn)
            pool.indirect_dma_start(dram["sum_gat"], bass.IndirectOffsetOnAxis(ap=final_at[u][:], axis=0),
                                    out[u][:], None, bounds_check=d.nodes - 1, oob_is_err=False)\
                .then_inc(scattered[u].sem, 16)

        for v in range(AHEAD):
            gather(0, v, 2 * v + 2)
        in_quads(pool, T, tile)
        for u in range(2):
            pool.wait_ge(scattered[u].sem, scattered[u].at(16 * H))

    def vector(dve):
        v = nc.vector
        v.memset(total[1][0][0:1, :], 0.0).then_inc(start.sem, 1)
        v.memset(total[1][1][0:1, :], 0.0).then_inc(start.sem, 1)
        v.memset(den_ps[1][0:1, :], 1.0).then_inc(start.sem, 1)
        v.memset(top[1][0:1, :], 0.0)
        for u in range(2):
            ins = v.memset(dval[u][:], 1.0)
        ins.then_inc(start.sem, 1)
        dve.wait_ge(start.sem, start.at(4))

        def scores(i, w):
            t = i * 4 + w
            j, u = in_two(i, w)
            c = CARRY_IN[u]
            front.begin(t * FRONT)
            own = front.sig.sem
            dve.wait_ge(src_in[w].sem, src_in[w].at(i * 16 + 16))
            dve.wait_ge(dst_in[w].sem, dst_in[w].at(i * 16 + 16))
            dve.wait_ge(weighed[u].sem, weighed[u].at(j))
            front.mark(v.tensor_tensor(score[u][:, 0:K], src_al[w][:, 0:K], dst_al[w][:, K:2 * K], ALU.add))
            n = front.mark(v.tensor_tensor(score[u][:, K:2 * K], dst_al[w][:, 0:K], dst_al[w][:, K:2 * K], ALU.add))
            dve.wait_ge(own, n)
            n = front.mark(v.scalar_tensor_tensor(out=score[u][:], in0=score[u][:], scalar=SLOPE, in1=score[u][:],
                                                  op0=ALU.mult, op1=ALU.max))
            front.mark(v.tensor_scalar(pen[u][:], kn.same[:, ds(t * P, P)], BIG, -BIG, ALU.mult, ALU.add))
            dve.wait_ge(own, n)
            n = front.mark(v.tensor_copy(score[u][c:c + 1, 0:K], top[1 - u][c:c + 1, :]))
            dve.wait_ge(own, n)
            v.tensor_copy(spread[u][:], score[u][:, 0:K].unsqueeze(2).broadcast_to([P, K, P]))\
                .then_inc(spread_ready[u].sem, 1)

        def maxima(i, w):
            j, u = in_two(i, w)
            own = front.sig.sem
            dve.wait_ge(row_done[u].sem, row_done[u].at(j + 1))
            n = front.mark(v.tensor_tensor(masked[u][:], row_ps[u], pen[u][:].unsqueeze(1).broadcast_to([P, K, P]),
                                           ALU.add))
            dve.wait_ge(own, n)
            n = front.mark(v.tensor_reduce(top[u][:], masked[u][:], AX.X, ALU.max))
            dve.wait_ge(own, n)
            n = front.mark(v.tensor_tensor(top[u][:], top[u][:], score[u][:, K:2 * K], ALU.max))
            dve.wait_ge(own, n)
            v.tensor_tensor(shifted[u][:, 0:K], score[u][:, 0:K], top[u][:], ALU.subtract)
            v.tensor_tensor(shifted[u][:, K:2 * K], score[u][:, K:2 * K], top[u][:], ALU.subtract)\
                .then_inc(shift_ready[u].sem, 1)
            assert front.n == FRONT

        def sums(i, w, left):
            t = i * 4 + w
            j, u = in_two(i, w)
            c = CARRY_IN[u]
            back.begin(t * BACK)
            own = back.sig.sem
            if left:
                scores(*after(i, w, 1))
            dve.wait_ge(weighed[u].sem, weighed[u].at(j + 1))
            dve.wait_ge(summed[u].sem, summed[u].at(j))
            dve.wait_ge(den_done[1 - u].sem, den_done[1 - u].at(j + u))
            back.mark(v.tensor_copy(dval[u][c:c + 1, :], den_ps[1 - u][c:c + 1, :]))
            v.tensor_tensor(lhs[u][:], kn.same[:, ds(t * P, P)].unsqueeze(1).broadcast_to([P, K, P]),
                            weight[u][:, 0:K].unsqueeze(2).broadcast_to([P, K, P]), ALU.mult)\
                .then_inc(lhs_ready[u].sem, 1)
            if left:
                maxima(*after(i, w, 1))
            dve.wait_ge(den_done[u].sem, den_done[u].at(j + 1))
            n = back.mark(v.tensor_tensor(den[u][:], den_ps[u], weight[u][:, K:2 * K], ALU.add))
            dve.wait_ge(own, n)
            dve.wait_ge(evacuated[u].sem, evacuated[u].at(j))
            dve.wait_ge(scattered[u].sem, scattered[u].at(j * 16))
            n = back.mark(v.reciprocal(rden[u][:], den[u][:]))
            dve.wait_ge(own, n)
            v.tensor_tensor(out[u][:, HC:HC + K], weight[u][:, K:2 * K], rden[u][:], ALU.mult)\
                .then_inc(rden_ready[u].sem, 1)
            assert back.n == BACK

        scores(0, 0)
        maxima(0, 0)
        in_quads(dve, T, sums)

    def scalar(act):
        act.wait_ge(start.sem, start.at(4))

        def weigh(i, v):
            j, u = in_two(i, v)
            act.wait_ge(shift_ready[u].sem, shift_ready[u].at(j + 1))
            act.wait_ge(rden_ready[u].sem, rden_ready[u].at(j))
            act.activation(weight[u][:], shifted[u][:], ACT.Exp).then_inc(weighed[u].sem, 1)

        def tile(i, v, left):
            j, u = in_two(i, v)
            c = CARRY_IN[u]
            act.wait_ge(gathered[v].sem, gathered[v].at(i * 16 + 16))
            act.wait_ge(summed[1 - u].sem, summed[1 - u].at(j + u))
            act.copy(rows[v][c:c + 1, 0:D], total[1 - u][0][c:c + 1, :])
            act.copy(rows[v][c:c + 1, D:HC], total[1 - u][1][c:c + 1, :]).then_inc(carried[u].sem, 1)
            if left:
                weigh(*after(i, v, 1))
            act.wait_ge(rden_ready[u].sem, rden_ready[u].at(j + 1))
            act.wait_ge(summed[u].sem, summed[u].at(j + 1))
            act.wait_ge(scattered[u].sem, scattered[u].at(j * 16))
            for h in range(K):
                ins = act.activation(out[u][:, h * C:(h + 1) * C],
                                     total[u][h // 2][:, (h % 2) * C:(h % 2 + 1) * C], ACT.Copy,
                                     scale=rden[u][:, h:h + 1])
            ins.then_inc(evacuated[u].sem, 1)

        weigh(0, 0)
        in_quads(act, T, tile)

    def tensor(pe):
        def score_rows(i, v):
            j, u = in_two(i, v)
            pe.wait_ge(spread_ready[u].sem, spread_ready[u].at(j + 1))
            for h in range(K):
                mm = pe.matmul(row_ps[u][:, h, :], spread[u][:, h, :], kn.ident[:], start=True, stop=True)
            mm.then_inc(row_done[u].sem, 1)

        def tile(i, v, left):
            j, u = in_two(i, v)
            if left:
                score_rows(*after(i, v, 1))
            pe.wait_ge(lhs_ready[u].sem, lhs_ready[u].at(j + 1))
            pe.wait_ge(rden_ready[u].sem, rden_ready[u].at(j))
            for h in range(K):
                mm = pe.matmul(den_ps[u][:, h:h + 1], lhs[u][:, h, :], dval[u][:, h:h + 1], start=True, stop=True)
            mm.then_inc(den_done[u].sem, 1)
            pe.wait_ge(carried[u].sem, carried[u].at(j + 1))
            pe.wait_ge(evacuated[u].sem, evacuated[u].at(j))
            for h in range(K):
                mm = pe.matmul(total[u][h // 2][:, (h % 2) * C:(h % 2 + 1) * C], lhs[u][:, h, :],
                               rows[v][:, h * C:(h + 1) * C], start=True, stop=True)
            mm.then_inc(summed[u].sem, 1)

        score_rows(0, 0)
        in_quads(pe, T, tile)

    mem.close()
    return {"gpsimd": gpsimd, "vector": vector, "scalar": scalar, "tensor": tensor}


class Norm:

    def __init__(self, kn, mem):
        self.kn, self.nc, n = kn, kn.nc, kn.d.groups
        self.stats = kn.buffer(mem, "n_stats", [P, 2, S, 6], F32)
        self.moments = kn.buffer(mem, "n_moments", [P, 2, S, 2], F32)
        self.power = kn.buffer(mem, "n_power", [P, 2, S], F32)
        self.seen = kn.sig.take("n_seen", 2 * S * n)
        self.rstd = kn.sig.take("n_rstd", 2 * n)

    def moments_of(self, dve, row, s, i, u):
        g = i * 2 + u
        self.nc.vector.bn_stats(self.stats[:, u, s, :], row).then_inc(self.seen.sem, 1)
        dve.wait_ge(self.seen.sem, self.seen.at(g * (2 * S) + 2 * s + 1))
        settle(dve, self.kn)
        self.nc.vector.bn_aggr(self.moments[:, u, s, :], self.stats[:, u, s, :]).then_inc(self.seen.sem, 1)

    def pool(self, pool, i, u):
        g = i * 2 + u
        pool.wait_ge(self.seen.sem, self.seen.at(g * (2 * S) + 2 * S))
        self.nc.gpsimd.tensor_tensor(self.power[:, u, :], self.moments[:, u, :, 1], self.kn.eps[:], ALU.add)\
            .then_inc(self.rstd.sem, 1)
        pool.wait_ge(self.rstd.sem, self.rstd.at(g * 2 + 1))
        self.nc.gpsimd.tensor_tensor(self.power[:, u, :], self.power[:, u, :],
                                     self.kn.minus_half[:, 0:1].broadcast_to([P, S]), ALU.pow)\
            .then_inc(self.rstd.sem, 1)

    def apply(self, dve, out, rows, i, u, done):
        dve.wait_ge(self.rstd.sem, self.rstd.at((i * 2 + u) * 2 + 2))
        for s in range(S):
            self.nc.vector.tensor_scalar(out[:, s, :], rows[:, s, :], self.moments[:, u, s, 0:1],
                                         self.power[:, u, s:s + 1], ALU.subtract, ALU.mult).then_inc(done.sem, 1)


def node_rows(ap, i, u):
    return ap[ds(i * (2 * GROUP) + u * GROUP, GROUP), :].rearrange("(s p) c -> p s c", p=P)


def gin_stage(kn):
    nc, d, dram, take, pair = kn.nc, kn.d, kn.dram, kn.sig.take, kn.sig.pair
    G, H = d.groups, d.groups // 2
    mem = ExitStack()

    def two(name, shape, dt):
        return [kn.buffer(mem, f"{name}{u}", shape, dt) for u in range(2)]

    x = two("g_x", [P, S, D], F32)
    z = two("g_z", [P, S, D], F32)
    z_hi = kn.buffer(mem, "g_z_hi", [P, 4, D], F16)
    z_lo = kn.buffer(mem, "g_z_lo", [P, 4, D], F16)
    r_f = two("g_r", [P, D], F32)
    r_hi = kn.buffer(mem, "g_r_hi", [P, 4, D], F16)
    r_lo = kn.buffer(mem, "g_r_lo", [P, 4, D], F16)
    y = two("g_y", [P, S, D], F32)
    norm = Norm(kn, mem)
    tp = [kn.bank[0], kn.bank[1]]
    mm = [kn.bank[2 + s] for s in range(S)]
    mid_ps = [kn.bank[6], kn.bank[7]]

    x_in = pair("x_in", 16 * H)
    sum_in = pair("sum_in", 16 * H)
    z_ready = pair("z_ready", H * S)
    x_ready = pair("x_ready", H)
    turned = pair("turned", 4 * H)
    hi_done = take("hi_done", 4 * G)
    lo_done = take("lo_done", 4 * G)
    mid = take("mid", 4 * G)
    r_done = take("r_done", 4 * G)
    r_hi_done = take("r_hi_done", 4 * G)
    r_lo_done = take("r_lo_done", 4 * G)
    prod = take("prod", S * G)
    y_done = pair("y_done_", S * H)
    rows_out = pair("rows_out", S * H)
    stored = pair("stored", 16 * H)

    def sync(sp):
        def load_x(i, u):
            sp.wait_ge(y_done[u].sem, y_done[u].at(i * S))
            sp.dma_start(x[u][:], node_rows(dram["x"], i, u)).then_inc(x_in[u].sem, 16)

        def load_sums(i, u):
            sp.wait_ge(turned[u].sem, turned[u].at(i * 4))
            sp.dma_start(z[u][:], node_rows(dram["sum"], i, u)).then_inc(sum_in[u].sem, 16)

        def group(i, u, last):
            if not last:
                load_x(*following(i, u))
            if ahead(i, G):
                load_sums(i + 1, u)
            sp.wait_ge(rows_out[u].sem, rows_out[u].at(i * S + S))
            sp.dma_start(node_rows(dram["x1"], i, u), y[u][:]).then_inc(stored[u].sem, 16)

        load_sums(0, 0)
        load_x(0, 0)
        load_sums(0, 1)
        in_pairs(sp, G, group)
        for u in range(2):
            sp.wait_ge(stored[u].sem, stored[u].at(16 * H))

    def gpsimd(pool):
        def group(i, u, last):
            pool.wait_ge(z_ready[u].sem, z_ready[u].at(i * S + S))
            nc.gpsimd.tensor_tensor(x[u][:], x[u][:], kn.gin_b2[:].unsqueeze(1).broadcast_to([P, S, D]), ALU.add)\
                .then_inc(x_ready[u].sem, 1)
            norm.pool(pool, i, u)

        in_pairs(pool, G, group)

    def vector(dve):
        v = nc.vector

        def add_sums(i, u):
            dve.wait_ge(x_in[u].sem, x_in[u].at(i * 16 + 16))
            dve.wait_ge(sum_in[u].sem, sum_in[u].at(i * 16 + 16))
            for s in range(S):
                v.tensor_tensor(z[u][:, s, :], z[u][:, s, :], x[u][:, s, :], ALU.add).then_inc(z_ready[u].sem, 1)

        def low_parts(i, u, chunks=range(4)):
            g = i * 2 + u
            for k in chunks:
                dve.wait_ge(hi_done.sem, hi_done.at(g * 4 + k + 1))
                v.scalar_tensor_tensor(out=z_lo[:, k, :], in0=tp[k % 2][:], scalar=GIN_SCALE, in1=z_hi[:, k, :],
                                       op0=ALU.mult, op1=ALU.subtract).then_inc(lo_done.sem, 1)

        def group(i, u, last):
            g = i * 2 + u
            for m in range(4):
                dve.wait_ge(r_hi_done.sem, r_hi_done.at(g * 4 + m + 1))
                v.tensor_tensor(r_lo[:, m, :], r_f[m % 2][:], r_hi[:, m, :], ALU.subtract).then_inc(r_lo_done.sem, 1)
            if not last:
                add_sums(*following(i, u))
            dve.wait_ge(x_ready[u].sem, x_ready[u].at(i + 1))
            dve.wait_ge(stored[u].sem, stored[u].at(i * 16))
            for s in range(S):
                if s >= 2 and not last:
                    low_parts(*following(i, u), (2 * s - 4, 2 * s - 3))
                dve.wait_ge(prod.sem, prod.at(g * S + s + 1))
                v.scalar_tensor_tensor(out=y[u][:, s, :], in0=mm[s][:], scalar=GIN_UNSCALE, in1=x[u][:, s, :],
                                       op0=ALU.mult, op1=ALU.add).then_inc(y_done[u].sem, 1)
                dve.wait_ge(y_done[u].sem, y_done[u].at(i * S + s + 1))
                norm.moments_of(dve, y[u][:, s, :], s, i, u)
            norm.apply(dve, y[u], y[u], i, u, rows_out[u])

        add_sums(0, 0)
        low_parts(0, 0)
        in_pairs(dve, G, group)

    def scalar(act):
        def high_parts(i, u):
            g = i * 2 + u
            for k in range(4):
                act.wait_ge(turned[u].sem, turned[u].at(i * 4 + k + 1))
                act.activation(z_hi[:, k, :], tp[k % 2][:], ACT.Copy, scale=GIN_SCALE).then_inc(hi_done.sem, 1)

        def group(i, u, last):
            g = i * 2 + u
            for m in range(4):
                act.wait_ge(mid.sem, mid.at(g * 4 + m + 1))
                if m >= 2:
                    act.wait_ge(r_lo_done.sem, r_lo_done.at(g * 4 + m - 1))
                act.wait_ge(prod.sem, prod.at(g * S))
                act.activation(r_f[m % 2][:], mid_ps[m % 2][:], ACT.Relu, scale=GIN_UNSCALE * GIN_SCALE,
                               bias=kn.vec_scaled[:, V_GIN_B1 + m:V_GIN_B1 + m + 1]).then_inc(r_done.sem, 1)
                act.wait_ge(r_done.sem, r_done.at(g * 4 + m + 1))
                act.copy(r_hi[:, m, :], r_f[m % 2][:]).then_inc(r_hi_done.sem, 1)
            if not last:
                high_parts(*following(i, u))

        high_parts(0, 0)
        in_pairs(act, G, group)

    def tensor(pe):
        def turn(i, u, chunks=range(4)):
            g = i * 2 + u
            pe.wait_ge(z_ready[u].sem, z_ready[u].at(i * S + S))
            for k in chunks:
                if k >= 2:
                    pe.wait_ge(lo_done.sem, lo_done.at(g * 4 + k - 1))
                else:
                    pe.wait_ge(lo_done.sem, lo_done.at(g * 4))
                for s in range(S):
                    ins = pe.transpose(tp[k % 2][:, s * P:(s + 1) * P], z[u][:, s, k * P:(k + 1) * P], kn.ident[:])
                ins.then_inc(turned[u].sem, 1)

        def group(i, u, last):
            g = i * 2 + u
            def split(k):
                pe.wait_ge(lo_done.sem, lo_done.at(g * 4 + k + 1))

            for m in range(4):
                pe.wait_ge(r_done.sem, r_done.at(g * 4 + (m - 1 if m >= 2 else 0)))
                split_product(pe, mid_ps[m % 2][:],
                              lambda k: (kn.weights(False, W_GIN1, k, 0, D)[:, m * P:(m + 1) * P],
                                         kn.weights(True, W_GIN1, k, 0, D)[:, m * P:(m + 1) * P]),
                              lambda k: (z_hi[:, k, :], z_lo[:, k, :]), 4, split if m == 0 else None)\
                    .then_inc(mid.sem, 1)

            def hidden(k):
                pe.wait_ge(r_lo_done.sem, r_lo_done.at(g * 4 + k + 1))

            for s in range(S):
                if s >= 2 and not last:
                    turn(*following(i, u), (2 * s - 4, 2 * s - 3))
                pe.wait_ge(y_done[1 - u].sem, y_done[1 - u].at((i + u - 1) * S + s + 1))
                split_product(pe, mm[s][:],
                              lambda k: (r_hi[:, k, s * P:(s + 1) * P], r_lo[:, k, s * P:(s + 1) * P]),
                              lambda k: (kn.weights(False, W_GIN2, k, 0, D), kn.weights(True, W_GIN2, k, 0, D)),
                              4, hidden if s == 0 else None).then_inc(prod.sem, 1)

        turn(0, 0)
        in_pairs(pe, G, group)

    mem.close()
    return {"sync": sync, "gpsimd": gpsimd, "vector": vector, "scalar": scalar, "tensor": tensor}


def linear_stage(kn, layer):
    nc, d, dram, take, pair = kn.nc, kn.d, kn.dram, kn.sig.take, kn.sig.pair
    G, H = d.groups, d.groups // 2
    sage = layer == "sage"
    chunks = 8 if sage else 4
    unit = W_SAGE_L if sage else W_GCN
    bias = V_SAGE_B if sage else V_GCN_B
    x_dram = dram["x1"] if sage else dram["x3"]
    turns = ((0, 1), (2, 3), (4, 5), (6, 7)) if sage else ((), (), (0, 1), (2, 3))
    mem = ExitStack()

    def two(name, shape, dt):
        return [kn.buffer(mem, f"{name}{u}", shape, dt) for u in range(2)]

    x = two("l_x", [P, S, D], F32)
    z = two("l_z", [P, S, D], F32)
    node_dinv = two("l_dinv", [P, S, 1], F32)
    z_hi = kn.buffer(mem, "l_z_hi", [P, 2, chunks, D], F16)
    z_lo = kn.buffer(mem, "l_z_lo", [P, 2, chunks, D], F16)
    h = two("l_h", [P, 4, D], F32)
    tp = [kn.bank[0], kn.bank[1]]
    mm = [kn.bank[2 + n] for n in range(4)]

    x_in = pair("x_in", 16 * H)
    sum_in = pair("sum_in", 16 * H)
    dinv_in = pair("dinv_in_", 0 if sage else 16 * H)
    z_ready = pair("z_ready", 0 if sage else H * 2 * S)
    turned = pair("turned", chunks * H)
    hi_done = take("hi_done", chunks * G)
    lo_done = take("lo_done", chunks * G)
    mid = take("mid", 4 * G)
    h_done = take("h_done", 4 * G)
    seen = take("h_seen", 4 * G)
    stored = pair("stored", 16 * H)

    def sync(sp):
        def load(i, u):
            sp.wait_ge(turned[u].sem, turned[u].at(i * chunks))
            sp.dma_start(x[u][:], node_rows(x_dram, i, u)).then_inc(x_in[u].sem, 16)
            sp.dma_start(z[u][:], node_rows(dram["sum"], i, u)).then_inc(sum_in[u].sem, 16)
            if not sage:
                sp.dma_start(node_dinv[u][:], node_rows(dram["dinv"], i, u),
                             allow_slow_non_contiguous=True).then_inc(dinv_in[u].sem, 16)

        def group(i, u, last):
            g = i * 2 + u
            if ahead(i, G):
                load(i + 1, u)
            sp.wait_ge(h_done.sem, h_done.at(g * 4 + 4))
            settle(sp, kn)
            sp.dma_start(dram["h"][:, :, ds(i * (2 * GROUP) + u * GROUP, GROUP)].rearrange("m p n -> p m n"), h[u][:])\
                .then_inc(stored[u].sem, 16)

        load(0, 0)
        load(0, 1)
        in_pairs(sp, G, group)
        for u in range(2):
            sp.wait_ge(stored[u].sem, stored[u].at(16 * H))

    def vector(dve):
        v = nc.vector

        def scale(i, u):
            if sage:
                return
            dve.wait_ge(x_in[u].sem, x_in[u].at(i * 16 + 16))
            dve.wait_ge(sum_in[u].sem, sum_in[u].at(i * 16 + 16))
            dve.wait_ge(dinv_in[u].sem, dinv_in[u].at(i * 16 + 16))
            for s in range(S):
                v.scalar_tensor_tensor(out=z[u][:, s, :], in0=x[u][:, s, :], scalar=node_dinv[u][:, s, :],
                                       in1=z[u][:, s, :], op0=ALU.mult, op1=ALU.add).then_inc(z_ready[u].sem, 1)
            dve.wait_ge(z_ready[u].sem, z_ready[u].at(i * (2 * S) + S))
            for s in range(S):
                v.tensor_scalar(z[u][:, s, :], z[u][:, s, :], node_dinv[u][:, s, :], None, ALU.mult)\
                    .then_inc(z_ready[u].sem, 1)

        def low_parts(i, u, some=range(chunks)):
            g = i * 2 + u
            for k in some:
                dve.wait_ge(hi_done.sem, hi_done.at(g * chunks + k + 1))
                v.scalar_tensor_tensor(out=z_lo[:, u, k, :], in0=tp[k % 2][:], scalar=A_SCALE, in1=z_hi[:, u, k, :],
                                       op0=ALU.mult, op1=ALU.subtract).then_inc(lo_done.sem, 1)

        def group(i, u, last):
            g = i * 2 + u

            real = d.last_real if last else GROUP
            if not last:
                scale(*following(i, u))
            for m in range(4):
                if not last:
                    low_parts(*following(i, u), turns[m])
                dve.wait_ge(h_done.sem, h_done.at(g * 4 + m + 1))
                v.bn_stats(kn.bn_stats[:, m, ds(g * 6, 6)], h[u][:, m, 0:real]).then_inc(seen.sem, 1)

        scale(0, 0)
        low_parts(0, 0)
        in_pairs(dve, G, group)

    def scalar(act):
        def high_parts(i, u, some=range(chunks)):
            g = i * 2 + u
            for k in some:
                act.wait_ge(turned[u].sem, turned[u].at(i * chunks + k + 1))
                act.activation(z_hi[:, u, k, :], tp[k % 2][:], ACT.Copy, scale=A_SCALE).then_inc(hi_done.sem, 1)

        def group(i, u, last):
            g = i * 2 + u

            act.wait_ge(stored[u].sem, stored[u].at(i * 16))
            act.wait_ge(seen.sem, seen.at((g - 1) * 4))
            for m in range(4):
                if not last:
                    high_parts(*following(i, u), turns[m])
                act.wait_ge(mid.sem, mid.at(g * 4 + m + 1))
                act.activation(h[u][:, m, :], mm[m][:], ACT.Identity, scale=UNSCALE,
                               bias=kn.vec[:, bias + m:bias + m + 1]).then_inc(h_done.sem, 1)

        high_parts(0, 0)
        in_pairs(act, G, group)

    def tensor(pe):
        def turn(i, u, some=range(chunks)):
            g = i * 2 + u
            if sage:
                pe.wait_ge(x_in[u].sem, x_in[u].at(i * 16 + 16))
                pe.wait_ge(sum_in[u].sem, sum_in[u].at(i * 16 + 16))
            else:
                pe.wait_ge(z_ready[u].sem, z_ready[u].at(i * (2 * S) + 2 * S))
            for k in some:
                pe.wait_ge(lo_done.sem, lo_done.at(g * chunks + (k - 1 if k >= 2 else 0)))
                rows = z[u] if k < 4 else x[u]
                for s in range(S):
                    ins = pe.transpose(tp[k % 2][:, s * P:(s + 1) * P], rows[:, s, (k % 4) * P:(k % 4 + 1) * P],
                                       kn.ident[:])
                ins.then_inc(turned[u].sem, 1)

        def group(i, u, last):
            g = i * 2 + u
            pe.wait_ge(lo_done.sem, lo_done.at(g * chunks + chunks))
            for m in range(4):
                if turns[m] and not last:
                    turn(*following(i, u), turns[m])
                pe.wait_ge(h_done.sem, h_done.at((g - 1) * 4 + m + 1))
                split_product(pe, mm[m][:],
                              lambda k: (kn.weights(False, unit, k, 0, D)[:, m * P:(m + 1) * P],
                                         kn.weights(True, unit, k, 0, D)[:, m * P:(m + 1) * P]),
                              lambda k: (z_hi[:, u, k, :], z_lo[:, u, k, :]), chunks).then_inc(mid.sem, 1)

        turn(0, 0)
        in_pairs(pe, G, group)

    mem.close()
    return {"sync": sync, "vector": vector, "scalar": scalar, "tensor": tensor}


def norm_coefficients_stage(kn, gamma, beta):
    nc, take = kn.nc, kn.sig.take
    mem = ExitStack()
    mv = kn.buffer(mem, "c_mv", [P, 4, 2], F32)
    rstd = kn.buffer(mem, "c_rstd", [P, 4], F32)
    neg = kn.buffer(mem, "c_neg", [P, 4], F32)
    steps = take("coef_steps", 9)

    def vector(dve):
        v = nc.vector
        for m in range(4):
            v.bn_aggr(mv[:, m, :], kn.bn_stats[:, m, :]).then_inc(steps.sem, 1)
        dve.wait_ge(steps.sem, steps.at(6))
        v.tensor_tensor(kn.bn_scale[:], rstd[:], kn.vec[:, gamma:gamma + 4], ALU.mult).then_inc(steps.sem, 1)
        dve.wait_ge(steps.sem, steps.at(7))
        v.tensor_tensor(neg[:], mv[:, :, 0], kn.bn_scale[:], ALU.mult).then_inc(steps.sem, 1)
        dve.wait_ge(steps.sem, steps.at(8))
        v.tensor_tensor(kn.bn_shift[:], kn.vec[:, beta:beta + 4], neg[:], ALU.subtract).then_inc(steps.sem, 1)

    def gpsimd(pool):
        g = nc.gpsimd
        pool.wait_ge(steps.sem, steps.at(4))
        g.tensor_scalar(rstd[:], mv[:, :, 1], EPS, None, ALU.add).then_inc(steps.sem, 1)
        pool.wait_ge(steps.sem, steps.at(5))
        g.tensor_tensor(rstd[:], rstd[:], kn.minus_half[:, 0:1].broadcast_to([P, 4]), ALU.pow).then_inc(steps.sem, 1)

    mem.close()
    return {"vector": vector, "gpsimd": gpsimd}


def batch_norm_stage(kn, layer):
    nc, d, dram, take, pair = kn.nc, kn.d, kn.dram, kn.sig.take, kn.sig.pair
    G, H = d.groups, d.groups // 2
    sage = layer == "sage"
    func = ACT.Relu if sage else ACT.Gelu
    x_dram, out_dram = (dram["x1"], dram["x2_biased"]) if sage else (dram["x3"], dram["out"])
    K = HEADS
    mem = ExitStack()

    def two(name, shape, dt):
        return [kn.buffer(mem, f"{name}{u}", shape, dt) for u in range(2)]

    h = two("b_h", [P, 4, D], F32)
    x = two("b_x", [P, S, D], F32)
    y = two("b_y", [P, S, D], F32) if not sage else [kn.buffer(mem, "b_y", [P, S, D], F32)] * 2
    o = two("b_o", [P, S, D], F32)
    if sage:
        z_hi = kn.buffer(mem, "b_z_hi", [P, 2, 4, D], F16)
        z_lo = kn.buffer(mem, "b_z_lo", [P, 2, 4, D], F16)
        wide = two("b_wide", [P, HC], F32)
        al = two("b_al", [P, S, 2 * K], F32)
    norm = Norm(kn, mem)
    tp = [[kn.bank[n] for n in (0, 1, 0, 1)]] * 2 if sage else [kn.bank[0:4], kn.bank[4:8]]
    tq = [kn.bank[2], kn.bank[3]]
    mm = [kn.bank[4], kn.bank[5]]
    al_ps = kn.bank[7][:, 0:2 * K]

    h_in = pair("h_in", 16 * H)
    x_in = pair("x_in", 16 * H)
    f_done = pair("f_done", 4 * H)
    rows_turned = pair("rows_turned", S * H)
    y_done = pair("y_done_", S * H)
    rows_out = pair("rows_out", S * H)
    stored = pair("stored", 16 * H)
    biased = pair("biased", H if sage else 0)
    turned = pair("turned", 4 * H if sage else 0)
    hi_done = take("hi_done", 4 * G if sage else 0)
    lo_done = take("lo_done", 4 * G if sage else 0)
    prod = take("prod", 2 * S * G if sage else 0)
    wide_done = take("wide_done", 2 * S * G if sage else 0)
    wide_stored = pair("wide_stored", 16 * 2 * G if sage else 0)
    al_prod = take("al_prod", S * G if sage else 0)
    al_done = take("al_done", S * G if sage else 0)
    al_stored = pair("al_stored", 16 * H if sage else 0)

    def sync(sp):
        def load(i, u):
            sp.wait_ge(rows_turned[u].sem, rows_turned[u].at(i * S))
            settle(sp, kn)
            sp.dma_start(h[u][:], dram["h"][:, :, ds(i * (2 * GROUP) + u * GROUP, GROUP)]
                         .rearrange("m p n -> p m n")).then_inc(h_in[u].sem, 16)
            sp.wait_ge(y_done[u].sem, y_done[u].at(i * S))
            sp.dma_start(x[u][:], node_rows(x_dram, i, u)).then_inc(x_in[u].sem, 16)

        def store(i, u):
            if sage:
                sp.wait_ge(biased[u].sem, biased[u].at(i + 1))
            else:
                sp.wait_ge(rows_out[u].sem, rows_out[u].at(i * S + S))
            sp.dma_start(node_rows(out_dram, i, u), o[u][:]).then_inc(stored[u].sem, 16)

        def group(i, u, last):
            g = i * 2 + u
            if ahead(i, G):
                load(i + 1, u)
            store(i, u)
            if sage:
                for s in range(S):
                    sp.wait_ge(wide_done.sem, wide_done.at(g * (2 * S) + 2 * s + 2))
                    sp.dma_start(dram["h1"][ds(i * (2 * GROUP) + u * GROUP + s * P, P), :], wide[s % 2][:])\
                        .then_inc(wide_stored[s % 2].sem, 16)
                sp.wait_ge(al_done.sem, al_done.at(g * S + S))
                sp.dma_start(node_rows(dram["al1"], i, u), al[u][:]).then_inc(al_stored[u].sem, 16)

        load(0, 0)
        load(0, 1)
        in_pairs(sp, G, group)
        for u in range(2):
            sp.wait_ge(stored[u].sem, stored[u].at(16 * H))
            if sage:
                sp.wait_ge(wide_stored[u].sem, wide_stored[u].at(16 * 2 * G))
                sp.wait_ge(al_stored[u].sem, al_stored[u].at(16 * H))

    def gpsimd(pool):
        def bias(i, u):
            pool.wait_ge(turned[u].sem, turned[u].at(i * 4 + 4))
            nc.gpsimd.tensor_tensor(o[u][:], o[u][:], kn.fc_b[:].unsqueeze(1).broadcast_to([P, S, D]), ALU.add)\
                .then_inc(biased[u].sem, 1)

        def group(i, u, last):
            if not last:
                norm.pool(pool, *following(i, u))
                bias(*following(i, u))

        if sage:
            norm.pool(pool, 0, 0)
            bias(0, 0)
            in_pairs(pool, G, group)
        else:
            in_pairs(pool, G, lambda i, u, last: norm.pool(pool, i, u))

    def vector(dve):
        v = nc.vector

        def residual(i, u, subtiles):
            g = i * 2 + u
            dve.wait_ge(x_in[u].sem, x_in[u].at(i * 16 + 16))
            dve.wait_ge(rows_out[u].sem, rows_out[u].at(i * S))
            for s in subtiles:
                dve.wait_ge(rows_turned[u].sem, rows_turned[u].at(i * S + s + 1))
                v.scalar_tensor_tensor(out=y[u][:, s, :], in0=x[u][:, s, :], scalar=2.0, in1=tp[u][s][:],
                                       op0=ALU.mult, op1=ALU.add).then_inc(y_done[u].sem, 1)
                dve.wait_ge(y_done[u].sem, y_done[u].at(i * S + s + 1))
                norm.moments_of(dve, y[u][:, s, :], s, i, u)

        def finish(i, u):
            dve.wait_ge(stored[u].sem, stored[u].at(i * 16))
            norm.apply(dve, o[u], y[u], i, u, rows_out[u])

        def low_parts(i, u):
            g = i * 2 + u
            for k in range(4):
                dve.wait_ge(hi_done.sem, hi_done.at(g * 4 + k + 1))
                v.scalar_tensor_tensor(out=z_lo[:, u, k, :], in0=tq[k % 2][:], scalar=A_SCALE, in1=z_hi[:, u, k, :],
                                       op0=ALU.mult, op1=ALU.subtract).then_inc(lo_done.sem, 1)

        def logits(i, u, s):
            g = i * 2 + u
            dve.wait_ge(al_prod.sem, al_prod.at(g * S + s + 1))
            v.tensor_scalar(al[u][:, s, :], al_ps, UNSCALE, None, ALU.mult).then_inc(al_done.sem, 1)

        def group(i, u, last):
            dve.wait_ge(al_stored[u].sem, al_stored[u].at(i * 16))
            if not last:
                residual(*following(i, u), (0, 1))
            logits(i, u, 0)
            if not last:
                residual(*following(i, u), (2, 3))
                finish(*following(i, u))
            logits(i, u, 1)
            logits(i, u, 2)
            if not last:
                low_parts(*following(i, u))
            logits(i, u, 3)

        def group_alone(i, u, last):
            if not last:
                residual(*following(i, u), range(S))
            finish(i, u)

        residual(0, 0, range(S))
        if sage:
            finish(0, 0)
            low_parts(0, 0)
        in_pairs(dve, G, group if sage else group_alone)

    def scalar(act):
        def apply(i, u):
            act.wait_ge(h_in[u].sem, h_in[u].at(i * 16 + 16))
            for m in range(4):
                act.activation(h[u][:, m, :], h[u][:, m, :], func, scale=kn.bn_scale[:, m:m + 1],
                               bias=kn.bn_shift[:, m:m + 1]).then_inc(f_done[u].sem, 1)

        def high_parts(i, u):
            g = i * 2 + u
            for k in range(4):
                act.wait_ge(turned[u].sem, turned[u].at(i * 4 + k + 1))
                act.activation(z_hi[:, u, k, :], tq[k % 2][:], ACT.Copy, scale=A_SCALE).then_inc(hi_done.sem, 1)

        def group(i, u, last):
            g = i * 2 + u
            for s in range(S):
                if s == 1 and ahead(i, G):
                    apply(i + 1, u)
                if s == 3 and not last:
                    high_parts(*following(i, u))
                w = wide_stored[s % 2]
                act.wait_ge(w.sem, w.at(g * 32 + (s // 2) * 16))
                for n in range(2):
                    act.wait_ge(prod.sem, prod.at(g * (2 * S) + 2 * s + n + 1))
                    act.activation(wide[s % 2][:, n * D:(n + 1) * D], mm[n][:], ACT.Copy, scale=UNSCALE)\
                       .then_inc(wide_done.sem, 1)

        if sage:
            apply(0, 0)
            apply(0, 1)
            high_parts(0, 0)
            in_pairs(act, G, group)
        else:
            in_pairs(act, G, lambda i, u, last: apply(i, u))

    def tensor(pe):
        def turn_rows(i, u, subtiles):
            pe.wait_ge(f_done[u].sem, f_done[u].at(i * 4 + 4))
            for s in subtiles:
                if not sage:
                    pe.wait_ge(y_done[u].sem, y_done[u].at((i - 1) * S + s + 1))
                elif s >= 2:
                    pe.wait_ge(y_done[u].sem, y_done[u].at(i * S + s - 1))
                else:
                    pe.wait_ge(y_done[1 - u].sem, y_done[1 - u].at((i + u) * S))
                for m in range(4):
                    ins = pe.transpose(tp[u][s][:, m * P:(m + 1) * P], h[u][:, m, s * P:(s + 1) * P], kn.ident[:])
                ins.then_inc(rows_turned[u].sem, 1)

        def turn_back(i, u):
            g = i * 2 + u
            pe.wait_ge(rows_out[u].sem, rows_out[u].at(i * S + S))
            for k in range(4):
                pe.wait_ge(lo_done.sem, lo_done.at(g * 4 + (k - 1 if k >= 2 else 0)))
                for s in range(S):
                    ins = pe.transpose(tq[k % 2][:, s * P:(s + 1) * P], o[u][:, s, k * P:(k + 1) * P], kn.ident[:])
                ins.then_inc(turned[u].sem, 1)

        def products(i, u, s):
            g = i * 2 + u
            parts = lambda k: (z_hi[:, u, k, s * P:(s + 1) * P], z_lo[:, u, k, s * P:(s + 1) * P])
            for n in range(2):
                if s:
                    pe.wait_ge(wide_done.sem, wide_done.at(g * (2 * S) + 2 * s + n - 1))
                else:
                    pe.wait_ge(wide_done.sem, wide_done.at(g * (2 * S)))
                split_product(pe, mm[n][:], parts,
                              lambda k: (kn.weights(False, W_GAT1, k, n, HC), kn.weights(True, W_GAT1, k, n, HC)),
                              4).then_inc(prod.sem, 1)
            pe.wait_ge(al_done.sem, al_done.at(g * S + s))
            split_product(pe, al_ps, parts, lambda k: (kn.wa_hi[:, k, :], kn.wa_lo[:, k, :]), 4)\
                .then_inc(al_prod.sem, 1)

        def group(i, u, last):
            pe.wait_ge(lo_done.sem, lo_done.at((i * 2 + u) * 4 + 4))
            if not last:
                turn_rows(*following(i, u), (0, 1))
            products(i, u, 0)
            if not last:
                turn_rows(*following(i, u), (2, 3))
            products(i, u, 1)
            products(i, u, 2)
            if not last:
                turn_back(*following(i, u))
            products(i, u, 3)

        if sage:
            turn_rows(0, 0, range(S))
            turn_back(0, 0)
            in_pairs(pe, G, group)
        else:
            in_pairs(pe, G, lambda i, u, last: turn_rows(i, u, range(S)))

    mem.close()
    return {"sync": sync, "gpsimd": gpsimd, "vector": vector, "scalar": scalar, "tensor": tensor}


def gat_stage(kn, layer):
    nc, d, dram, take, pair, four = kn.nc, kn.d, kn.dram, kn.sig.take, kn.sig.pair, kn.sig.four
    G, H = d.groups, d.groups // 2
    first = layer == 1
    K = HEADS
    CH = HC // P
    bias = V_GAT1_B if first else V_GAT2_B
    h_dram = dram["h1"] if first else dram["h2"]
    products = 2 * S if first else S
    turns = [(n,) for n in range(CH)] if first else [(0, 1, 2), (3, 4, 5), (6, 7), ()]
    mem = ExitStack()

    def two(name, shape, dt):
        return [kn.buffer(mem, f"{name}{u}", shape, dt) for u in range(2)]

    z = two("t_z", [P, S, HC + K], F32)
    hrow = two("t_h", [P, HC], F32)
    r_f = two("t_r", [P, D], F32)
    r_hi = kn.buffer(mem, "t_r_hi", [P, 2, CH, D], F16)
    r_lo = kn.buffer(mem, "t_r_lo", [P, 2, CH, D], F16)
    if first:
        wide = two("t_wide", [P, HC], F32)
        al = two("t_al", [P, S, 2 * K], F32)
    else:
        x = [kn.w_hi[:, 2 * u:2 * u + 2, :].bitcast(F32).rearrange("p a (b c) -> p (a b) c", c=D) for u in range(2)]
        norm = Norm(kn, mem)
    tp = [kn.bank[n] for n in ((0, 1, 4, 5) if first else (0, 1, 6, 7))]
    mm = [kn.bank[2], kn.bank[3]] if first else [kn.bank[2 + s] for s in range(S)]
    al_ps = kn.bank[7][:, 0:2 * K]

    sum_in = [four(f"sum_in{u}_", 16 * H) for u in range(2)]
    h_in = pair("h_in", 16 * 2 * G)
    z_ready = pair("z_ready", S * H)
    turned = pair("turned", CH * H)
    r_done = take("r_done", CH * G)
    r_hi_done = take("r_hi_done", CH * G)
    r_lo_done = take("r_lo_done", CH * G)
    prod = take("prod", products * G)
    if first:
        wide_done = take("wide_done", 2 * S * G)
        wide_stored = pair("wide_stored", 16 * 2 * G)
        al_prod = take("al_prod", S * G)
        al_done = take("al_done", S * G)
        al_stored = pair("al_stored", 16 * H)
    else:
        x_in = pair("x_in", 16 * H)
        y_done = take("y_done", S * G)
        rows_out = take("x3_out", S * G)
        stored = pair("stored", 16 * H)

    def sync(sp):
        def load(i, u):
            sp.wait_ge(turned[u].sem, turned[u].at(i * CH))
            for s in range(S):
                rows = ds(i * (2 * GROUP) + u * GROUP + s * P, P)
                sp.dma_start(z[u][:, s, :], dram["sum_gat"][rows, :])\
                    .then_inc(sum_in[u][s].sem, 16)
                if s >= 2:
                    sp.wait_ge(z_ready[u].sem, z_ready[u].at(i * S + s - 1))
                else:
                    sp.wait_ge(z_ready[1 - u].sem, z_ready[1 - u].at((i + u) * S))
                sp.dma_start(hrow[s % 2][:], h_dram[rows, :])\
                    .then_inc(h_in[s % 2].sem, 16)

        def load_x(i, u):
            sp.wait_ge(stored[u].sem, stored[u].at(i * 16))
            sp.dma_start(x[u], node_rows(dram["x2_biased"], i, u)).then_inc(x_in[u].sem, 16)

        def group(i, u, last):
            g = i * 2 + u
            if ahead(i, G):
                load(i + 1, u)
            if not first and not last:
                load_x(*following(i, u))
            if first:
                for s in range(S):
                    sp.wait_ge(wide_done.sem, wide_done.at(g * (2 * S) + 2 * s + 2))
                    sp.dma_start(dram["h2"][ds(i * (2 * GROUP) + u * GROUP + s * P, P), :], wide[s % 2][:])\
                        .then_inc(wide_stored[s % 2].sem, 16)
                sp.wait_ge(al_done.sem, al_done.at(g * S + S))
                sp.dma_start(node_rows(dram["al2"], i, u), al[u][:]).then_inc(al_stored[u].sem, 16)
            else:
                sp.wait_ge(rows_out.sem, rows_out.at(g * S + S))
                sp.dma_start(node_rows(dram["x3"], i, u), x[u]).then_inc(stored[u].sem, 16)

        load(0, 0)
        load(0, 1)
        if not first:
            load_x(0, 0)
        in_pairs(sp, G, group)
        if first:
            for u in range(2):
                sp.wait_ge(wide_stored[u].sem, wide_stored[u].at(16 * 2 * G))
                sp.wait_ge(al_stored[u].sem, al_stored[u].at(16 * H))
        else:
            for u in range(2):
                sp.wait_ge(stored[u].sem, stored[u].at(16 * H))

    def gpsimd(pool):
        g_ = nc.gpsimd

        def low_parts(i, u, chunks):
            g = i * 2 + u
            for k in chunks:
                pool.wait_ge(r_hi_done.sem, r_hi_done.at(g * CH + k + 1))
                g_.tensor_tensor(r_lo[:, u, k, :], r_f[k % 2][:], r_hi[:, u, k, :], ALU.subtract)\
                  .then_inc(r_lo_done.sem, 1)

        def group(i, u, last):
            g = i * 2 + u
            if not last:
                low_parts(*following(i, u), range(CH))
            if not first:
                norm.pool(pool, i, u)

        low_parts(0, 0, range(CH))
        in_pairs(pool, G, group)

    def vector(dve):
        v = nc.vector

        def combine(i, u, subtiles=range(S)):
            for s in subtiles:
                dve.wait_ge(sum_in[u][s].sem, sum_in[u][s].at(i * 16 + 16))
                w = h_in[s % 2]
                dve.wait_ge(w.sem, w.at(i * 64 + u * 32 + (s // 2) * 16 + 16))
                for h in range(K):
                    cols = slice(h * C, (h + 1) * C)
                    ins = v.scalar_tensor_tensor(out=z[u][:, s, cols], in0=hrow[s % 2][:, cols],
                                                 scalar=z[u][:, s, HC + h:HC + h + 1], in1=z[u][:, s, cols],
                                                 op0=ALU.mult, op1=ALU.add)
                ins.then_inc(z_ready[u].sem, 1)

        def group(i, u, last):
            g = i * 2 + u
            if first:
                if ahead(i, G):
                    combine(i + 1, u)
                dve.wait_ge(al_stored[u].sem, al_stored[u].at(i * 16))
                for s in range(S):
                    dve.wait_ge(al_prod.sem, al_prod.at(g * S + s + 1))
                    v.tensor_scalar(al[u][:, s, :], al_ps, UNSCALE, None, ALU.mult).then_inc(al_done.sem, 1)
                return
            dve.wait_ge(x_in[u].sem, x_in[u].at(i * 16 + 16))
            for s in range(S):
                if ahead(i, G):
                    combine(i + 1, u, (s,))
                dve.wait_ge(prod.sem, prod.at(g * S + s + 1))
                v.scalar_tensor_tensor(out=x[u][:, s, :], in0=mm[s][:], scalar=UNSCALE, in1=x[u][:, s, :],
                                       op0=ALU.mult, op1=ALU.add).then_inc(y_done.sem, 1)
                dve.wait_ge(y_done.sem, y_done.at(g * S + s + 1))
                norm.moments_of(dve, x[u][:, s, :], s, i, u)
            norm.apply(dve, x[u], x[u], i, u, rows_out)

        combine(0, 0)
        combine(0, 1)
        in_pairs(dve, G, group)

    def scalar(act):
        def parts(i, u, chunks):
            g = i * 2 + u
            for k in chunks:
                act.wait_ge(turned[u].sem, turned[u].at(i * CH + k + 1))
                act.wait_ge(r_lo_done.sem, r_lo_done.at(g * CH + (k - 1 if k >= 2 else 0)))
                act.activation(r_f[k % 2][:], tp[k % 4][:], ACT.Relu, scale=A_SCALE,
                               bias=kn.vec_scaled[:, bias + k:bias + k + 1]).then_inc(r_done.sem, 1)
                act.wait_ge(r_done.sem, r_done.at(g * CH + k + 1))
                act.copy(r_hi[:, u, k, :], r_f[k % 2][:]).then_inc(r_hi_done.sem, 1)

        def group(i, u, last):
            g = i * 2 + u
            for n in range(products):
                if not last:
                    parts(*following(i, u), turns[n])
                if first:
                    s, half = divmod(n, 2)
                    w = wide_stored[s % 2]
                    act.wait_ge(w.sem, w.at(g * 32 + (s // 2) * 16))
                    act.wait_ge(prod.sem, prod.at(g * products + n + 1))
                    act.activation(wide[s % 2][:, half * D:(half + 1) * D], mm[half][:], ACT.Copy, scale=UNSCALE)\
                       .then_inc(wide_done.sem, 1)

        parts(0, 0, range(CH))
        in_pairs(act, G, group)

    def tensor(pe):
        def turn(i, u, chunks):
            g = i * 2 + u
            pe.wait_ge(z_ready[u].sem, z_ready[u].at(i * S + S))
            for k in chunks:
                pe.wait_ge(r_done.sem, r_done.at(g * CH + k - 3))
                for s in range(S):
                    ins = pe.transpose(tp[k % 4][:, s * P:(s + 1) * P], z[u][:, s, k * P:(k + 1) * P], kn.ident[:])
                ins.then_inc(turned[u].sem, 1)

        def group(i, u, last):
            g = i * 2 + u
            pe.wait_ge(r_lo_done.sem, r_lo_done.at(g * CH + CH))
            for n in range(products):
                s, half = divmod(n, 2) if first else (n, 0)
                split = lambda k: (r_hi[:, u, k, s * P:(s + 1) * P], r_lo[:, u, k, s * P:(s + 1) * P])
                unit, width = (W_GAT2, HC) if first else (W_FC, D)
                if not last:
                    turn(*following(i, u), turns[n])
                if first:
                    pe.wait_ge(wide_done.sem, wide_done.at(g * (2 * S) + (n - 1 if s else 0)))
                else:
                    pe.wait_ge(y_done.sem, y_done.at((g - 1) * S + s + 1))
                split_product(pe, mm[half if first else s][:], split,
                              lambda k: (kn.weights(False, unit, k, half, width),
                                         kn.weights(True, unit, k, half, width)), CH).then_inc(prod.sem, 1)
                if first and half:
                    pe.wait_ge(al_done.sem, al_done.at(g * S + s))
                    split_product(pe, al_ps, split,
                                  lambda k: (kn.wa_hi[:, 4 + k, :], kn.wa_lo[:, 4 + k, :]), CH)\
                        .then_inc(al_prod.sem, 1)

        turn(0, 0, range(CH))
        in_pairs(pe, G, group)

    mem.close()
    return {"sync": sync, "gpsimd": gpsimd, "vector": vector, "scalar": scalar, "tensor": tensor}


def graph_layers_kernel(nc, nodes, edges, io):
    d = Dims(nodes, edges)
    dram = dict(io)

    def scratch(name, shape, dt=F32):
        dram[name] = nc.dram_tensor(name, shape, dt, kind="Internal").ap()

    scratch("sorted", (d.edge_rows + 1, 2), I32)
    scratch("sum", (d.padded, D))
    scratch("sum_gat", (d.padded, HC + HEADS))
    scratch("dinv", (d.padded, 1))
    for name in ("x1", "x2_biased", "x3"):
        scratch(name, (d.padded, D))
    for name in ("h1", "h2"):
        scratch(name, (d.padded, HC))
    for name in ("al1", "al2"):
        scratch(name, (d.padded, 2 * HEADS))
    scratch("h", (4, P, d.padded))

    with ExitStack() as ctx:
        kn = Kernel(nc, ctx, d, dram)
        ones = kn.ones
        kn.add(setup_stage(kn))
        with ExitStack() as mem:
            weights = plain_weights(kn, mem)
            kn.add(together(tiles_stage(kn), weights))
        with ExitStack() as mem:
            weights = attention_weights(kn, mem)
            kn.add(together(edge_sum_stage(kn, dram["x"], ones, ones), weights))
        kn.add(gin_stage(kn))
        kn.add(edge_sum_stage(kn, dram["x1"], ones, kn.mean_scale))
        kn.add(together(linear_stage(kn, "sage"), degree_stage(kn)))
        kn.add(norm_coefficients_stage(kn, V_SAGE_G, V_SAGE_BETA))
        kn.add(batch_norm_stage(kn, "sage"))
        kn.add(edge_attention_stage(kn, dram["h1"], dram["al1"]))
        kn.add(gat_stage(kn, 1))
        kn.add(edge_attention_stage(kn, dram["h2"], dram["al2"]))
        kn.add(gat_stage(kn, 2))
        kn.add(edge_sum_stage(kn, dram["x3"], kn.src_dinv, ones))
        kn.add(linear_stage(kn, "gcn"))
        kn.add(norm_coefficients_stage(kn, V_GCN_G, V_GCN_BETA))
        kn.add(batch_norm_stage(kn, "gcn"))
        kn.run()


def lay_out(inputs, d):
    import numpy as np

    x = np.asarray(inputs["x"])
    pad = np.zeros((d.padded - d.nodes, D), x.dtype)
    src, dst = np.asarray(inputs["src"]), np.asarray(inputs["dst"])
    more = d.edge_rows - d.edges
    src = np.concatenate([src, np.zeros(more, src.dtype)])
    dst = np.concatenate([dst, np.full(more, d.sent, dst.dtype)])

    def unit(w):
        k, n = w.shape
        per = 4 * D // n
        return w.reshape(k // P // per, per, P, n).transpose(0, 2, 1, 3).reshape(-1, P, 4 * D)

    weights = [np.asarray(inputs["L0_gnn_W1"]), np.asarray(inputs["L0_gnn_W2"]),
               np.asarray(inputs["L1_gnn_W_l"]).T, np.asarray(inputs["L1_gnn_W_r"]).T,
               np.asarray(inputs["L2_gnn_W1"]), np.asarray(inputs["L2_gnn_W2"]), np.asarray(inputs["L2_gnn_Wfc"]),
               np.asarray(inputs["L3_gnn_W"]).T]
    vectors = [np.asarray(inputs[n]).reshape(-1, P).T for n in (
        "L0_gnn_b1", "L1_gnn_b_l", "L1_gnn_gamma", "L1_gnn_beta", "L2_gnn_b1", "L2_gnn_b2",
        "L3_gnn_b", "L3_gnn_gamma", "L3_gnn_beta")]
    attention = np.stack([np.stack([np.asarray(inputs[f"L2_gnn_a_src{n}"]).reshape(-1),
                                    np.asarray(inputs[f"L2_gnn_a_dst{n}"]).reshape(-1)]) for n in (1, 2)])
    return {
        "x": np.concatenate([x, pad]),
        "dst": dst,
        "edges": np.stack([src, dst], axis=-1).reshape(d.edge_cols, P, 2).transpose(1, 0, 2),
        "weights": np.concatenate([unit(w) for w in weights]),
        "vectors": np.ascontiguousarray(np.concatenate(vectors, axis=1)),
        "attention": attention,
        "gin_b2": np.asarray(inputs["L0_gnn_b2"]),
        "fc_b": np.asarray(inputs["L2_gnn_bfc"]),
    }


def program(nc, inputs):
    import numpy as np

    nodes, edges = inputs["x"].shape[0], inputs["src"].shape[0]
    d = Dims(nodes, edges)
    arrays = {f"in_{n}": np.ascontiguousarray(a) for n, a in lay_out(inputs, d).items()}
    io = {n[3:]: nc.dram_tensor(n, a.shape, mybir.dt.from_np(a.dtype), kind="ExternalInput").ap()
          for n, a in arrays.items()}
    io["out"] = nc.dram_tensor("out", (d.padded, D), F32, kind="ExternalOutput").ap()
    graph_layers_kernel(nc, nodes, edges, io)
    return arrays


def kernel(**inputs):
    import concourse.bacc as bacc
    from concourse.bass_utils import run_bass_kernel_spmd

    nc = bacc.Bacc("TRN2", target_bir_lowering=False, num_devices=1)
    arrays = program(nc, inputs)
    return run_bass_kernel_spmd(nc, [arrays], core_ids=[0]).results[0]["out"][:inputs["x"].shape[0]]
```

```python
from contextlib import ExitStack

import concourse.bass as bass
from concourse import mybir

F32 = mybir.dt.float32
F16 = mybir.dt.float16
I32 = mybir.dt.int32
ALU = mybir.AluOpType
ACT = mybir.ActivationFunctionType
AX = mybir.AxisListType
ds = bass.ds

P = 128
D = 512
HC = 1024
HEADS = 4
C = HC // HEADS
S = 4
GROUP = S * P
EDGES = P - 1
EPS = 1e-5
SLOPE = 0.2
A_SCALE = 16.0
GIN_SCALE = 2.0
W_SCALE = 256.0
UNSCALE = 1.0 / (A_SCALE * W_SCALE)
GIN_UNSCALE = 1.0 / (GIN_SCALE * W_SCALE)
FAR = 20000
LOGITS = 2 * HEADS
GAT_ROW = LOGITS + HC
THIRDS = 3
THIRD = GAT_ROW // THIRDS
BIG = 1e30
START = 8
CARRY_IN = (0, 96)
CARRY_OUT = (96, 0)

W_GIN1, W_GIN2, W_SAGE_L, W_SAGE_R, W_GAT1, W_GAT2, W_FC, W_GCN = 0, 1, 2, 3, 4, 6, 10, 12
UNITS = 13
GAT_CHUNKS = 2 * (W_FC - W_GAT1)
V_GIN_B1, V_SAGE_B, V_SAGE_G, V_SAGE_BETA, V_GAT1_B, V_GAT2_B, V_GCN_B, V_GCN_G, V_GCN_BETA = (
    0, 4, 8, 12, 16, 24, 32, 36, 40)
VECTORS = 44


ENGINES = ("sync", "gpsimd", "scalar", "vector", "tensor")


class Dims:
    def __init__(self, nodes, edges):
        self.nodes = nodes
        self.edges = edges
        self.groups = -(-nodes // (2 * GROUP)) * 2
        self.padded = self.groups * GROUP
        self.sent = self.padded - 1
        self.edge_cols = -(-(edges + 1) // P)
        self.edge_rows = self.edge_cols * P
        self.tiles = -(-edges // (8 * EDGES)) * 8
        self.last_real = nodes - (self.groups - 1) * GROUP
        assert self.sent >= nodes and 0 < self.last_real <= GROUP
        assert self.tiles * EDGES + 2 <= self.edge_rows + 1
        assert self.padded * self.edge_cols < 1 << 24


class Signal:

    def __init__(self, sem, base):
        self.sem, self.base = sem, base

    def at(self, n):
        return self.base + n


class Signals:

    def __init__(self, nc, ctx):
        self.nc, self.ctx, self.sems, self.total, self.raised = nc, ctx, {}, {}, []

    def take(self, name, total, software=False):
        if name not in self.sems:
            self.sems[name] = self.ctx.enter_context(self.nc.semaphore(name))
            self.total[name] = 0 if software else START
            if not software:
                self.raised.append(self.sems[name])
        s = Signal(self.sems[name], self.total[name])
        self.total[name] += total
        return s

    def raise_all(self, eng, which):
        for sem in self.raised[which::5]:
            eng.sem_inc(sem, START)

    def pair(self, name, total, software=False):
        return [self.take(f"{name}{u}", total, software) for u in range(2)]

    def several(self, n, name, total, software=False):
        return [self.take(f"{name}{v}", total, software) for v in range(n)]


class Steps:

    def __init__(self, sig):
        self.sig, self.first, self.n = sig, 0, 0

    def begin(self, first):
        self.first, self.n = first, 0

    def mark(self, ins):
        ins.then_inc(self.sig.sem, 1)
        self.n += 1
        return self.sig.at(self.first + self.n)


def settle(eng, kn):
    eng.sem_inc(kn.passed, 1)


def in_pairs(eng, n, body):
    if n > 2:
        with eng.Fori(0, n // 2 - 1) as i:
            for u in range(2):
                body(i, u, False)
    body(n // 2 - 1, 0, False)
    body(n // 2 - 1, 1, True)


def ahead(i, n):
    return not (isinstance(i, int) and i == n // 2 - 1)


def following(i, u):
    return i + u, 1 - u


def in_runs(eng, n, width, body):
    if n > width:
        with eng.Fori(0, n // width - 1) as i:
            for v in range(width):
                body(i, v, width)
    for v in range(width):
        body(n // width - 1, v, width - 1 - v)


def after(i, v, by, width):
    return i + (v + by) // width, (v + by) % width


def in_two(i, v, width):
    return i * (width // 2) + v // 2, v % 2


class Kernel:
    def __init__(self, nc, ctx, dims, dram):
        self.nc, self.ctx, self.d, self.dram = nc, ctx, dims, dram
        self.sig = Signals(nc, ctx)
        self.stages = []
        self.meet = ctx.enter_context(nc.semaphore("meet"))
        self.passed = ctx.enter_context(nc.semaphore("passed"))
        self.buffers = 0
        d = dims

        def sb(name, shape, dt):
            return ctx.enter_context(nc.sbuf_tensor(name, shape, dt))

        self.ident = sb("ident", [P, P], F32)
        self.ones = sb("ones", [P, P], F32)
        self.w_hi = sb("w_hi", [P, UNITS * 4 * D + GAT_CHUNKS * LOGITS], F16)
        self.w_lo = sb("w_lo", [P, UNITS * 4 * D + GAT_CHUNKS * LOGITS], F16)
        self.vec = sb("vec", [P, VECTORS], F32)
        self.vec_scaled = sb("vec_scaled", [P, VECTORS], F32)
        self.gin_b2 = sb("gin_b2", [P, D], F32)
        self.fc_b = sb("fc_b", [P, D], F32)
        self.same = sb("same", [P, d.tiles * P], F16)
        self.dst_f = sb("dst_f", [P, d.tiles], F32)
        self.src_i = sb("src_i", [P, d.tiles], I32)
        self.dst_logits_i = sb("dst_logits_i", [P, d.tiles], I32)
        self.final_i = sb("final_i", [P, d.tiles], I32)
        self.count = sb("count", [P, d.tiles], F32)
        self.mean_scale = sb("mean_scale", [P, d.tiles], F32)
        self.degree = sb("degree", [P, d.tiles], F32)
        self.dinv = sb("dinv_sb", [P, d.tiles], F32)
        self.src_dinv = sb("src_dinv", [P, d.tiles], F32)
        self.bn_scale = sb("bn_scale", [P, 4], F32)
        self.bn_shift = sb("bn_shift", [P, 4], F32)
        self.bn_stats = sb("bn_stats", [P, 4, 2 * 6 * (d.groups // 2)], F32)
        self.minus_half = sb("minus_half", [P, d.tiles], F32)
        self.eps = sb("eps", [P, S], F32)
        self.bank = [ctx.enter_context(nc.psum_tensor(f"bank{n}", [P, D], F32)) for n in range(8)]

    def unit_at(self, unit):
        return unit * 4 * D + LOGITS * min(max(2 * (unit - W_GAT1), 0), GAT_CHUNKS)

    def unit(self, lo, unit):
        w = self.w_lo if lo else self.w_hi
        at = self.unit_at(unit)
        if W_GAT1 <= unit < W_FC:
            return w[:, at:at + 2 * GAT_ROW].rearrange("p (k c) -> p k c", c=GAT_ROW)[:, :, LOGITS:]
        return w[:, at:at + 4 * D].rearrange("p (k c) -> p k c", k=1)

    def weights(self, lo, unit, k):
        w = self.w_lo if lo else self.w_hi
        at = self.unit_at(unit) + k * D
        return w[:, at:at + D]

    def gat_weights(self, lo, unit, k, third):
        w = self.w_lo if lo else self.w_hi
        at = self.unit_at(unit) + k * GAT_ROW + third * THIRD
        return w[:, at:at + THIRD]

    def logit_weights(self, lo):
        w = self.w_lo if lo else self.w_hi
        at = self.unit_at(W_GAT1)
        return w[:, at:at + GAT_CHUNKS * GAT_ROW].rearrange("p (k c) -> p k c", c=GAT_ROW)[:, :, 0:LOGITS]

    def buffer(self, mem, name, shape, dt):
        self.buffers += 1
        return mem.enter_context(self.nc.sbuf_tensor(f"{name}_{self.buffers}", shape, dt))

    def add(self, stage):
        self.stages.append(stage)

    def run(self):
        nc = self.nc
        meet = self.meet
        block = self.ctx.enter_context(nc.Block())
        stages = self.stages

        def program(eng, which):
            self.sig.raise_all(eng, ENGINES.index(which))
            eng.drain().then_inc(meet, 1)
            eng.wait_ge(meet, 5)
            for n, stage in enumerate(stages):
                if which in stage:
                    stage[which](eng)
                eng.drain().then_inc(meet, 1)
                eng.wait_ge(meet, 5 * (n + 2))

        @block.sync
        def _(sp):
            program(sp, "sync")

        @block.gpsimd
        def _(pool):
            program(pool, "gpsimd")

        @block.scalar
        def _(act):
            program(act, "scalar")

        @block.vector
        def _(dve):
            program(dve, "vector")

        @block.tensor
        def _(pe):
            program(pe, "tensor")


def split_product(pe, out, stationary, moving, chunks, before=None):
    for k in range(chunks):
        if before:
            before(k)
        s_hi, s_lo = stationary(k)
        m_hi, m_lo = moving(k)
        last = k == chunks - 1
        pe.matmul(out, s_lo, m_hi, start=(k == 0), stop=False)
        pe.matmul(out, s_hi, m_lo, start=False, stop=False)
        mm = pe.matmul(out, s_hi, m_hi, start=False, stop=last)
    return mm


def together(*stages):
    def programs(which):
        def run(eng):
            for stage in stages:
                if which in stage:
                    stage[which](eng)
        return run

    return {which: programs(which) for which in ENGINES}


def setup_stage(kn):
    nc, d, dram, take = kn.nc, kn.d, kn.dram, kn.sig.take
    J = d.edge_cols
    JV = -(-J * 3 // 7)
    mem = ExitStack()

    def sb(name, shape, dt):
        return kn.buffer(mem, name, shape, dt)

    blank = sb("blank", [P, D], F32)
    dst_row = sb("dst_row", [P, J * P], I32)
    key_row = sb("key_row", [P, J * P], F32)
    junk = [dst_row[:, u * (J * P // 2):(u + 1) * (J * P // 2)].bitcast(F16) for u in range(2)]
    pairs = sb("pairs", [P, J, 2], I32)
    key_col = sb("key_col", [P, J], F32)
    key_half = sb("key_half", [P, J], F32)
    j_col = sb("j_col", [P, J], F32)
    before = sb("before", [P, P], F32)
    junk2 = sb("junk2", [P, P], F16)
    less = sb("less", [P, J], F32)
    tied = sb("tied", [P, J], F32)
    signs = sb("signs", [P, J], F32)
    place = sb("place", [P, J], I32)
    sentinel = sb("sentinel", [1, 2], I32)

    small_in = take("small_in", 16 * 3)
    dst_in = take("dst_in", 16)
    pairs_in = take("pairs_in", 16)
    blank_ready = take("blank_ready", 1)
    zeroed = take("zeroed", 16 * (d.groups + 1))
    pool_steps = Steps(take("pool_steps", 10))
    keys = take("keys", 3)
    ties = take("ties", J)
    counted = take("counted", JV)
    placed = take("placed", 2 * J + (J - JV))
    sign_steps = take("sign_steps", J - JV)
    vec_done = take("vec_done", 2)
    sorted_out = take("sorted_out", 16 * (J - 1), software=True)
    sorted_first = kn.sig.pair("scattered", 16, software=True)

    def sync(sp):
        sp.dma_start(dst_row[:], dram["dst"].partition_broadcast(P)).then_inc(dst_in.sem, 16)
        sp.dma_start(pairs[:], dram["edges"]).then_inc(pairs_in.sem, 16)
        sp.dma_start(kn.vec[:], dram["vectors"]).then_inc(small_in.sem, 16)
        sp.dma_start(kn.gin_b2[:], dram["gin_b2"].partition_broadcast(P)).then_inc(small_in.sem, 16)
        sp.dma_start(kn.fc_b[:], dram["fc_b"].partition_broadcast(P)).then_inc(small_in.sem, 16)
        sp.wait_ge(blank_ready.sem, blank_ready.at(1))
        rows = d.padded // P
        per = rows // d.groups
        thin = dram["sum"].rearrange("(p r) c -> p r c", r=rows)
        for g in range(d.groups):
            sp.dma_start(thin[:, g * per:(g + 1) * per, :],
                         blank[:].unsqueeze(1).broadcast_to([P, per, D])).then_inc(zeroed.sem, 16)
        sp.dma_start(dram["dinv"].rearrange("(p r) c -> p (r c)", p=P), kn.ones[:, 0:rows]).then_inc(zeroed.sem, 16)
        sp.wait_ge(zeroed.sem, zeroed.at(16 * (d.groups + 1)))

    def gpsimd(pool):
        st = pool_steps
        st.begin(0)
        g = nc.gpsimd
        st.mark(g.memset(kn.ones[:], 1.0))
        st.mark(g.memset(kn.ident[:], 0.0))
        g.memset(kn.eps[:], EPS)
        b = st.mark(g.memset(kn.minus_half[:], -0.5))
        pool.wait_ge(st.sig.sem, b)
        g.memset(blank[:], 0.0).then_inc(blank_ready.sem, 1)
        st.mark(g.iota(key_row[:].rearrange("p (j q) -> p j q", q=P), [[1, J], [0, P]], base=0,
                       channel_multiplier=0, allow_small_or_imprecise_dtypes=True))
        st.mark(g.iota(j_col[:], [[1, J]], base=0, channel_multiplier=0,
                       allow_small_or_imprecise_dtypes=True))
        st.mark(g.affine_select(out=before[:], in_=kn.ones[:], compare_op=ALU.is_ge, fill=0.0,
                                base=0, pattern=[[-1, P]], channel_multiplier=1))
        st.mark(g.affine_select(out=kn.ident[:], in_=kn.ident[:], compare_op=ALU.not_equal, fill=1.0,
                                base=0, pattern=[[-1, P]], channel_multiplier=1))
        st.mark(g.memset(sentinel[:, 0:1], 0))
        st.mark(g.memset(sentinel[:, 1:2], d.sent))
        n = st.mark(g.memset(kn.src_dinv[:], 1.0))
        pool.wait_ge(st.sig.sem, n)
        pool.dma_start(dram["sorted"][0:1, :], sentinel[:]).then_inc(sorted_out.sem, 16)
        pool.wait_ge(small_in.sem, small_in.at(48))
        pool.wait_ge(pairs_in.sem, pairs_in.at(16))
        pool.wait_ge(ties.sem, ties.at(J))
        columns = [j for pair in zip(range(JV), range(JV, J)) for j in pair] + list(range(2 * JV, J))
        done = 0
        for j in columns:
            if j < JV:
                pool.wait_ge(counted.sem, counted.at(j + 1))
            else:
                pool.wait_ge(sign_steps.sem, sign_steps.at(j - JV + 1))
                g.tensor_scalar(less[:, j:j + 1], signs[:, j:j + 1], float(J * P), 0.5, ALU.add, ALU.mult)\
                 .then_inc(placed.sem, 1)
                done += 1
                pool.wait_ge(placed.sem, placed.at(done))
            g.tensor_tensor(less[:, j:j + 1], less[:, j:j + 1], tied[:, j:j + 1], ALU.add).then_inc(placed.sem, 1)
            done += 1
            pool.wait_ge(placed.sem, placed.at(done))
            g.tensor_copy(place[:, j:j + 1], less[:, j:j + 1]).then_inc(placed.sem, 1)
            done += 1
            pool.wait_ge(placed.sem, placed.at(done))
            pool.indirect_dma_start(dram["sorted"], bass.IndirectOffsetOnAxis(ap=place[:, j:j + 1], axis=0),
                                    pairs[:, j, :], None)\
                .then_inc((sorted_first[j] if j < 2 else sorted_out).sem, 16)
        pool.wait_ge(sorted_out.sem, sorted_out.at(16 * (J - 1)))
        for first in sorted_first:
            pool.wait_ge(first.sem, first.at(16))

    def scalar(act):
        act.wait_ge(keys.sem, keys.at(3))
        with act.Fori(0, J - JV) as j:
            act.wait_ge(sign_steps.sem, sign_steps.at(j))
            settle(act, kn)
            act.activation(junk[1], key_row[:], ACT.Sign, scale=-1.0, bias=key_half[:, ds(j + JV, 1)],
                           accum_out=signs[:, ds(j + JV, 1)]).then_inc(sign_steps.sem, 1)
        act.wait_ge(small_in.sem, small_in.at(48))
        act.mul(kn.vec_scaled[:, 0:V_GIN_B1 + 4], kn.vec[:, 0:V_GIN_B1 + 4], GIN_SCALE).then_inc(vec_done.sem, 1)
        act.mul(kn.vec_scaled[:, V_GIN_B1 + 4:], kn.vec[:, V_GIN_B1 + 4:], A_SCALE).then_inc(vec_done.sem, 1)

    def vector(dve):
        v = nc.vector
        dve.wait_ge(pool_steps.sig.sem, pool_steps.sig.at(6))
        dve.wait_ge(dst_in.sem, dst_in.at(16))
        dve.wait_ge(pairs_in.sem, pairs_in.at(16))
        v.scalar_tensor_tensor(out=key_row[:], in0=dst_row[:], scalar=float(J), in1=key_row[:],
                               op0=ALU.mult, op1=ALU.add).then_inc(keys.sem, 1)
        v.scalar_tensor_tensor(out=key_col[:], in0=pairs[:, :, 1], scalar=float(J), in1=j_col[:],
                               op0=ALU.mult, op1=ALU.add).then_inc(keys.sem, 1)
        dve.wait_ge(keys.sem, keys.at(2))
        v.tensor_scalar(key_half[:], key_col[:], -0.5, None, ALU.add).then_inc(keys.sem, 1)
        with dve.Fori(0, J) as j:
            dve.wait_ge(ties.sem, ties.at(j))
            v.scalar_tensor_tensor(out=junk2[:], in0=key_row[:, ds(j * P, P)], scalar=key_col[:, ds(j, 1)],
                                   in1=before[:], op0=ALU.is_equal, op1=ALU.mult,
                                   accum_out=tied[:, ds(j, 1)]).then_inc(ties.sem, 1)
        with dve.Fori(0, JV) as j:
            dve.wait_ge(counted.sem, counted.at(j))
            v.tensor_scalar(junk[0], key_row[:], key_col[:, ds(j, 1)], None, ALU.is_lt, ALU.add,
                            accum_out=less[:, ds(j, 1)]).then_inc(counted.sem, 1)
        v.memset(kn.bn_stats[:], 0.0)

    mem.close()
    return {"sync": sync, "gpsimd": gpsimd, "scalar": scalar, "vector": vector}


def plain_weights(kn, mem):
    nc, dram, take = kn.nc, kn.dram, kn.sig.take
    units = [n for n in range(UNITS) if not W_GAT1 <= n < W_FC]
    stage_w = [kn.buffer(mem, f"p_stage{u}", [P, 4 * D], F32) for u in range(2)]
    w_in = [take("w_in0", 16 * 4), take("w_in1", 16 * 3)]
    scaled = take("w_scaled", len(units))
    hi_done = take("w_hi_done", len(units))
    lo_done = take("w_lo_done", len(units))

    def sync(sp):
        for n, unit in enumerate(units):
            if n >= 2:
                sp.wait_ge(lo_done.sem, lo_done.at(n - 1))
            sp.dma_start(stage_w[n % 2][:], dram["weights"][unit]).then_inc(w_in[n % 2].sem, 16)

    def scalar(act):
        for n, unit in enumerate(units):
            w = stage_w[n % 2]
            act.wait_ge(w_in[n % 2].sem, w_in[n % 2].at(16 * (n // 2 + 1)))
            act.mul(w[:], w[:], W_SCALE).then_inc(scaled.sem, 1)
            act.wait_ge(scaled.sem, scaled.at(n + 1))
            act.copy(kn.unit(False, unit)[:, 0, :], w[:]).then_inc(hi_done.sem, 1)

    def gpsimd(pool):
        for n, unit in enumerate(units):
            pool.wait_ge(hi_done.sem, hi_done.at(n + 1))
            nc.gpsimd.tensor_tensor(kn.unit(True, unit)[:, 0, :], stage_w[n % 2][:], kn.unit(False, unit)[:, 0, :],
                                    ALU.subtract)\
                .then_inc(lo_done.sem, 1)

    return {"sync": sync, "scalar": scalar, "gpsimd": gpsimd}


def attention_weights(kn, mem):
    nc, dram, take = kn.nc, kn.dram, kn.sig.take
    units = list(range(W_GAT1, W_FC))
    stage_w = [kn.buffer(mem, f"f_stage{u}", [P, 4 * D], F32) for u in range(2)]
    a_rows = kn.buffer(mem, "a_rows", [P, 2, HC], F32)
    prod = kn.buffer(mem, "f_prod", [P, HC], F32)
    wa = kn.buffer(mem, "f_wa", [P, GAT_CHUNKS, 2 * HEADS], F32)
    a_in = [take(f"a_in{n}", 16) for n in range(2)]
    w_in = [take(f"w_in{n}", 16 * 3) for n in range(2)]
    w_hi_done = take("w_hi_done", len(units))
    w_done = take("w_lo_done", len(units))
    wa_read = take("wa_read", 4 * len(units))
    wa_done = take("wa_done", 4 * len(units) + 2)

    def sync(sp):
        sp.dma_start(a_rows[:], dram["attention"][0].partition_broadcast(P)).then_inc(a_in[0].sem, 16)
        for n, unit in enumerate(units):
            if n >= 2:
                sp.wait_ge(w_done.sem, w_done.at(n - 1))
                sp.wait_ge(wa_read.sem, wa_read.at(4 * (n - 1)))
            if unit == W_GAT2:
                sp.wait_ge(wa_read.sem, wa_read.at(4 * n))
                sp.dma_start(a_rows[:], dram["attention"][1].partition_broadcast(P)).then_inc(a_in[1].sem, 16)
            sp.dma_start(stage_w[n % 2][:], dram["weights"][unit]).then_inc(w_in[n % 2].sem, 16)

    def vector(dve):
        v = nc.vector
        done = 0
        for n, unit in enumerate(units):
            layer = 0 if unit < W_GAT2 else 1
            dve.wait_ge(w_in[n % 2].sem, w_in[n % 2].at(16 * (n // 2 + 1)))
            rows = stage_w[n % 2][:].rearrange("p (k c) -> p k c", c=HC)
            v.tensor_scalar(kn.unit(False, unit), rows, W_SCALE, None, ALU.mult)\
                .then_inc(w_hi_done.sem, 1)
            dve.wait_ge(w_hi_done.sem, w_hi_done.at(n + 1))
            v.scalar_tensor_tensor(out=kn.unit(True, unit), in0=rows, scalar=W_SCALE,
                                   in1=kn.unit(False, unit), op0=ALU.mult, op1=ALU.subtract)\
                .then_inc(w_done.sem, 1)
            dve.wait_ge(a_in[layer].sem, a_in[layer].at(16))
            for half in range(2):
                w = stage_w[n % 2][:, half * HC:(half + 1) * HC]
                for side in range(2):
                    dve.wait_ge(wa_done.sem, wa_done.at(done))
                    v.tensor_tensor(prod[:], w, a_rows[:, side, :], ALU.mult).then_inc(wa_read.sem, 1)
                    done += 1
                    dve.wait_ge(wa_read.sem, wa_read.at(done))
                    v.tensor_reduce(wa[:, 2 * n + half, side * HEADS:(side + 1) * HEADS],
                                    prod[:].rearrange("p (h c) -> p h c", h=HEADS), AX.X, ALU.add)\
                        .then_inc(wa_done.sem, 1)
        dve.wait_ge(wa_done.sem, wa_done.at(done))
        v.tensor_scalar(kn.logit_weights(False), wa[:], W_SCALE, None, ALU.mult).then_inc(wa_done.sem, 1)
        dve.wait_ge(wa_done.sem, wa_done.at(done + 1))
        v.scalar_tensor_tensor(out=kn.logit_weights(True), in0=wa[:], scalar=W_SCALE, in1=kn.logit_weights(False),
                               op0=ALU.mult, op1=ALU.subtract).then_inc(wa_done.sem, 1)

    return {"sync": sync, "vector": vector}


def tiles_stage(kn):
    nc, d, dram, take = kn.nc, kn.d, kn.dram, kn.sig.take
    T = d.tiles
    mem = ExitStack()

    def sb(name, shape, dt):
        return kn.buffer(mem, name, shape, dt)

    rec = sb("rec", [P, T, 4], I32)
    equal_next = sb("equal_next", [P, T], F32)
    next_f = sb("next_f", [P, T], F32)
    spread = [sb(f"spread{u}", [P, P], F32) for u in range(2)]
    same_f = [sb(f"same_f{u}", [P, P], F32) for u in range(2)]
    one = [sb(f"one{u}", [P, 1], F32) for u in range(2)]
    tmp = sb("tmp", [P, T], F32)
    row_ps = [kn.bank[u][:, 0:P] for u in range(2)]
    count_ps = [kn.bank[2 + u][:, 0:1] for u in range(2)]

    rec_in = take("rec_in", 16 * 6)
    cols = take("cols", 9)
    spread_done = kn.sig.pair("spread_done", T // 2)
    row_done = kn.sig.pair("row_done", T // 2)
    same_done = kn.sig.pair("same_done", T // 2)
    same_f_done = kn.sig.pair("same_f_done", T // 2)
    count_done = kn.sig.pair("count_done", T // 2)
    carried = kn.sig.pair("carried", T // 2)
    counts = take("counts", T)
    ends = take("ends", 3)

    def rows(first, partitions, step, n):
        base = dram["sorted"]
        return bass.AP(base.tensor, base.offset + 2 * first, [[2, partitions], [2 * step, n], [1, 4]])

    def sync(sp):
        sp.dma_start(rec[1:96], rows(1, 95, EDGES, T)).then_inc(rec_in.sem, 16)
        sp.dma_start(rec[97:128], rows(96, 31, EDGES, T)).then_inc(rec_in.sem, 16)
        for u in range(2):
            for p, first in ((CARRY_IN[u], u * EDGES), (CARRY_OUT[u], (u + 1) * EDGES)):
                sp.dma_start(rec[p:p + 1, u:T:2, :], rows(first, 1, 2 * EDGES, T // 2)).then_inc(rec_in.sem, 16)

    def vector(dve):
        v = nc.vector
        dve.wait_ge(rec_in.sem, rec_in.at(16 * 6))
        v.tensor_copy(kn.dst_f[:], rec[:, :, 1]).then_inc(cols.sem, 1)
        v.tensor_copy(next_f[:], rec[:, :, 3]).then_inc(cols.sem, 1)
        v.tensor_copy(kn.src_i[:], rec[:, :, 0]).then_inc(cols.sem, 1)
        v.tensor_scalar(kn.dst_logits_i[:], rec[:, :, 1], float(GAT_ROW // LOGITS), None, ALU.mult)\
            .then_inc(cols.sem, 1)
        dve.wait_ge(cols.sem, cols.at(2))
        v.tensor_tensor(equal_next[:], kn.dst_f[:], next_f[:], ALU.is_equal).then_inc(cols.sem, 1)
        dve.wait_ge(cols.sem, cols.at(5))
        v.scalar_tensor_tensor(out=kn.final_i[:], in0=equal_next[:], scalar=float(FAR), in1=kn.dst_f[:],
                               op0=ALU.mult, op1=ALU.add).then_inc(cols.sem, 1)
        dve.wait_ge(cols.sem, cols.at(6))
        for u in range(2):
            v.memset(kn.final_i[CARRY_IN[u]:CARRY_IN[u] + 1, u:T:2], FAR).then_inc(cols.sem, 1)
        for u in range(2):
            ins = v.memset(one[u][:], 1.0)
        ins.then_inc(cols.sem, 1)
        dve.wait_ge(cols.sem, cols.at(9))

        def spread_out(i, u):
            v.tensor_scalar(spread[u][:], kn.ones[:], kn.dst_f[:, ds(i * 2 + u, 1)], None, ALU.mult)\
                .then_inc(spread_done[u].sem, 1)

        def compare(i, u):
            t = i * 2 + u
            dve.wait_ge(row_done[u].sem, row_done[u].at(i + 1))
            v.tensor_scalar(same_f[u][:], row_ps[u], kn.dst_f[:, ds(t, 1)], None, ALU.is_equal)\
                .then_inc(same_f_done[u].sem, 1)
            v.tensor_scalar(kn.same[:, ds(t * P, P)], row_ps[u], kn.dst_f[:, ds(t, 1)], None, ALU.is_equal)\
                .then_inc(same_done[u].sem, 1)

        def tile(i, u, last):
            c = CARRY_OUT[u]
            if not last:
                compare(*following(i, u))
            if ahead(i, T):
                spread_out(i + 1, u)
            dve.wait_ge(count_done[u].sem, count_done[u].at(i + 1))
            v.tensor_copy(one[1 - u][c:c + 1, :], count_ps[u][c:c + 1, :]).then_inc(carried[u].sem, 1)
            v.tensor_copy(kn.count[:, ds(i * 2 + u, 1)], count_ps[u]).then_inc(counts.sem, 1)

        spread_out(0, 0)
        spread_out(0, 1)
        compare(0, 0)
        in_pairs(dve, T, tile)
        dve.wait_ge(counts.sem, counts.at(T))
        v.tensor_scalar(tmp[:], kn.count[:], 1.0, None, ALU.max).then_inc(ends.sem, 1)
        v.tensor_scalar(kn.degree[:], kn.count[:], 1.0, None, ALU.add).then_inc(ends.sem, 1)
        dve.wait_ge(ends.sem, ends.at(1))
        v.reciprocal(kn.mean_scale[:], tmp[:]).then_inc(ends.sem, 1)

    def tensor(pe):
        def row(i, u):
            pe.wait_ge(spread_done[u].sem, spread_done[u].at(i + 1))
            pe.wait_ge(same_done[u].sem, same_done[u].at(i))
            pe.matmul(row_ps[u], spread[u][:], kn.ident[:], start=True, stop=True).then_inc(row_done[u].sem, 1)

        def tile(i, u, last):
            pe.wait_ge(same_f_done[u].sem, same_f_done[u].at(i + 1))
            pe.wait_ge(carried[1 - u].sem, carried[1 - u].at(i + u))
            pe.wait_ge(counts.sem, counts.at(i * 2))
            pe.matmul(count_ps[u], same_f[u][:], one[u][:], start=True, stop=True).then_inc(count_done[u].sem, 1)
            if ahead(i, T):
                row(i + 1, u)

        row(0, 0)
        row(0, 1)
        in_pairs(pe, T, tile)

    mem.close()
    return {"sync": sync, "vector": vector, "tensor": tensor}


def edge_sum_stage(kn, rows_dram, in_scale, out_scale):
    nc, d, dram, take, pair = kn.nc, kn.d, kn.dram, kn.sig.take, kn.sig.pair
    T, H = d.tiles, d.tiles // 2
    W = 4
    AHEAD = 3
    mem = ExitStack()

    def several(n, name, shape, dt):
        return [kn.buffer(mem, f"{name}{u}", shape, dt) for u in range(n)]

    rows = several(W, "e_rows", [P, D], F32)
    gather_at = several(W, "e_gather_at", [P, 1], I32)
    lhs = several(2, "e_lhs", [P, P], F32)
    out = several(2, "e_out", [P, D], F32)
    final_at = several(2, "e_final_at", [P, 1], I32)
    halves = [slice(0, D // 2), slice(D // 2, D)]
    total = [[kn.bank[2 * u + half][:, 0:D // 2] for half in range(2)] for u in range(2)]

    indexed = take("indexed", 2 * T)
    gathered = kn.sig.several(W, "gathered", 16 * (T // W), software=True)
    scattered = pair("scattered", 16 * H, software=True)
    lhs_ready = pair("lhs_ready", H)
    carried = [pair(f"carried{half}_", H) for half in range(2)]
    summed = [pair(f"summed{half}_", H) for half in range(2)]
    evacuated = pair("evacuated", 2 * H)
    start = take("start", 2)

    def gpsimd(pool):
        g = nc.gpsimd

        def gather(i, v, n):
            j, u = in_two(i, v, W)
            if not (isinstance(i, int) and i == 0):
                pool.wait_ge(summed[1][u].sem, summed[1][u].at(j + 1 - W // 2))
            g.tensor_copy(gather_at[v][:], kn.src_i[:, ds(i * W + v, 1)]).then_inc(indexed.sem, 1)
            pool.wait_ge(indexed.sem, indexed.at(n))
            settle(pool, kn)
            pool.indirect_dma_start(rows[v][:], None, rows_dram,
                                    bass.IndirectOffsetOnAxis(ap=gather_at[v][:], axis=0),
                                    bounds_check=d.padded - 1, oob_is_err=False)\
                .then_inc(gathered[v].sem, 16)

        def tile(i, v, left):
            t = i * W + v
            j, u = in_two(i, v, W)
            n = t + 1 + AHEAD + t if left >= AHEAD else T + t
            if left >= AHEAD:
                gather(*after(i, v, AHEAD, W), n)
            pool.wait_ge(scattered[u].sem, scattered[u].at(j * 16))
            g.tensor_copy(final_at[u][:], kn.final_i[:, ds(t, 1)]).then_inc(indexed.sem, 1)
            pool.wait_ge(indexed.sem, indexed.at(n + 1))
            pool.wait_ge(evacuated[u].sem, evacuated[u].at(j * 2 + 2))
            settle(pool, kn)
            pool.indirect_dma_start(dram["sum"], bass.IndirectOffsetOnAxis(ap=final_at[u][:], axis=0),
                                    out[u][:], None, bounds_check=d.nodes - 1, oob_is_err=False)\
                .then_inc(scattered[u].sem, 16)

        for v in range(AHEAD):
            gather(0, v, v + 1)
        in_runs(pool, T, W, tile)
        for u in range(2):
            pool.wait_ge(scattered[u].sem, scattered[u].at(16 * H))

    def vector(dve):
        for half in range(2):
            nc.vector.memset(total[1][half][0:1, :], 0.0).then_inc(start.sem, 1)

    def scalar(act):
        act.wait_ge(start.sem, start.at(2))

        def matrix_and_carry(i, v):
            t = i * W + v
            j, u = in_two(i, v, W)
            c = CARRY_IN[u]
            act.wait_ge(summed[1][u].sem, summed[1][u].at(j))
            settle(act, kn)
            act.activation(lhs[u][:], kn.same[:, ds(t * P, P)], ACT.Copy, scale=in_scale[:, ds(t, 1)])\
               .then_inc(lhs_ready[u].sem, 1)
            act.wait_ge(gathered[v].sem, gathered[v].at(i * 16 + 16))
            for half in range(2):
                act.wait_ge(summed[half][1 - u].sem, summed[half][1 - u].at(j + u))
                act.copy(rows[v][c:c + 1, halves[half]], total[1 - u][half][c:c + 1, :])\
                   .then_inc(carried[half][u].sem, 1)

        def tile(i, v, left):
            j, u = in_two(i, v, W)
            if left:
                matrix_and_carry(*after(i, v, 1, W))
            act.wait_ge(scattered[u].sem, scattered[u].at(j * 16))
            for half in range(2):
                act.wait_ge(summed[half][u].sem, summed[half][u].at(j + 1))
                settle(act, kn)
                act.activation(out[u][:, halves[half]], total[u][half], ACT.Copy,
                               scale=out_scale[:, ds(i * W + v, 1)]).then_inc(evacuated[u].sem, 1)

        matrix_and_carry(0, 0)
        in_runs(act, T, W, tile)

    def tensor(pe):
        def tile(i, v, left):
            j, u = in_two(i, v, W)
            pe.wait_ge(lhs_ready[u].sem, lhs_ready[u].at(j + 1))
            for half in range(2):
                pe.wait_ge(carried[half][u].sem, carried[half][u].at(j + 1))
                pe.wait_ge(evacuated[u].sem, evacuated[u].at(j * 2 - 1 + half))
                pe.matmul(total[u][half], lhs[u][:], rows[v][:, halves[half]], start=True, stop=True)\
                  .then_inc(summed[half][u].sem, 1)

        in_runs(pe, T, W, tile)

    mem.close()
    return {"gpsimd": gpsimd, "vector": vector, "scalar": scalar, "tensor": tensor}


def degree_stage(kn):
    nc, d, dram, take = kn.nc, kn.d, kn.dram, kn.sig.take
    T = d.tiles
    dinv_out = take("dinv_out", 16 * T, software=True)
    dinv_in = take("dinv_in", 16 * T, software=True)
    fixed = take("fixed", 2)
    dinv_done = take("dinv_done", 1)

    def gpsimd(pool):
        nc.gpsimd.tensor_tensor(kn.dinv[:], kn.degree[:], kn.minus_half[:], ALU.pow).then_inc(dinv_done.sem, 1)
        pool.wait_ge(dinv_done.sem, dinv_done.at(1))
        for t in range(T):
            pool.indirect_dma_start(dram["dinv"], bass.IndirectOffsetOnAxis(ap=kn.final_i[:, t:t + 1], axis=0),
                                    kn.dinv[:, t:t + 1], None, bounds_check=d.nodes - 1, oob_is_err=False)\
                .then_inc(dinv_out.sem, 16)
        pool.wait_ge(dinv_out.sem, dinv_out.at(16 * T))
        for t in range(T):
            pool.indirect_dma_start(kn.src_dinv[:, t:t + 1], None, dram["dinv"],
                                    bass.IndirectOffsetOnAxis(ap=kn.src_i[:, t:t + 1], axis=0),
                                    bounds_check=d.padded - 1, oob_is_err=False).then_inc(dinv_in.sem, 16)
        pool.wait_ge(dinv_in.sem, dinv_in.at(16 * T))
        for u in range(2):
            nc.gpsimd.memset(kn.src_dinv[CARRY_IN[u]:CARRY_IN[u] + 1, u:T:2], 1.0).then_inc(fixed.sem, 1)
        pool.wait_ge(fixed.sem, fixed.at(2))

    return {"gpsimd": gpsimd}


def edge_attention_stage(kn, rows_dram):
    nc, d, dram, take, pair = kn.nc, kn.d, kn.dram, kn.sig.take, kn.sig.pair
    T, H = d.tiles, d.tiles // 2
    W = 8
    AHEAD = 6
    logits_dram = rows_dram.rearrange("n (a b) -> (n a) b", b=LOGITS)
    mem = ExitStack()

    def two(name, shape, dt):
        return [kn.buffer(mem, f"{name}{u}", shape, dt) for u in range(2)]

    def several(name, shape, dt):
        return [kn.buffer(mem, f"{name}{v}", shape, dt) for v in range(W)]

    K = HEADS
    rows = several("a_rows_", [P, GAT_ROW], F32)
    src_al = [row[:, 0:LOGITS] for row in rows]
    dst_al = several("a_dst", [P, 2 * K], F32)
    gather_at = several("a_gather_at", [P, 1], I32)
    dst_at = several("a_dst_at", [P, 1], I32)
    score = two("a_score", [P, 2 * K], F32)
    spread = two("a_spread", [P, K, P], F32)
    pen = two("a_pen", [P, P], F32)
    masked = two("a_masked", [P, K, P], F32)
    top = two("a_top", [P, K], F32)
    shifted = two("a_shifted", [P, 2 * K], F32)
    weight = two("a_weight", [P, 2 * K], F32)
    lhs = two("a_lhs", [P, K, P], F32)
    dval = two("a_dval", [P, K], F32)
    den = two("a_den", [P, K], F32)
    rden = two("a_rden", [P, K], F32)
    out = two("a_out", [P, HC + K], F32)
    final_at = two("a_final_at", [P, 1], I32)
    total = [[kn.bank[2 * u], kn.bank[2 * u + 1]] for u in range(2)]
    row_ps = [kn.bank[4 + u][:].rearrange("p (h q) -> p h q", h=K) for u in range(2)]
    den_ps = [kn.bank[6 + u][:, 0:K] for u in range(2)]

    indexed = take("indexed", 3 * T)
    gathered = kn.sig.several(W, "gathered", 16 * (T // W), software=True)
    dst_in = kn.sig.several(W, "dst_in_", 16 * (T // W), software=True)
    scattered = pair("scattered", 16 * H, software=True)
    PRE, FRONT, BACK = 4, 4, 3
    pre = Steps(take("pre_steps", PRE * T))
    front = Steps(take("front_steps", FRONT * T))
    back = Steps(take("back_steps", BACK * T))
    spread_ready = pair("spread_ready", H)
    row_done = pair("row_done", H)
    shift_ready = pair("shift_ready", H)
    weighed = pair("weighed", H)
    lhs_ready = pair("lhs_ready", H)
    den_done = pair("den_done", H)
    summed = pair("summed", H)
    carried = pair("carried", H)
    rden_ready = pair("rden_ready", H)
    evacuated = pair("evacuated", H)
    start = take("start", 4)

    def gpsimd(pool):
        g = nc.gpsimd

        def gather(i, v, n):
            t = i * W + v
            j, u = in_two(i, v, W)
            if not (isinstance(i, int) and i == 0):
                pool.wait_ge(summed[u].sem, summed[u].at(j + 1 - W // 2))
            g.tensor_copy(gather_at[v][:], kn.src_i[:, ds(t, 1)]).then_inc(indexed.sem, 1)
            g.tensor_copy(dst_at[v][:], kn.dst_logits_i[:, ds(t, 1)]).then_inc(indexed.sem, 1)
            pool.wait_ge(indexed.sem, indexed.at(n))
            settle(pool, kn)
            pool.indirect_dma_start(dst_al[v][:], None, logits_dram,
                                    bass.IndirectOffsetOnAxis(ap=dst_at[v][:], axis=0),
                                    bounds_check=d.padded * (GAT_ROW // LOGITS) - 1, oob_is_err=False)\
                .then_inc(dst_in[v].sem, 16)
            pool.indirect_dma_start(rows[v][:], None, rows_dram,
                                    bass.IndirectOffsetOnAxis(ap=gather_at[v][:], axis=0),
                                    bounds_check=d.padded - 1, oob_is_err=False)\
                .then_inc(gathered[v].sem, 16)

        def tile(i, v, left):
            t = i * W + v
            j, u = in_two(i, v, W)
            n = (t + 1 + AHEAD) * 2 + t if left >= AHEAD else 2 * T + t
            if left >= AHEAD:
                gather(*after(i, v, AHEAD, W), n)
            pool.wait_ge(scattered[u].sem, scattered[u].at(j * 16))
            g.tensor_copy(final_at[u][:], kn.final_i[:, ds(t, 1)]).then_inc(indexed.sem, 1)
            pool.wait_ge(indexed.sem, indexed.at(n + 1))
            pool.wait_ge(evacuated[u].sem, evacuated[u].at(j + 1))
            settle(pool, kn)
            pool.indirect_dma_start(dram["sum_gat"], bass.IndirectOffsetOnAxis(ap=final_at[u][:], axis=0),
                                    out[u][:], None, bounds_check=d.nodes - 1, oob_is_err=False)\
                .then_inc(scattered[u].sem, 16)

        for v in range(AHEAD):
            gather(0, v, 2 * v + 2)
        in_runs(pool, T, W, tile)
        for u in range(2):
            pool.wait_ge(scattered[u].sem, scattered[u].at(16 * H))

    def vector(dve):
        v = nc.vector
        v.memset(total[1][0][0:1, :], 0.0).then_inc(start.sem, 1)
        v.memset(total[1][1][0:1, :], 0.0).then_inc(start.sem, 1)
        v.memset(den_ps[1][0:1, :], 1.0).then_inc(start.sem, 1)
        v.memset(top[1][0:1, :], 0.0)
        for u in range(2):
            ins = v.memset(dval[u][:], 1.0)
        ins.then_inc(start.sem, 1)
        dve.wait_ge(start.sem, start.at(4))

        def scores(i, w):
            t = i * W + w
            j, u = in_two(i, w, W)
            pre.begin(t * PRE)
            own = pre.sig.sem
            dve.wait_ge(gathered[w].sem, gathered[w].at(i * 16 + 16))
            dve.wait_ge(dst_in[w].sem, dst_in[w].at(i * 16 + 16))
            dve.wait_ge(shift_ready[u].sem, shift_ready[u].at(j))
            pre.mark(v.tensor_tensor(score[u][:, 0:K], src_al[w][:, 0:K], dst_al[w][:, K:2 * K], ALU.add))
            n = pre.mark(v.tensor_tensor(score[u][:, K:2 * K], dst_al[w][:, 0:K], dst_al[w][:, K:2 * K], ALU.add))
            dve.wait_ge(own, n)
            pre.mark(v.scalar_tensor_tensor(out=score[u][:], in0=score[u][:], scalar=SLOPE, in1=score[u][:],
                                            op0=ALU.mult, op1=ALU.max))
            pre.mark(v.tensor_scalar(pen[u][:], kn.same[:, ds(t * P, P)], BIG, -BIG, ALU.mult, ALU.add))
            assert pre.n == PRE

        def spread_out(i, w):
            t = i * W + w
            _, u = in_two(i, w, W)
            c = CARRY_IN[u]
            front.begin(t * FRONT)
            own = front.sig.sem
            dve.wait_ge(pre.sig.sem, pre.sig.at(t * PRE + PRE))
            n = front.mark(v.tensor_copy(score[u][c:c + 1, 0:K], top[1 - u][c:c + 1, :]))
            dve.wait_ge(own, n)
            v.tensor_copy(spread[u][:], score[u][:, 0:K].unsqueeze(2).broadcast_to([P, K, P]))\
                .then_inc(spread_ready[u].sem, 1)

        def maxima(i, w):
            j, u = in_two(i, w, W)
            own = front.sig.sem
            dve.wait_ge(weighed[u].sem, weighed[u].at(j))
            dve.wait_ge(row_done[u].sem, row_done[u].at(j + 1))
            n = front.mark(v.tensor_tensor(masked[u][:], row_ps[u], pen[u][:].unsqueeze(1).broadcast_to([P, K, P]),
                                           ALU.add))
            dve.wait_ge(own, n)
            n = front.mark(v.tensor_reduce(top[u][:], masked[u][:], AX.X, ALU.max))
            dve.wait_ge(own, n)
            n = front.mark(v.tensor_tensor(top[u][:], top[u][:], score[u][:, K:2 * K], ALU.max))
            dve.wait_ge(own, n)
            v.tensor_tensor(shifted[u][:, 0:K], score[u][:, 0:K], top[u][:], ALU.subtract)
            v.tensor_tensor(shifted[u][:, K:2 * K], score[u][:, K:2 * K], top[u][:], ALU.subtract)\
                .then_inc(shift_ready[u].sem, 1)
            assert front.n == FRONT

        def sums(i, w, left):
            t = i * W + w
            j, u = in_two(i, w, W)
            c = CARRY_IN[u]
            back.begin(t * BACK)
            own = back.sig.sem
            if left:
                spread_out(*after(i, w, 1, W))
            dve.wait_ge(weighed[u].sem, weighed[u].at(j + 1))
            dve.wait_ge(summed[u].sem, summed[u].at(j))
            dve.wait_ge(den_done[1 - u].sem, den_done[1 - u].at(j + u))
            back.mark(v.tensor_copy(dval[u][c:c + 1, :], den_ps[1 - u][c:c + 1, :]))
            v.tensor_tensor(lhs[u][:], kn.same[:, ds(t * P, P)].unsqueeze(1).broadcast_to([P, K, P]),
                            weight[u][:, 0:K].unsqueeze(2).broadcast_to([P, K, P]), ALU.mult)\
                .then_inc(lhs_ready[u].sem, 1)
            if left >= 2:
                scores(*after(i, w, 2, W))
            if left:
                maxima(*after(i, w, 1, W))
            dve.wait_ge(den_done[u].sem, den_done[u].at(j + 1))
            n = back.mark(v.tensor_tensor(den[u][:], den_ps[u], weight[u][:, K:2 * K], ALU.add))
            dve.wait_ge(own, n)
            dve.wait_ge(evacuated[u].sem, evacuated[u].at(j))
            dve.wait_ge(scattered[u].sem, scattered[u].at(j * 16))
            n = back.mark(v.reciprocal(rden[u][:], den[u][:]))
            dve.wait_ge(own, n)
            v.tensor_tensor(out[u][:, HC:HC + K], weight[u][:, K:2 * K], rden[u][:], ALU.mult)\
                .then_inc(rden_ready[u].sem, 1)
            assert back.n == BACK

        scores(0, 0)
        scores(0, 1)
        spread_out(0, 0)
        maxima(0, 0)
        in_runs(dve, T, W, sums)

    def scalar(act):
        act.wait_ge(start.sem, start.at(4))

        def weigh(i, v):
            j, u = in_two(i, v, W)
            act.wait_ge(shift_ready[u].sem, shift_ready[u].at(j + 1))
            act.wait_ge(rden_ready[u].sem, rden_ready[u].at(j))
            act.activation(weight[u][:], shifted[u][:], ACT.Exp).then_inc(weighed[u].sem, 1)

        def tile(i, v, left):
            j, u = in_two(i, v, W)
            c = CARRY_IN[u]
            act.wait_ge(gathered[v].sem, gathered[v].at(i * 16 + 16))
            act.wait_ge(summed[1 - u].sem, summed[1 - u].at(j + u))
            act.copy(rows[v][c:c + 1, LOGITS:LOGITS + D], total[1 - u][0][c:c + 1, :])
            act.copy(rows[v][c:c + 1, LOGITS + D:], total[1 - u][1][c:c + 1, :]).then_inc(carried[u].sem, 1)
            if left:
                weigh(*after(i, v, 1, W))
            act.wait_ge(rden_ready[u].sem, rden_ready[u].at(j + 1))
            act.wait_ge(summed[u].sem, summed[u].at(j + 1))
            act.wait_ge(scattered[u].sem, scattered[u].at(j * 16))
            for h in range(K):
                ins = act.activation(out[u][:, h * C:(h + 1) * C],
                                     total[u][h // 2][:, (h % 2) * C:(h % 2 + 1) * C], ACT.Copy,
                                     scale=rden[u][:, h:h + 1])
            ins.then_inc(evacuated[u].sem, 1)

        weigh(0, 0)
        in_runs(act, T, W, tile)

    def tensor(pe):
        def score_rows(i, v):
            j, u = in_two(i, v, W)
            pe.wait_ge(spread_ready[u].sem, spread_ready[u].at(j + 1))
            for h in range(K):
                mm = pe.matmul(row_ps[u][:, h, :], spread[u][:, h, :], kn.ident[:], start=True, stop=True)
            mm.then_inc(row_done[u].sem, 1)

        def tile(i, v, left):
            j, u = in_two(i, v, W)
            if left:
                score_rows(*after(i, v, 1, W))
            pe.wait_ge(lhs_ready[u].sem, lhs_ready[u].at(j + 1))
            pe.wait_ge(rden_ready[u].sem, rden_ready[u].at(j))
            for h in range(K):
                mm = pe.matmul(den_ps[u][:, h:h + 1], lhs[u][:, h, :], dval[u][:, h:h + 1], start=True, stop=True)
            mm.then_inc(den_done[u].sem, 1)
            pe.wait_ge(carried[u].sem, carried[u].at(j + 1))
            pe.wait_ge(evacuated[u].sem, evacuated[u].at(j))
            for h in range(K):
                mm = pe.matmul(total[u][h // 2][:, (h % 2) * C:(h % 2 + 1) * C], lhs[u][:, h, :],
                               rows[v][:, LOGITS + h * C:LOGITS + (h + 1) * C], start=True, stop=True)
            mm.then_inc(summed[u].sem, 1)

        score_rows(0, 0)
        in_runs(pe, T, W, tile)

    mem.close()
    return {"gpsimd": gpsimd, "vector": vector, "scalar": scalar, "tensor": tensor}


class Norm:

    def __init__(self, kn, mem):
        self.kn, self.nc, n = kn, kn.nc, kn.d.groups
        self.stats = kn.buffer(mem, "n_stats", [P, 2, S, 6], F32)
        self.moments = kn.buffer(mem, "n_moments", [P, 2, S, 2], F32)
        self.power = kn.buffer(mem, "n_power", [P, 2, S], F32)
        self.seen = kn.sig.take("n_seen", 2 * S * n)
        self.rstd = kn.sig.take("n_rstd", 2 * n)

    def moments_of(self, dve, row, s, i, u):
        g = i * 2 + u
        self.nc.vector.bn_stats(self.stats[:, u, s, :], row).then_inc(self.seen.sem, 1)
        dve.wait_ge(self.seen.sem, self.seen.at(g * (2 * S) + 2 * s + 1))
        settle(dve, self.kn)
        self.nc.vector.bn_aggr(self.moments[:, u, s, :], self.stats[:, u, s, :]).then_inc(self.seen.sem, 1)

    def pool(self, pool, i, u):
        g = i * 2 + u
        pool.wait_ge(self.seen.sem, self.seen.at(g * (2 * S) + 2 * S))
        self.nc.gpsimd.tensor_tensor(self.power[:, u, :], self.moments[:, u, :, 1], self.kn.eps[:], ALU.add)\
            .then_inc(self.rstd.sem, 1)
        pool.wait_ge(self.rstd.sem, self.rstd.at(g * 2 + 1))
        self.nc.gpsimd.tensor_tensor(self.power[:, u, :], self.power[:, u, :],
                                     self.kn.minus_half[:, 0:1].broadcast_to([P, S]), ALU.pow)\
            .then_inc(self.rstd.sem, 1)

    def apply(self, dve, out, rows, i, u, done):
        dve.wait_ge(self.rstd.sem, self.rstd.at((i * 2 + u) * 2 + 2))
        for s in range(S):
            self.nc.vector.tensor_scalar(out[:, s, :], rows[:, s, :], self.moments[:, u, s, 0:1],
                                         self.power[:, u, s:s + 1], ALU.subtract, ALU.mult).then_inc(done.sem, 1)


def node_rows(ap, i, u):
    return ap[ds(i * (2 * GROUP) + u * GROUP, GROUP), :].rearrange("(s p) c -> p s c", p=P)


def gin_stage(kn):
    nc, d, dram, take, pair = kn.nc, kn.d, kn.dram, kn.sig.take, kn.sig.pair
    G, H = d.groups, d.groups // 2
    mem = ExitStack()

    def two(name, shape, dt):
        return [kn.buffer(mem, f"{name}{u}", shape, dt) for u in range(2)]

    x = two("g_x", [P, S, D], F32)
    z = two("g_z", [P, S, D], F32)
    z_hi = kn.buffer(mem, "g_z_hi", [P, 4, D], F16)
    z_lo = kn.buffer(mem, "g_z_lo", [P, 4, D], F16)
    r_f = two("g_r", [P, D], F32)
    r_hi = kn.buffer(mem, "g_r_hi", [P, 4, D], F16)
    r_lo = kn.buffer(mem, "g_r_lo", [P, 4, D], F16)
    y = two("g_y", [P, S, D], F32)
    blank = kn.buffer(mem, "g_blank", [P, HC + HEADS], F32)
    norm = Norm(kn, mem)
    tp = [kn.bank[0], kn.bank[1]]
    mm = [kn.bank[2 + s] for s in range(S)]
    mid_ps = [kn.bank[6], kn.bank[7]]

    x_in = pair("x_in", 16 * H)
    sum_in = pair("sum_in", 16 * H)
    z_ready = pair("z_ready", H * S)
    x_ready = pair("x_ready", H)
    turned = pair("turned", 4 * H)
    hi_done = take("hi_done", 4 * G)
    lo_done = take("lo_done", 4 * G)
    mid = take("mid", 4 * G)
    r_done = take("r_done", 4 * G)
    r_hi_done = take("r_hi_done", 4 * G)
    r_lo_done = take("r_lo_done", 4 * G)
    prod = take("prod", S * G)
    y_done = pair("y_done_", S * H)
    rows_out = pair("rows_out", S * H)
    stored = pair("stored", 16 * H)
    blank_ready = take("blank_ready", 2)
    zeroed = take("zeroed", 16 * G)

    def sync(sp):
        def load_x(i, u):
            sp.wait_ge(y_done[u].sem, y_done[u].at(i * S))
            sp.dma_start(x[u][:], node_rows(dram["x"], i, u)).then_inc(x_in[u].sem, 16)

        def load_sums(i, u):
            sp.wait_ge(turned[u].sem, turned[u].at(i * 4))
            sp.dma_start(z[u][:], node_rows(dram["sum"], i, u)).then_inc(sum_in[u].sem, 16)

        def group(i, u, last):
            if not last:
                load_x(*following(i, u))
            if ahead(i, G):
                load_sums(i + 1, u)
            sp.dma_start(node_rows(dram["sum_gat"], i, u), blank[:].unsqueeze(1).broadcast_to([P, S, HC + HEADS]))\
                .then_inc(zeroed.sem, 16)
            sp.wait_ge(rows_out[u].sem, rows_out[u].at(i * S + S))
            sp.dma_start(node_rows(dram["x1"], i, u), y[u][:]).then_inc(stored[u].sem, 16)

        load_sums(0, 0)
        load_x(0, 0)
        load_sums(0, 1)
        sp.wait_ge(blank_ready.sem, blank_ready.at(2))
        in_pairs(sp, G, group)
        for u in range(2):
            sp.wait_ge(stored[u].sem, stored[u].at(16 * H))
        sp.wait_ge(zeroed.sem, zeroed.at(16 * G))

    def gpsimd(pool):
        nc.gpsimd.memset(blank[:, 0:HC], 0.0).then_inc(blank_ready.sem, 1)
        nc.gpsimd.memset(blank[:, HC:], 1.0).then_inc(blank_ready.sem, 1)

        def group(i, u, last):
            pool.wait_ge(z_ready[u].sem, z_ready[u].at(i * S + S))
            nc.gpsimd.tensor_tensor(x[u][:], x[u][:], kn.gin_b2[:].unsqueeze(1).broadcast_to([P, S, D]), ALU.add)\
                .then_inc(x_ready[u].sem, 1)
            norm.pool(pool, i, u)

        in_pairs(pool, G, group)

    def vector(dve):
        v = nc.vector

        def add_sums(i, u):
            dve.wait_ge(x_in[u].sem, x_in[u].at(i * 16 + 16))
            dve.wait_ge(sum_in[u].sem, sum_in[u].at(i * 16 + 16))
            for s in range(S):
                v.tensor_tensor(z[u][:, s, :], z[u][:, s, :], x[u][:, s, :], ALU.add).then_inc(z_ready[u].sem, 1)

        def low_parts(i, u, chunks=range(4)):
            g = i * 2 + u
            for k in chunks:
                dve.wait_ge(hi_done.sem, hi_done.at(g * 4 + k + 1))
                v.scalar_tensor_tensor(out=z_lo[:, k, :], in0=tp[k % 2][:], scalar=GIN_SCALE, in1=z_hi[:, k, :],
                                       op0=ALU.mult, op1=ALU.subtract).then_inc(lo_done.sem, 1)

        def group(i, u, last):
            g = i * 2 + u
            for m in range(4):
                dve.wait_ge(r_hi_done.sem, r_hi_done.at(g * 4 + m + 1))
                v.tensor_tensor(r_lo[:, m, :], r_f[m % 2][:], r_hi[:, m, :], ALU.subtract).then_inc(r_lo_done.sem, 1)
            if not last:
                add_sums(*following(i, u))
            dve.wait_ge(x_ready[u].sem, x_ready[u].at(i + 1))
            dve.wait_ge(stored[u].sem, stored[u].at(i * 16))
            for s in range(S):
                if s >= 2 and not last:
                    low_parts(*following(i, u), (2 * s - 4, 2 * s - 3))
                dve.wait_ge(prod.sem, prod.at(g * S + s + 1))
                v.scalar_tensor_tensor(out=y[u][:, s, :], in0=mm[s][:], scalar=GIN_UNSCALE, in1=x[u][:, s, :],
                                       op0=ALU.mult, op1=ALU.add).then_inc(y_done[u].sem, 1)
                dve.wait_ge(y_done[u].sem, y_done[u].at(i * S + s + 1))
                norm.moments_of(dve, y[u][:, s, :], s, i, u)
            norm.apply(dve, y[u], y[u], i, u, rows_out[u])

        add_sums(0, 0)
        low_parts(0, 0)
        in_pairs(dve, G, group)

    def scalar(act):
        def high_parts(i, u):
            for k in range(4):
                act.wait_ge(turned[u].sem, turned[u].at(i * 4 + k + 1))
                act.activation(z_hi[:, k, :], tp[k % 2][:], ACT.Copy, scale=GIN_SCALE).then_inc(hi_done.sem, 1)

        def group(i, u, last):
            g = i * 2 + u
            for m in range(4):
                act.wait_ge(mid.sem, mid.at(g * 4 + m + 1))
                if m >= 2:
                    act.wait_ge(r_lo_done.sem, r_lo_done.at(g * 4 + m - 1))
                act.wait_ge(prod.sem, prod.at(g * S))
                act.activation(r_f[m % 2][:], mid_ps[m % 2][:], ACT.Relu, scale=GIN_UNSCALE * GIN_SCALE,
                               bias=kn.vec_scaled[:, V_GIN_B1 + m:V_GIN_B1 + m + 1]).then_inc(r_done.sem, 1)
                act.wait_ge(r_done.sem, r_done.at(g * 4 + m + 1))
                act.copy(r_hi[:, m, :], r_f[m % 2][:]).then_inc(r_hi_done.sem, 1)
            if not last:
                high_parts(*following(i, u))

        high_parts(0, 0)
        in_pairs(act, G, group)

    def tensor(pe):
        def turn(i, u, chunks=range(4)):
            g = i * 2 + u
            pe.wait_ge(z_ready[u].sem, z_ready[u].at(i * S + S))
            for k in chunks:
                if k >= 2:
                    pe.wait_ge(lo_done.sem, lo_done.at(g * 4 + k - 1))
                else:
                    pe.wait_ge(lo_done.sem, lo_done.at(g * 4))
                for s in range(S):
                    ins = pe.transpose(tp[k % 2][:, s * P:(s + 1) * P], z[u][:, s, k * P:(k + 1) * P], kn.ident[:])
                ins.then_inc(turned[u].sem, 1)

        def group(i, u, last):
            g = i * 2 + u
            def split(k):
                pe.wait_ge(lo_done.sem, lo_done.at(g * 4 + k + 1))

            for m in range(4):
                pe.wait_ge(r_done.sem, r_done.at(g * 4 + (m - 1 if m >= 2 else 0)))
                split_product(pe, mid_ps[m % 2][:],
                              lambda k: (kn.weights(False, W_GIN1, k)[:, m * P:(m + 1) * P],
                                         kn.weights(True, W_GIN1, k)[:, m * P:(m + 1) * P]),
                              lambda k: (z_hi[:, k, :], z_lo[:, k, :]), 4, split if m == 0 else None)\
                    .then_inc(mid.sem, 1)

            def hidden(k):
                pe.wait_ge(r_lo_done.sem, r_lo_done.at(g * 4 + k + 1))

            for s in range(S):
                if s >= 2 and not last:
                    turn(*following(i, u), (2 * s - 4, 2 * s - 3))
                pe.wait_ge(y_done[1 - u].sem, y_done[1 - u].at((i + u - 1) * S + s + 1))
                split_product(pe, mm[s][:],
                              lambda k: (r_hi[:, k, s * P:(s + 1) * P], r_lo[:, k, s * P:(s + 1) * P]),
                              lambda k: (kn.weights(False, W_GIN2, k), kn.weights(True, W_GIN2, k)),
                              4, hidden if s == 0 else None).then_inc(prod.sem, 1)

        turn(0, 0)
        in_pairs(pe, G, group)

    mem.close()
    return {"sync": sync, "gpsimd": gpsimd, "vector": vector, "scalar": scalar, "tensor": tensor}


def linear_stage(kn, layer):
    nc, d, dram, take, pair = kn.nc, kn.d, kn.dram, kn.sig.take, kn.sig.pair
    G, H = d.groups, d.groups // 2
    sage = layer == "sage"
    chunks = 8 if sage else 4
    unit = W_SAGE_L if sage else W_GCN
    bias = V_SAGE_B if sage else V_GCN_B
    x_dram = dram["x1"] if sage else dram["x3"]
    turns = ((0, 1), (2, 3), (4, 5), (6, 7)) if sage else ((), (), (0, 1), (2, 3))
    mem = ExitStack()

    def two(name, shape, dt):
        return [kn.buffer(mem, f"{name}{u}", shape, dt) for u in range(2)]

    x = two("l_x", [P, S, D], F32)
    z = two("l_z", [P, S, D], F32)
    node_dinv = two("l_dinv", [P, S, 1], F32)
    z_hi = kn.buffer(mem, "l_z_hi", [P, 2, chunks, D], F16)
    z_lo = kn.buffer(mem, "l_z_lo", [P, 2, chunks, D], F16)
    h = two("l_h", [P, 4, D], F32)
    tp = [kn.bank[0], kn.bank[1]]
    mm = [kn.bank[2 + n] for n in range(4)]

    x_in = pair("x_in", 16 * H)
    sum_in = pair("sum_in", 16 * H)
    dinv_in = pair("dinv_in_", 0 if sage else 16 * H)
    z_ready = pair("z_ready", 0 if sage else H * 2 * S)
    turned = pair("turned", chunks * H)
    hi_done = take("hi_done", chunks * G)
    lo_done = take("lo_done", chunks * G)
    mid = take("mid", 4 * G)
    h_done = take("h_done", 4 * G)
    seen = take("h_seen", 4 * G)
    stored = pair("stored", 16 * H)

    def sync(sp):
        def load(i, u):
            sp.wait_ge(turned[u].sem, turned[u].at(i * chunks))
            sp.dma_start(x[u][:], node_rows(x_dram, i, u)).then_inc(x_in[u].sem, 16)
            sp.dma_start(z[u][:], node_rows(dram["sum"], i, u)).then_inc(sum_in[u].sem, 16)
            if not sage:
                sp.dma_start(node_dinv[u][:], node_rows(dram["dinv"], i, u),
                             allow_slow_non_contiguous=True).then_inc(dinv_in[u].sem, 16)

        def group(i, u, last):
            g = i * 2 + u
            if ahead(i, G):
                load(i + 1, u)
            sp.wait_ge(h_done.sem, h_done.at(g * 4 + 4))
            settle(sp, kn)
            sp.dma_start(dram["h"][:, :, ds(i * (2 * GROUP) + u * GROUP, GROUP)].rearrange("m p n -> p m n"), h[u][:])\
                .then_inc(stored[u].sem, 16)

        load(0, 0)
        load(0, 1)
        in_pairs(sp, G, group)
        for u in range(2):
            sp.wait_ge(stored[u].sem, stored[u].at(16 * H))

    def vector(dve):
        v = nc.vector

        def scale(i, u):
            if sage:
                return
            dve.wait_ge(x_in[u].sem, x_in[u].at(i * 16 + 16))
            dve.wait_ge(sum_in[u].sem, sum_in[u].at(i * 16 + 16))
            dve.wait_ge(dinv_in[u].sem, dinv_in[u].at(i * 16 + 16))
            for s in range(S):
                v.scalar_tensor_tensor(out=z[u][:, s, :], in0=x[u][:, s, :], scalar=node_dinv[u][:, s, :],
                                       in1=z[u][:, s, :], op0=ALU.mult, op1=ALU.add).then_inc(z_ready[u].sem, 1)
            dve.wait_ge(z_ready[u].sem, z_ready[u].at(i * (2 * S) + S))
            for s in range(S):
                v.tensor_scalar(z[u][:, s, :], z[u][:, s, :], node_dinv[u][:, s, :], None, ALU.mult)\
                    .then_inc(z_ready[u].sem, 1)

        def low_parts(i, u, some=range(chunks)):
            g = i * 2 + u
            for k in some:
                dve.wait_ge(hi_done.sem, hi_done.at(g * chunks + k + 1))
                v.scalar_tensor_tensor(out=z_lo[:, u, k, :], in0=tp[k % 2][:], scalar=A_SCALE, in1=z_hi[:, u, k, :],
                                       op0=ALU.mult, op1=ALU.subtract).then_inc(lo_done.sem, 1)

        def group(i, u, last):
            g = i * 2 + u

            real = d.last_real if last else GROUP
            if not last:
                scale(*following(i, u))
            for m in range(4):
                if not last:
                    low_parts(*following(i, u), turns[m])
                dve.wait_ge(h_done.sem, h_done.at(g * 4 + m + 1))
                v.bn_stats(kn.bn_stats[:, m, ds(g * 6, 6)], h[u][:, m, 0:real]).then_inc(seen.sem, 1)

        scale(0, 0)
        low_parts(0, 0)
        in_pairs(dve, G, group)

    def scalar(act):
        def high_parts(i, u, some=range(chunks)):
            for k in some:
                act.wait_ge(turned[u].sem, turned[u].at(i * chunks + k + 1))
                act.activation(z_hi[:, u, k, :], tp[k % 2][:], ACT.Copy, scale=A_SCALE).then_inc(hi_done.sem, 1)

        def group(i, u, last):
            g = i * 2 + u

            act.wait_ge(stored[u].sem, stored[u].at(i * 16))
            act.wait_ge(seen.sem, seen.at((g - 1) * 4))
            for m in range(4):
                if not last:
                    high_parts(*following(i, u), turns[m])
                act.wait_ge(mid.sem, mid.at(g * 4 + m + 1))
                act.activation(h[u][:, m, :], mm[m][:], ACT.Identity, scale=UNSCALE,
                               bias=kn.vec[:, bias + m:bias + m + 1]).then_inc(h_done.sem, 1)

        high_parts(0, 0)
        in_pairs(act, G, group)

    def tensor(pe):
        def turn(i, u, some=range(chunks)):
            g = i * 2 + u
            if sage:
                pe.wait_ge(x_in[u].sem, x_in[u].at(i * 16 + 16))
                pe.wait_ge(sum_in[u].sem, sum_in[u].at(i * 16 + 16))
            else:
                pe.wait_ge(z_ready[u].sem, z_ready[u].at(i * (2 * S) + 2 * S))
            for k in some:
                pe.wait_ge(lo_done.sem, lo_done.at(g * chunks + (k - 1 if k >= 2 else 0)))
                rows = z[u] if k < 4 else x[u]
                for s in range(S):
                    ins = pe.transpose(tp[k % 2][:, s * P:(s + 1) * P], rows[:, s, (k % 4) * P:(k % 4 + 1) * P],
                                       kn.ident[:])
                ins.then_inc(turned[u].sem, 1)

        def group(i, u, last):
            g = i * 2 + u
            pe.wait_ge(lo_done.sem, lo_done.at(g * chunks + chunks))
            for m in range(4):
                if turns[m] and not last:
                    turn(*following(i, u), turns[m])
                pe.wait_ge(h_done.sem, h_done.at((g - 1) * 4 + m + 1))
                split_product(pe, mm[m][:],
                              lambda k: (kn.weights(False, unit, k)[:, m * P:(m + 1) * P],
                                         kn.weights(True, unit, k)[:, m * P:(m + 1) * P]),
                              lambda k: (z_hi[:, u, k, :], z_lo[:, u, k, :]), chunks).then_inc(mid.sem, 1)

        turn(0, 0)
        in_pairs(pe, G, group)

    mem.close()
    return {"sync": sync, "vector": vector, "scalar": scalar, "tensor": tensor}


def norm_coefficients_stage(kn, gamma, beta):
    nc, take = kn.nc, kn.sig.take
    mem = ExitStack()
    mv = kn.buffer(mem, "c_mv", [P, 4, 2], F32)
    rstd = kn.buffer(mem, "c_rstd", [P, 4], F32)
    neg = kn.buffer(mem, "c_neg", [P, 4], F32)
    steps = take("coef_steps", 9)

    def vector(dve):
        v = nc.vector
        for m in range(4):
            v.bn_aggr(mv[:, m, :], kn.bn_stats[:, m, :]).then_inc(steps.sem, 1)
        dve.wait_ge(steps.sem, steps.at(6))
        v.tensor_tensor(kn.bn_scale[:], rstd[:], kn.vec[:, gamma:gamma + 4], ALU.mult).then_inc(steps.sem, 1)
        dve.wait_ge(steps.sem, steps.at(7))
        v.tensor_tensor(neg[:], mv[:, :, 0], kn.bn_scale[:], ALU.mult).then_inc(steps.sem, 1)
        dve.wait_ge(steps.sem, steps.at(8))
        v.tensor_tensor(kn.bn_shift[:], kn.vec[:, beta:beta + 4], neg[:], ALU.subtract).then_inc(steps.sem, 1)

    def gpsimd(pool):
        g = nc.gpsimd
        pool.wait_ge(steps.sem, steps.at(4))
        g.tensor_scalar(rstd[:], mv[:, :, 1], EPS, None, ALU.add).then_inc(steps.sem, 1)
        pool.wait_ge(steps.sem, steps.at(5))
        g.tensor_tensor(rstd[:], rstd[:], kn.minus_half[:, 0:1].broadcast_to([P, 4]), ALU.pow).then_inc(steps.sem, 1)

    mem.close()
    return {"vector": vector, "gpsimd": gpsimd}


def batch_norm_stage(kn, layer):
    nc, d, dram, take, pair = kn.nc, kn.d, kn.dram, kn.sig.take, kn.sig.pair
    G, H = d.groups, d.groups // 2
    sage = layer == "sage"
    func = ACT.Relu if sage else ACT.Gelu
    x_dram, out_dram = (dram["x1"], dram["x2_biased"]) if sage else (dram["x3"], dram["out"])
    mem = ExitStack()

    def two(name, shape, dt):
        return [kn.buffer(mem, f"{name}{u}", shape, dt) for u in range(2)]

    h = two("b_h", [P, 4, D], F32)
    x = two("b_x", [P, S, D], F32)
    y = two("b_y", [P, S, D], F32) if not sage else [kn.buffer(mem, "b_y", [P, S, D], F32)] * 2
    o = two("b_o", [P, S, D], F32)
    if sage:
        z_hi = kn.buffer(mem, "b_z_hi", [P, 2, 4, D], F16)
        z_lo = kn.buffer(mem, "b_z_lo", [P, 2, 4, D], F16)
        wide = two("b_wide", [P, GAT_ROW], F32)
    norm = Norm(kn, mem)
    tp = [[kn.bank[n] for n in (0, 1, 0, 1)]] * 2 if sage else [kn.bank[0:4], kn.bank[4:8]]
    tq = [kn.bank[2], kn.bank[3]]
    mm = [kn.bank[4 + n][:, 0:THIRD] for n in range(THIRDS)]

    h_in = pair("h_in", 16 * H)
    x_in = pair("x_in", 16 * H)
    f_done = pair("f_done", 4 * H)
    rows_turned = pair("rows_turned", S * H)
    y_done = pair("y_done_", S * H)
    rows_out = pair("rows_out", S * H)
    stored = pair("stored", 16 * H)
    biased = pair("biased", H if sage else 0)
    turned = pair("turned", 4 * H if sage else 0)
    hi_done = take("hi_done", 4 * G if sage else 0)
    lo_done = take("lo_done", 4 * G if sage else 0)
    prod = take("prod", THIRDS * S * G if sage else 0)
    wide_done = take("wide_done", THIRDS * S * G if sage else 0)
    wide_stored = pair("wide_stored", 16 * 2 * G if sage else 0)

    def sync(sp):
        def load(i, u):
            sp.wait_ge(rows_turned[u].sem, rows_turned[u].at(i * S))
            settle(sp, kn)
            sp.dma_start(h[u][:], dram["h"][:, :, ds(i * (2 * GROUP) + u * GROUP, GROUP)]
                         .rearrange("m p n -> p m n")).then_inc(h_in[u].sem, 16)
            sp.wait_ge(y_done[u].sem, y_done[u].at(i * S))
            sp.dma_start(x[u][:], node_rows(x_dram, i, u)).then_inc(x_in[u].sem, 16)

        def store(i, u):
            if sage:
                sp.wait_ge(biased[u].sem, biased[u].at(i + 1))
            else:
                sp.wait_ge(rows_out[u].sem, rows_out[u].at(i * S + S))
            sp.dma_start(node_rows(out_dram, i, u), o[u][:]).then_inc(stored[u].sem, 16)

        def group(i, u, last):
            g = i * 2 + u
            if ahead(i, G):
                load(i + 1, u)
            store(i, u)
            if sage:
                for s in range(S):
                    sp.wait_ge(wide_done.sem, wide_done.at((g * S + s + 1) * THIRDS))
                    sp.dma_start(dram["h1"][ds(i * (2 * GROUP) + u * GROUP + s * P, P), :], wide[s % 2][:])\
                        .then_inc(wide_stored[s % 2].sem, 16)

        load(0, 0)
        load(0, 1)
        in_pairs(sp, G, group)
        for u in range(2):
            sp.wait_ge(stored[u].sem, stored[u].at(16 * H))
            if sage:
                sp.wait_ge(wide_stored[u].sem, wide_stored[u].at(16 * 2 * G))

    def gpsimd(pool):
        def bias(i, u):
            pool.wait_ge(turned[u].sem, turned[u].at(i * 4 + 4))
            nc.gpsimd.tensor_tensor(o[u][:], o[u][:], kn.fc_b[:].unsqueeze(1).broadcast_to([P, S, D]), ALU.add)\
                .then_inc(biased[u].sem, 1)

        def group(i, u, last):
            if not last:
                norm.pool(pool, *following(i, u))
                bias(*following(i, u))

        if sage:
            norm.pool(pool, 0, 0)
            bias(0, 0)
            in_pairs(pool, G, group)
        else:
            in_pairs(pool, G, lambda i, u, last: norm.pool(pool, i, u))

    def vector(dve):
        v = nc.vector

        def residual(i, u, subtiles):
            dve.wait_ge(x_in[u].sem, x_in[u].at(i * 16 + 16))
            dve.wait_ge(rows_out[u].sem, rows_out[u].at(i * S))
            for s in subtiles:
                dve.wait_ge(rows_turned[u].sem, rows_turned[u].at(i * S + s + 1))
                v.scalar_tensor_tensor(out=y[u][:, s, :], in0=x[u][:, s, :], scalar=2.0, in1=tp[u][s][:],
                                       op0=ALU.mult, op1=ALU.add).then_inc(y_done[u].sem, 1)
                dve.wait_ge(y_done[u].sem, y_done[u].at(i * S + s + 1))
                norm.moments_of(dve, y[u][:, s, :], s, i, u)

        def finish(i, u):
            dve.wait_ge(stored[u].sem, stored[u].at(i * 16))
            norm.apply(dve, o[u], y[u], i, u, rows_out[u])

        def low_parts(i, u):
            g = i * 2 + u
            for k in range(4):
                dve.wait_ge(hi_done.sem, hi_done.at(g * 4 + k + 1))
                v.scalar_tensor_tensor(out=z_lo[:, u, k, :], in0=tq[k % 2][:], scalar=A_SCALE, in1=z_hi[:, u, k, :],
                                       op0=ALU.mult, op1=ALU.subtract).then_inc(lo_done.sem, 1)

        def group(i, u, last):
            if not last:
                residual(*following(i, u), range(S))
                finish(*following(i, u))
                low_parts(*following(i, u))

        def group_alone(i, u, last):
            if not last:
                residual(*following(i, u), range(S))
            finish(i, u)

        residual(0, 0, range(S))
        if sage:
            finish(0, 0)
            low_parts(0, 0)
        in_pairs(dve, G, group if sage else group_alone)

    def scalar(act):
        def apply(i, u):
            act.wait_ge(h_in[u].sem, h_in[u].at(i * 16 + 16))
            for m in range(4):
                act.activation(h[u][:, m, :], h[u][:, m, :], func, scale=kn.bn_scale[:, m:m + 1],
                               bias=kn.bn_shift[:, m:m + 1]).then_inc(f_done[u].sem, 1)

        def high_parts(i, u):
            for k in range(4):
                act.wait_ge(turned[u].sem, turned[u].at(i * 4 + k + 1))
                act.activation(z_hi[:, u, k, :], tq[k % 2][:], ACT.Copy, scale=A_SCALE).then_inc(hi_done.sem, 1)

        def group(i, u, last):
            g = i * 2 + u
            for s in range(S):
                if s == 1 and ahead(i, G):
                    apply(i + 1, u)
                if s == 3 and not last:
                    high_parts(*following(i, u))
                w = wide_stored[s % 2]
                act.wait_ge(w.sem, w.at(g * 32 + (s // 2) * 16))
                for n in range(THIRDS):
                    act.wait_ge(prod.sem, prod.at((g * S + s) * THIRDS + n + 1))
                    act.activation(wide[s % 2][:, n * THIRD:(n + 1) * THIRD], mm[n], ACT.Copy, scale=UNSCALE)\
                       .then_inc(wide_done.sem, 1)

        if sage:
            apply(0, 0)
            apply(0, 1)
            high_parts(0, 0)
            in_pairs(act, G, group)
        else:
            in_pairs(act, G, lambda i, u, last: apply(i, u))

    def tensor(pe):
        def turn_rows(i, u, subtiles):
            pe.wait_ge(f_done[u].sem, f_done[u].at(i * 4 + 4))
            for s in subtiles:
                if not sage:
                    pe.wait_ge(y_done[u].sem, y_done[u].at((i - 1) * S + s + 1))
                elif s >= 2:
                    pe.wait_ge(y_done[u].sem, y_done[u].at(i * S + s - 1))
                else:
                    pe.wait_ge(y_done[1 - u].sem, y_done[1 - u].at((i + u) * S))
                for m in range(4):
                    ins = pe.transpose(tp[u][s][:, m * P:(m + 1) * P], h[u][:, m, s * P:(s + 1) * P], kn.ident[:])
                ins.then_inc(rows_turned[u].sem, 1)

        def turn_back(i, u):
            g = i * 2 + u
            pe.wait_ge(rows_out[u].sem, rows_out[u].at(i * S + S))
            for k in range(4):
                pe.wait_ge(lo_done.sem, lo_done.at(g * 4 + (k - 1 if k >= 2 else 0)))
                for s in range(S):
                    ins = pe.transpose(tq[k % 2][:, s * P:(s + 1) * P], o[u][:, s, k * P:(k + 1) * P], kn.ident[:])
                ins.then_inc(turned[u].sem, 1)

        def products(i, u, s):
            g = i * 2 + u
            parts = lambda k: (z_hi[:, u, k, s * P:(s + 1) * P], z_lo[:, u, k, s * P:(s + 1) * P])
            for n in range(THIRDS):
                pe.wait_ge(wide_done.sem, wide_done.at((g * S + s - 1) * THIRDS + n + 1))
                split_product(pe, mm[n], parts,
                              lambda k: (kn.gat_weights(False, W_GAT1, k, n), kn.gat_weights(True, W_GAT1, k, n)),
                              4).then_inc(prod.sem, 1)

        def group(i, u, last):
            pe.wait_ge(lo_done.sem, lo_done.at((i * 2 + u) * 4 + 4))
            if not last:
                turn_rows(*following(i, u), (0, 1))
            products(i, u, 0)
            if not last:
                turn_rows(*following(i, u), (2, 3))
            products(i, u, 1)
            products(i, u, 2)
            if not last:
                turn_back(*following(i, u))
            products(i, u, 3)

        if sage:
            turn_rows(0, 0, range(S))
            turn_back(0, 0)
            in_pairs(pe, G, group)
        else:
            in_pairs(pe, G, lambda i, u, last: turn_rows(i, u, range(S)))

    mem.close()
    return {"sync": sync, "gpsimd": gpsimd, "vector": vector, "scalar": scalar, "tensor": tensor}


def gat_stage(kn, layer):
    nc, d, dram, take, pair = kn.nc, kn.d, kn.dram, kn.sig.take, kn.sig.pair
    G, H = d.groups, d.groups // 2
    first = layer == 1
    K = HEADS
    CH = HC // P
    bias = V_GAT1_B if first else V_GAT2_B
    h_dram = dram["h1"] if first else dram["h2"]
    products = THIRDS * S if first else S
    turns = [(n,) if n < CH else () for n in range(products)] if first else [(0, 1, 2), (3, 4, 5), (6, 7), ()]
    mem = ExitStack()

    def two(name, shape, dt):
        return [kn.buffer(mem, f"{name}{u}", shape, dt) for u in range(2)]

    z = two("t_z", [P, S, HC + K], F32)
    hrow = two("t_h", [P, HC], F32)
    r_f = two("t_r", [P, D], F32)
    r_hi = kn.buffer(mem, "t_r_hi", [P, 2, CH, D], F16)
    r_lo = kn.buffer(mem, "t_r_lo", [P, 2, CH, D], F16)
    if first:
        wide = two("t_wide", [P, GAT_ROW], F32)
    else:
        dead = kn.w_hi[:, 0:kn.unit_at(W_GAT1)].bitcast(F32).rearrange("p (u s c) -> p u s c", u=2, c=D)
        x = [dead[:, u] for u in range(2)]
        norm = Norm(kn, mem)
    tp = [kn.bank[n] for n in ((0, 1, 4, 5) if first else (0, 1, 6, 7))]
    mm = [kn.bank[n][:, 0:THIRD] for n in (2, 3, 6)] if first else [kn.bank[2 + s][:] for s in range(S)]

    sum_in = [kn.sig.several(S, f"sum_in{u}_", 16 * H) for u in range(2)]
    h_in = pair("h_in", 16 * 2 * G)
    z_ready = pair("z_ready", S * H)
    turned = pair("turned", CH * H)
    r_done = take("r_done", CH * G)
    r_hi_done = take("r_hi_done", CH * G)
    r_lo_done = take("r_lo_done", CH * G)
    prod = take("prod", products * G)
    if first:
        wide_done = take("wide_done", THIRDS * S * G)
        wide_stored = pair("wide_stored", 16 * 2 * G)
    else:
        x_in = pair("x_in", 16 * H)
        y_done = take("y_done", S * G)
        rows_out = take("x3_out", S * G)
        stored = pair("stored", 16 * H)

    def sync(sp):
        def load(i, u):
            sp.wait_ge(turned[u].sem, turned[u].at(i * CH))
            for s in range(S):
                rows = ds(i * (2 * GROUP) + u * GROUP + s * P, P)
                sp.dma_start(z[u][:, s, :], dram["sum_gat"][rows, :])\
                    .then_inc(sum_in[u][s].sem, 16)
                if s >= 2:
                    sp.wait_ge(z_ready[u].sem, z_ready[u].at(i * S + s - 1))
                else:
                    sp.wait_ge(z_ready[1 - u].sem, z_ready[1 - u].at((i + u) * S))
                sp.dma_start(hrow[s % 2][:], h_dram[rows, LOGITS:])\
                    .then_inc(h_in[s % 2].sem, 16)

        def load_x(i, u):
            sp.wait_ge(stored[u].sem, stored[u].at(i * 16))
            sp.dma_start(x[u], node_rows(dram["x2_biased"], i, u)).then_inc(x_in[u].sem, 16)

        def group(i, u, last):
            g = i * 2 + u
            if ahead(i, G):
                load(i + 1, u)
            if not first and not last:
                load_x(*following(i, u))
            if first:
                for s in range(S):
                    sp.wait_ge(wide_done.sem, wide_done.at((g * S + s + 1) * THIRDS))
                    sp.dma_start(dram["h2"][ds(i * (2 * GROUP) + u * GROUP + s * P, P), :], wide[s % 2][:])\
                        .then_inc(wide_stored[s % 2].sem, 16)
            else:
                sp.wait_ge(rows_out.sem, rows_out.at(g * S + S))
                sp.dma_start(node_rows(dram["x3"], i, u), x[u]).then_inc(stored[u].sem, 16)

        load(0, 0)
        load(0, 1)
        if not first:
            load_x(0, 0)
        in_pairs(sp, G, group)
        if first:
            for u in range(2):
                sp.wait_ge(wide_stored[u].sem, wide_stored[u].at(16 * 2 * G))
        else:
            for u in range(2):
                sp.wait_ge(stored[u].sem, stored[u].at(16 * H))

    def gpsimd(pool):
        g_ = nc.gpsimd

        def low_parts(i, u, chunks):
            g = i * 2 + u
            for k in chunks:
                pool.wait_ge(r_hi_done.sem, r_hi_done.at(g * CH + k + 1))
                g_.tensor_tensor(r_lo[:, u, k, :], r_f[k % 2][:], r_hi[:, u, k, :], ALU.subtract)\
                  .then_inc(r_lo_done.sem, 1)

        def group(i, u, last):
            if not last:
                low_parts(*following(i, u), range(CH))
            if not first:
                norm.pool(pool, i, u)

        low_parts(0, 0, range(CH))
        in_pairs(pool, G, group)

    def vector(dve):
        v = nc.vector

        def combine(i, u, subtiles=range(S)):
            for s in subtiles:
                dve.wait_ge(sum_in[u][s].sem, sum_in[u][s].at(i * 16 + 16))
                w = h_in[s % 2]
                dve.wait_ge(w.sem, w.at(i * 64 + u * 32 + (s // 2) * 16 + 16))
                for h in range(K):
                    cols = slice(h * C, (h + 1) * C)
                    ins = v.scalar_tensor_tensor(out=z[u][:, s, cols], in0=hrow[s % 2][:, cols],
                                                 scalar=z[u][:, s, HC + h:HC + h + 1], in1=z[u][:, s, cols],
                                                 op0=ALU.mult, op1=ALU.add)
                ins.then_inc(z_ready[u].sem, 1)

        def group(i, u, last):
            g = i * 2 + u
            if first:
                if ahead(i, G):
                    combine(i + 1, u)
                return
            dve.wait_ge(x_in[u].sem, x_in[u].at(i * 16 + 16))
            for s in range(S):
                if ahead(i, G):
                    combine(i + 1, u, (s,))
                dve.wait_ge(prod.sem, prod.at(g * S + s + 1))
                v.scalar_tensor_tensor(out=x[u][:, s, :], in0=mm[s], scalar=UNSCALE, in1=x[u][:, s, :],
                                       op0=ALU.mult, op1=ALU.add).then_inc(y_done.sem, 1)
                dve.wait_ge(y_done.sem, y_done.at(g * S + s + 1))
                norm.moments_of(dve, x[u][:, s, :], s, i, u)
            norm.apply(dve, x[u], x[u], i, u, rows_out)

        combine(0, 0)
        combine(0, 1)
        in_pairs(dve, G, group)

    def scalar(act):
        def parts(i, u, chunks):
            g = i * 2 + u
            for k in chunks:
                act.wait_ge(turned[u].sem, turned[u].at(i * CH + k + 1))
                act.wait_ge(r_lo_done.sem, r_lo_done.at(g * CH + (k - 1 if k >= 2 else 0)))
                act.activation(r_f[k % 2][:], tp[k % 4][:], ACT.Relu, scale=A_SCALE,
                               bias=kn.vec_scaled[:, bias + k:bias + k + 1]).then_inc(r_done.sem, 1)
                act.wait_ge(r_done.sem, r_done.at(g * CH + k + 1))
                act.copy(r_hi[:, u, k, :], r_f[k % 2][:]).then_inc(r_hi_done.sem, 1)

        def group(i, u, last):
            g = i * 2 + u
            for n in range(products):
                if not last:
                    parts(*following(i, u), turns[n])
                if first:
                    s, third = divmod(n, THIRDS)
                    w = wide_stored[s % 2]
                    act.wait_ge(w.sem, w.at(g * 32 + (s // 2) * 16))
                    act.wait_ge(prod.sem, prod.at(g * products + n + 1))
                    act.activation(wide[s % 2][:, third * THIRD:(third + 1) * THIRD], mm[third], ACT.Copy,
                                   scale=UNSCALE)\
                       .then_inc(wide_done.sem, 1)

        parts(0, 0, range(CH))
        in_pairs(act, G, group)

    def tensor(pe):
        def turn(i, u, chunks):
            g = i * 2 + u
            pe.wait_ge(z_ready[u].sem, z_ready[u].at(i * S + S))
            for k in chunks:
                pe.wait_ge(r_done.sem, r_done.at(g * CH + k - 3))
                for s in range(S):
                    ins = pe.transpose(tp[k % 4][:, s * P:(s + 1) * P], z[u][:, s, k * P:(k + 1) * P], kn.ident[:])
                ins.then_inc(turned[u].sem, 1)

        def group(i, u, last):
            g = i * 2 + u
            pe.wait_ge(r_lo_done.sem, r_lo_done.at(g * CH + CH))
            for n in range(products):
                s, third = divmod(n, THIRDS) if first else (n, 0)
                split = lambda k: (r_hi[:, u, k, s * P:(s + 1) * P], r_lo[:, u, k, s * P:(s + 1) * P])
                if not last:
                    turn(*following(i, u), turns[n])
                if first:
                    pe.wait_ge(wide_done.sem, wide_done.at((g * S + s - 1) * THIRDS + third + 1))
                    moving = lambda k: (kn.gat_weights(False, W_GAT2, k, third), kn.gat_weights(True, W_GAT2, k, third))
                else:
                    pe.wait_ge(y_done.sem, y_done.at((g - 1) * S + s + 1))
                    moving = lambda k: (kn.weights(False, W_FC, k), kn.weights(True, W_FC, k))
                split_product(pe, mm[third if first else s], split, moving, CH).then_inc(prod.sem, 1)

        turn(0, 0, range(CH))
        in_pairs(pe, G, group)

    mem.close()
    return {"sync": sync, "gpsimd": gpsimd, "vector": vector, "scalar": scalar, "tensor": tensor}


def graph_layers_kernel(nc, nodes, edges, io):
    d = Dims(nodes, edges)
    dram = dict(io)

    def scratch(name, shape, dt=F32):
        dram[name] = nc.dram_tensor(name, shape, dt, kind="Internal").ap()

    scratch("sorted", (d.edge_rows + 1, 2), I32)
    scratch("sum", (d.padded, D))
    scratch("sum_gat", (d.padded, HC + HEADS))
    scratch("dinv", (d.padded, 1))
    for name in ("x1", "x2_biased", "x3"):
        scratch(name, (d.padded, D))
    for name in ("h1", "h2"):
        scratch(name, (d.padded, GAT_ROW))
    scratch("h", (4, P, d.padded))

    with ExitStack() as ctx:
        kn = Kernel(nc, ctx, d, dram)
        ones = kn.ones
        kn.add(setup_stage(kn))
        with ExitStack() as mem:
            weights = plain_weights(kn, mem)
            kn.add(together(tiles_stage(kn), weights))
        with ExitStack() as mem:
            weights = attention_weights(kn, mem)
            kn.add(together(edge_sum_stage(kn, dram["x"], ones, ones), weights))
        kn.add(gin_stage(kn))
        kn.add(edge_sum_stage(kn, dram["x1"], ones, kn.mean_scale))
        kn.add(together(linear_stage(kn, "sage"), degree_stage(kn)))
        kn.add(norm_coefficients_stage(kn, V_SAGE_G, V_SAGE_BETA))
        kn.add(batch_norm_stage(kn, "sage"))
        kn.add(edge_attention_stage(kn, dram["h1"]))
        kn.add(gat_stage(kn, 1))
        kn.add(edge_attention_stage(kn, dram["h2"]))
        kn.add(gat_stage(kn, 2))
        kn.add(edge_sum_stage(kn, dram["x3"], kn.src_dinv, ones))
        kn.add(linear_stage(kn, "gcn"))
        kn.add(norm_coefficients_stage(kn, V_GCN_G, V_GCN_BETA))
        kn.add(batch_norm_stage(kn, "gcn"))
        kn.run()


def lay_out(inputs, d):
    import numpy as np

    x = np.asarray(inputs["x"])
    pad = np.zeros((d.padded - d.nodes, D), x.dtype)
    src, dst = np.asarray(inputs["src"]), np.asarray(inputs["dst"])
    more = d.edge_rows - d.edges
    src = np.concatenate([src, np.zeros(more, src.dtype)])
    dst = np.concatenate([dst, np.full(more, d.sent, dst.dtype)])

    def unit(w):
        k, n = w.shape
        per = 4 * D // n
        return w.reshape(k // P // per, per, P, n).transpose(0, 2, 1, 3).reshape(-1, P, 4 * D)

    weights = [np.asarray(inputs["L0_gnn_W1"]), np.asarray(inputs["L0_gnn_W2"]),
               np.asarray(inputs["L1_gnn_W_l"]).T, np.asarray(inputs["L1_gnn_W_r"]).T,
               np.asarray(inputs["L2_gnn_W1"]), np.asarray(inputs["L2_gnn_W2"]), np.asarray(inputs["L2_gnn_Wfc"]),
               np.asarray(inputs["L3_gnn_W"]).T]
    vectors = [np.asarray(inputs[n]).reshape(-1, P).T for n in (
        "L0_gnn_b1", "L1_gnn_b_l", "L1_gnn_gamma", "L1_gnn_beta", "L2_gnn_b1", "L2_gnn_b2",
        "L3_gnn_b", "L3_gnn_gamma", "L3_gnn_beta")]
    attention = np.stack([np.stack([np.asarray(inputs[f"L2_gnn_a_src{n}"]).reshape(-1),
                                    np.asarray(inputs[f"L2_gnn_a_dst{n}"]).reshape(-1)]) for n in (1, 2)])
    return {
        "x": np.concatenate([x, pad]),
        "dst": dst,
        "edges": np.stack([src, dst], axis=-1).reshape(d.edge_cols, P, 2).transpose(1, 0, 2),
        "weights": np.concatenate([unit(w) for w in weights]),
        "vectors": np.ascontiguousarray(np.concatenate(vectors, axis=1)),
        "attention": attention,
        "gin_b2": np.asarray(inputs["L0_gnn_b2"]),
        "fc_b": np.asarray(inputs["L2_gnn_bfc"]),
    }


def program(nc, inputs):
    import numpy as np

    nodes, edges = inputs["x"].shape[0], inputs["src"].shape[0]
    d = Dims(nodes, edges)
    arrays = {f"in_{n}": np.ascontiguousarray(a) for n, a in lay_out(inputs, d).items()}
    io = {n[3:]: nc.dram_tensor(n, a.shape, mybir.dt.from_np(a.dtype), kind="ExternalInput").ap()
          for n, a in arrays.items()}
    io["out"] = nc.dram_tensor("out", (d.padded, D), F32, kind="ExternalOutput").ap()
    graph_layers_kernel(nc, nodes, edges, io)
    return arrays


def kernel(**inputs):
    import concourse.bacc as bacc
    from concourse.bass_utils import run_bass_kernel_spmd

    nc = bacc.Bacc("TRN2", target_bir_lowering=False, num_devices=1)
    arrays = program(nc, inputs)
    return run_bass_kernel_spmd(nc, [arrays], core_ids=[0]).results[0]["out"][:inputs["x"].shape[0]]
```
